# Optimizing a Trainium2 kernel written in Bass

```python
import numpy as np
import jax
import jax.numpy as jnp

def _softmax(x, axis=-1):
    return jax.nn.softmax(x, axis=axis)

def _gelu(x):
    return jax.nn.gelu(x, approximate=True)

def _silu(x):
    return jax.nn.silu(x)

def _sigmoid(x):
    return jax.nn.sigmoid(x)

def _layernorm(x, axis=-1, eps=1e-05):
    m = jnp.mean(x, axis=axis, keepdims=True)
    v = jnp.var(x, axis=axis, keepdims=True)
    return (x - m) / jnp.sqrt(v + eps)

def _scatter_add(tgt, idx, src, axis=0):
    return tgt.at[idx].add(src)

def _segment_sum(src, seg, n):
    return jax.ops.segment_sum(src, seg, n)
kernel_name = 'mk_xattn_ffn_d2_seqx_r4_afe425'

def setup_inputs(seed: int=0):
    np.random.seed(seed)
    _w = jnp.asarray

    def _rec_inputs():
        import jax
        import jax.numpy as jnp
        _rk = jax.random.key(seed)
        x = 7.22e-05 + 1 * jax.random.normal(jax.random.fold_in(_rk, 1), (8, 256, 256), jnp.float32)
        _lenS = 256 - jax.random.randint(jax.random.fold_in(_rk, 7), (8,), 0, max(1, 256 // 4) + 1, jnp.int32)
        _lenS2 = 77 - jax.random.randint(jax.random.fold_in(_rk, 8), (8,), 0, max(1, 77 // 4) + 1, jnp.int32)
        _ctx_768P = jax.random.normal(jax.random.fold_in(_rk, 11), (8, 16, 192), jnp.float32)
        _ctx_768c = jax.random.dirichlet(jax.random.fold_in(_rk, 511), 0.3 * jnp.ones((16,), jnp.float32), (8, 77))
        _ctx_768t = jnp.einsum('bsk,bkd->bsd', _ctx_768c, _ctx_768P)
        _ctx_768t = _ctx_768t * jax.lax.rsqrt(jnp.mean(jnp.square(_ctx_768t)) + 1e-12) * 0.953939
        ctx_768 = -0.000191848 + 0.999787 * (_ctx_768t + 0.3 * jax.random.normal(jax.random.fold_in(_rk, 611), (8, 77, 192), jnp.float32))
        return (x, ctx_768)
    x, ctx_768 = _rec_inputs()

    def _L0_xattn_setup():
        import jax, jax.numpy as jnp
        import numpy as np
        NUM_HEADS = 16
        CLAMP = 10000.0
        key = jax.random.key(seed)
        ks = jax.random.split(key, 8)
        B, Nq, Nkv, Cq, Ckv = (4, 512, 512, 256, 192)
        s_q = 1.0 / np.sqrt(Cq)
        s_kv = 1.0 / np.sqrt(Ckv)
        return {'query': jax.random.normal(ks[0], (B, Nq, Cq), jnp.float32), 'key_value': jax.random.normal(ks[1], (B, Nkv, Ckv), jnp.float32), 'Wq': jax.random.normal(ks[2], (Cq, Cq), jnp.float32) * s_q, 'bq': jnp.zeros((Cq,), jnp.float32), 'Wk': jax.random.normal(ks[3], (Ckv, Cq), jnp.float32) * s_kv, 'bk': jnp.zeros((Cq,), jnp.float32), 'Wv': jax.random.normal(ks[4], (Ckv, Cq), jnp.float32) * s_kv, 'bv': jnp.zeros((Cq,), jnp.float32), 'Wo': jax.random.normal(ks[5], (Cq, Cq), jnp.float32) * s_q, 'bo': jnp.zeros((Cq,), jnp.float32)}
    _L0_xattn_all = _L0_xattn_setup()
    _L0_xattn_in = {k: v for k, v in _L0_xattn_all.items() if k in ('Wq', 'bq', 'Wk', 'bk', 'Wv', 'bv', 'Wo', 'bo')}
    del _L0_xattn_all

    def _L0_ffn_setup():
        import jax, jax.numpy as jnp
        import numpy as np
        B, S, H, F, E = (4, 512, 256, 1024, 8)
        key = jax.random.key(seed)
        ks = jax.random.split(key, 8)
        s = 1.0 / np.sqrt(H)
        sf = 1.0 / np.sqrt(F)
        return {'x': jax.random.normal(ks[0], (B, S, H), jnp.float32), 'wr': jax.random.uniform(ks[1], (H, E), jnp.float32, -s, s), 'br': jax.random.uniform(ks[2], (E,), jnp.float32, -s, s), 'w1': jax.random.uniform(ks[3], (E, H, F), jnp.float32, -s, s), 'b1': jax.random.uniform(ks[4], (E, F), jnp.float32, -s, s), 'w2': jax.random.uniform(ks[5], (E, F, H), jnp.float32, -sf, sf), 'b2': jax.random.uniform(ks[6], (E, H), jnp.float32, -sf, sf)}
    _L0_ffn_all = _L0_ffn_setup()
    _L0_ffn_in = {k: v for k, v in _L0_ffn_all.items() if k in ('wr', 'br', 'w1', 'b1', 'w2', 'b2')}
    del _L0_ffn_all

    def _L1_xattn_setup():
        import jax, jax.numpy as jnp
        import numpy as np
        HEADS = 8
        DIM_HEAD = 64
        SCALE = DIM_HEAD ** (-0.5)
        key = jax.random.key(seed)
        ks = jax.random.split(key, 7)
        B, Nq, Nc = (4, 512, 512)
        Dq, Dc = (256, 192)
        inner = HEADS * DIM_HEAD
        x = jax.random.normal(ks[0], (B, Nq, Dq), dtype=jnp.float32)
        context = jax.random.normal(ks[1], (B, Nc, Dc), dtype=jnp.float32)
        Wq = jax.random.normal(ks[2], (Dq, inner), dtype=jnp.float32) * Dq ** (-0.5)
        Wk = jax.random.normal(ks[3], (Dc, inner), dtype=jnp.float32) * Dc ** (-0.5)
        Wv = jax.random.normal(ks[4], (Dc, inner), dtype=jnp.float32) * Dc ** (-0.5)
        Wo = jax.random.normal(ks[5], (inner, Dq), dtype=jnp.float32) * inner ** (-0.5)
        bo = jax.random.normal(ks[6], (Dq,), dtype=jnp.float32) * 0.01
        return {'x': x, 'context': context, 'Wq': Wq, 'Wk': Wk, 'Wv': Wv, 'Wo': Wo, 'bo': bo}
    _L1_xattn_all = _L1_xattn_setup()
    _L1_xattn_in = {k: v for k, v in _L1_xattn_all.items() if k in ('Wq', 'Wk', 'Wv', 'Wo', 'bo')}
    del _L1_xattn_all

    def _L1_ffn_setup():
        import jax, jax.numpy as jnp
        import numpy as np
        B, L, M = (4, 512, 256)
        G, E = (8, 8)
        CAP_FACTOR = 2.0

        def _ffn_size(m, widening=8.0):
            f = int(widening * m) * 2 // 3
            return f + (8 - f) % 8
        H = _ffn_size(M)

        def _gating_top2(logits, C):
            Gd, Sd, Ed = logits.shape
            raw = jax.nn.softmax(logits, axis=-1)
            idx1 = jnp.argmax(raw, axis=-1)
            m1 = jax.nn.one_hot(idx1, Ed, dtype=logits.dtype)
            gate1 = jnp.sum(raw * m1, axis=-1)
            rest = raw * (1.0 - m1)
            idx2 = jnp.argmax(rest, axis=-1)
            m2 = jax.nn.one_hot(idx2, Ed, dtype=logits.dtype)
            gate2 = jnp.sum(rest * m2, axis=-1)
            p1 = jnp.cumsum(m1, axis=-2) - m1
            m1 = m1 * (p1 < C).astype(m1.dtype)
            p1 = jnp.sum(p1 * m1, axis=-1)
            m1_flat = jnp.sum(m1, axis=-1)
            m1_count = jnp.sum(m1, axis=-2)
            p2 = jnp.cumsum(m2, axis=-2) - m2 + m1_count[:, None, :]
            m2 = m2 * (p2 < C).astype(m2.dtype)
            p2 = jnp.sum(p2 * m2, axis=-1)
            m2_flat = jnp.sum(m2, axis=-1)
            gate1 = gate1 * m1_flat
            gate2 = gate2 * m2_flat
            c1 = (gate1[..., None] * jax.nn.one_hot(idx1, Ed, dtype=jnp.float32))[..., None] * jax.nn.one_hot(p1.astype(jnp.int32), C, dtype=jnp.float32)[:, :, None, :]
            c2 = (gate2[..., None] * jax.nn.one_hot(idx2, Ed, dtype=jnp.float32))[..., None] * jax.nn.one_hot(p2.astype(jnp.int32), C, dtype=jnp.float32)[:, :, None, :]
            combine = (c1 + c2).astype(logits.dtype)
            dispatch = (combine != 0).astype(logits.dtype)
            return (dispatch, combine)
        key = jax.random.key(seed)
        k0, k1, k2, k3, k4 = jax.random.split(key, 5)
        return {'inputs': jax.random.normal(k0, (B, L, M), jnp.float32), 'router_w': jax.random.normal(k1, (M, E), jnp.float32) * 0.02, 'w0_kernel': jax.random.normal(k2, (E, M, H), jnp.float32) * 0.02, 'w1_kernel': jax.random.normal(k3, (E, M, H), jnp.float32) * 0.02, 'wo_kernel': jax.random.normal(k4, (E, H, M), jnp.float32) * 0.02}
    _L1_ffn_all = _L1_ffn_setup()
    _L1_ffn_in = {k: v for k, v in _L1_ffn_all.items() if k in ('router_w', 'w0_kernel', 'w1_kernel', 'wo_kernel')}
    del _L1_ffn_all
    return {'x': x, 'ctx_768': ctx_768, 'L0_xattn_Wq': _L0_xattn_in['Wq'], 'L0_xattn_bq': _L0_xattn_in['bq'], 'L0_xattn_Wk': _L0_xattn_in['Wk'], 'L0_xattn_bk': _L0_xattn_in['bk'], 'L0_xattn_Wv': _L0_xattn_in['Wv'], 'L0_xattn_bv': _L0_xattn_in['bv'], 'L0_xattn_Wo': _L0_xattn_in['Wo'], 'L0_xattn_bo': _L0_xattn_in['bo'], 'L0_ffn_wr': _L0_ffn_in['wr'], 'L0_ffn_br': _L0_ffn_in['br'], 'L0_ffn_w1': _L0_ffn_in['w1'], 'L0_ffn_b1': _L0_ffn_in['b1'], 'L0_ffn_w2': _L0_ffn_in['w2'], 'L0_ffn_b2': _L0_ffn_in['b2'], 'L1_xattn_Wq': _L1_xattn_in['Wq'], 'L1_xattn_Wk': _L1_xattn_in['Wk'], 'L1_xattn_Wv': _L1_xattn_in['Wv'], 'L1_xattn_Wo': _L1_xattn_in['Wo'], 'L1_xattn_bo': _L1_xattn_in['bo'], 'L1_ffn_router_w': _L1_ffn_in['router_w'], 'L1_ffn_w0_kernel': _L1_ffn_in['w0_kernel'], 'L1_ffn_w1_kernel': _L1_ffn_in['w1_kernel'], 'L1_ffn_wo_kernel': _L1_ffn_in['wo_kernel']}

def reference(x, ctx_768, L0_xattn_Wq, L0_xattn_bq, L0_xattn_Wk, L0_xattn_bk, L0_xattn_Wv, L0_xattn_bv, L0_xattn_Wo, L0_xattn_bo, L0_ffn_wr, L0_ffn_br, L0_ffn_w1, L0_ffn_b1, L0_ffn_w2, L0_ffn_b2, L1_xattn_Wq, L1_xattn_Wk, L1_xattn_Wv, L1_xattn_Wo, L1_xattn_bo, L1_ffn_router_w, L1_ffn_w0_kernel, L1_ffn_w1_kernel, L1_ffn_wo_kernel):
    import jax
    import jax.numpy as jnp

    def _L0_xattn_ref(query, key_value, Wq, bq, Wk, bk, Wv, bv, Wo, bo):
        import jax, jax.numpy as jnp
        import numpy as np
        NUM_HEADS = 16
        CLAMP = 10000.0
        B, Nq, Cq = query.shape
        Nkv = key_value.shape[1]
        H = NUM_HEADS
        D = Cq // H
        scale = D ** (-0.5)
        q = (query @ Wq + bq).reshape(B, Nq, H, D).transpose(0, 2, 1, 3)
        k = (key_value @ Wk + bk).reshape(B, Nkv, H, D).transpose(0, 2, 1, 3)
        v = (key_value @ Wv + bv).reshape(B, Nkv, H, D).transpose(0, 2, 1, 3)
        attn = jnp.einsum('bhqd,bhkd->bhqk', q, k) * scale
        attn = jnp.clip(attn, -CLAMP, CLAMP)
        attn = jax.nn.softmax(attn, axis=-1)
        attn = jnp.where(jnp.any(jnp.isnan(attn)), jnp.asarray(1.0 / Nkv, attn.dtype), attn)
        x = jnp.einsum('bhqk,bhkd->bqhd', attn, v).reshape(B, Nq, Cq)
        return x @ Wo + bo

    def _L0_ffn_ref(x, wr, br, w1, b1, w2, b2):
        import jax, jax.numpy as jnp
        import numpy as np
        B, S, H, F, E = (4, 512, 256, 1024, 8)
        scores = jnp.einsum('bsh,he->bse', x, wr) + br
        expert_id = jnp.argmax(scores, axis=-1)
        h = jnp.einsum('bsh,ehf->ebsf', x, w1) + b1[:, None, None, :]
        h = jax.nn.gelu(h, approximate=False)
        y = jnp.einsum('ebsf,efh->ebsh', h, w2) + b2[:, None, None, :]
        one_hot = jax.nn.one_hot(expert_id, E, dtype=x.dtype)
        out = jnp.einsum('ebsh,bse->bsh', y, one_hot)
        return out

    def _L1_xattn_ref(x, context, Wq, Wk, Wv, Wo, bo):
        import jax, jax.numpy as jnp
        import numpy as np
        HEADS = 8
        DIM_HEAD = 64
        SCALE = DIM_HEAD ** (-0.5)
        B, Nq, _ = x.shape
        q = (x @ Wq).reshape(B, Nq, HEADS, DIM_HEAD)
        k = (context @ Wk).reshape(B, context.shape[1], HEADS, DIM_HEAD)
        v = (context @ Wv).reshape(B, context.shape[1], HEADS, DIM_HEAD)
        sim = jnp.einsum('bihd,bjhd->bhij', q, k) * SCALE
        attn = jax.nn.softmax(sim, axis=-1)
        out = jnp.einsum('bhij,bjhd->bihd', attn, v)
        out = out.reshape(B, Nq, HEADS * DIM_HEAD)
        return out @ Wo + bo

    def _L1_ffn_ref(inputs, router_w, w0_kernel, w1_kernel, wo_kernel):
        import jax, jax.numpy as jnp
        import numpy as np
        B, L, M = (4, 512, 256)
        G, E = (8, 8)
        CAP_FACTOR = 2.0

        def _ffn_size(m, widening=8.0):
            f = int(widening * m) * 2 // 3
            return f + (8 - f) % 8
        H = _ffn_size(M)

        def _gating_top2(logits, C):
            Gd, Sd, Ed = logits.shape
            raw = jax.nn.softmax(logits, axis=-1)
            idx1 = jnp.argmax(raw, axis=-1)
            m1 = jax.nn.one_hot(idx1, Ed, dtype=logits.dtype)
            gate1 = jnp.sum(raw * m1, axis=-1)
            rest = raw * (1.0 - m1)
            idx2 = jnp.argmax(rest, axis=-1)
            m2 = jax.nn.one_hot(idx2, Ed, dtype=logits.dtype)
            gate2 = jnp.sum(rest * m2, axis=-1)
            p1 = jnp.cumsum(m1, axis=-2) - m1
            m1 = m1 * (p1 < C).astype(m1.dtype)
            p1 = jnp.sum(p1 * m1, axis=-1)
            m1_flat = jnp.sum(m1, axis=-1)
            m1_count = jnp.sum(m1, axis=-2)
            p2 = jnp.cumsum(m2, axis=-2) - m2 + m1_count[:, None, :]
            m2 = m2 * (p2 < C).astype(m2.dtype)
            p2 = jnp.sum(p2 * m2, axis=-1)
            m2_flat = jnp.sum(m2, axis=-1)
            gate1 = gate1 * m1_flat
            gate2 = gate2 * m2_flat
            c1 = (gate1[..., None] * jax.nn.one_hot(idx1, Ed, dtype=jnp.float32))[..., None] * jax.nn.one_hot(p1.astype(jnp.int32), C, dtype=jnp.float32)[:, :, None, :]
            c2 = (gate2[..., None] * jax.nn.one_hot(idx2, Ed, dtype=jnp.float32))[..., None] * jax.nn.one_hot(p2.astype(jnp.int32), C, dtype=jnp.float32)[:, :, None, :]
            combine = (c1 + c2).astype(logits.dtype)
            dispatch = (combine != 0).astype(logits.dtype)
            return (dispatch, combine)
        Bb, Ll, Mm = inputs.shape
        S = Bb * Ll // G
        x = inputs.reshape(G, S, Mm)
        logits = jnp.einsum('GSM,ME->GSE', x, router_w)
        cap = int(CAP_FACTOR * S / E)
        C = (cap + 3) // 4 * 4
        dispatch, combine = _gating_top2(logits, C)
        expert_inputs = jnp.einsum('GSEC,GSM->EGCM', dispatch, x)
        layer_w0 = jnp.einsum('EGCM,EMH->EGCH', expert_inputs, w0_kernel)
        layer_w1 = jnp.einsum('EGCM,EMH->EGCH', expert_inputs, w1_kernel)
        hidden = jax.nn.gelu(layer_w0, approximate=True) * layer_w1
        expert_outputs = jnp.einsum('EGCH,EHM->EGCM', hidden, wo_kernel)
        out = jnp.einsum('EGCM,GSEC->GSM', expert_outputs, combine)
        return out.reshape(Bb, Ll, Mm)
    x = x + _L0_xattn_ref(_layernorm(x, axis=-1), ctx_768, L0_xattn_Wq, L0_xattn_bq, L0_xattn_Wk, L0_xattn_bk, L0_xattn_Wv, L0_xattn_bv, L0_xattn_Wo, L0_xattn_bo)
    x = x + _L0_ffn_ref(_layernorm(x, axis=-1), L0_ffn_wr, L0_ffn_br, L0_ffn_w1, L0_ffn_b1, L0_ffn_w2, L0_ffn_b2)
    x = x + _L1_xattn_ref(_layernorm(x, axis=-1), ctx_768, L1_xattn_Wq, L1_xattn_Wk, L1_xattn_Wv, L1_xattn_Wo, L1_xattn_bo)
    x = x + _L1_ffn_ref(_layernorm(x, axis=-1), L1_ffn_router_w, L1_ffn_w0_kernel, L1_ffn_w1_kernel, L1_ffn_wo_kernel)
    return x

_drawn_inputs = setup_inputs


def setup_inputs(seed=0):
    import zlib

    import numpy as np

    out = dict(_drawn_inputs(seed))
    spreads = {'L0_xattn_bq': (0.0, 0.1),
     'L0_xattn_bk': (0.0, 0.8),
     'L0_xattn_bv': (0.0, 0.1),
     'L0_xattn_bo': (0.0, 0.1)}
    factors = {'L0_ffn_b1': 5.489,
     'L0_ffn_b2': 3.879,
     'L1_xattn_bo': 6.933,
     'L1_ffn_router_w': 8.0,
     'L1_ffn_w0_kernel': 8.0,
     'L1_ffn_w1_kernel': 8.0,
     'L1_ffn_wo_kernel': 8.0}
    for name, (base, spread) in spreads.items():
        noise = np.random.default_rng([zlib.crc32(name.encode()), seed]).standard_normal(out[name].shape)
        drawn = base * np.exp(spread * noise) if base else spread * noise
        out[name] = jnp.asarray(drawn.astype(out[name].dtype))
    for name, factor in factors.items():
        out[name] = (out[name] * factor).astype(out[name].dtype)
    return out
```

```python
from contextlib import ExitStack

import concourse.bass as bass
from concourse import mybir

F32 = mybir.dt.float32
F16 = mybir.dt.float16
U32 = mybir.dt.uint32
ALU = mybir.AluOpType
ACT = mybir.ActivationFunctionType
AX = mybir.AxisListType.X

P = 128
NB = 8
TPB = 2
NT = NB * TPB
D = 256
DC = D // P
CK = 77
CC = 192
CR = 96
E = 8
F0 = 1024
FC0 = F0 // P
F1 = 1368
FC1 = (F1 + P - 1) // P
FT1 = F1 - (FC1 - 1) * P
CAP = 64
SL = NB * CAP
EPS = 1e-5
CLAMP = 10000.0

WS = 128.0
XS = 64.0
HS0 = 8.0
HS1 = 1.0 / 32

C_ID, C_TRI, C_ONE, C_IOTA, C_REV, C_ROW, C_COL, C_HM0, C_HM1 = 0, 128, 256, 384, 896, 1024, 1152, 1280, 1288
C_END = 1290
V_BQ, V_BK, V_B1, V_BV, V_BO0, V_BO1, V_BR, V_WR0, V_WR1 = 0, 2, 4, 68, 324, 580, 836, 844, 860
V_END = 876


def build(nc, x, ctx_t, consts, vecs, b2, wq0, wk0, wv0, wo0, wq1, wk1, wv1, wo1, f0w1, f0w2, f1w0, f1w1, f1wo, out):
    y_dram = nc.dram_tensor("y_rows", (E * SL, D), F32, kind="Internal").ap()
    ctx = ExitStack()
    with ctx:
        def sb(name, shape, dt=F32):
            return ctx.enter_context(nc.sbuf_tensor(name, shape, dt))

        sems = {}

        def sem(name):
            if name not in sems:
                sems[name] = ctx.enter_context(nc.semaphore(name))
            return sems[name]

        x_sb = sb("x_sb", [P, NT * D])
        cst = sb("cst", [P, C_END])
        vec = sb("vec", [P, V_END])
        b2_sb = sb("b2_sb", [E, D])
        aw = sb("aw", [P, 16 * D])
        xt = sb("xt", [P, 2, DC, E * SL], F16)
        stage = sb("stage", [P, 2, FC1 * D])
        W1 = 2 * DC * F1 + FC1 * D
        arena = sb("arena", [P, 2, 2, W1], F16)
        s_exp = sb("s_exp", [P, 16 * CK])
        p_exp = sb("p_exp", [P, 16 * CK])
        xn = sb("xn", [P, 2, D])
        xnt = sb("xnt", [P, 2, D])
        red = sb("red", [P, 16])
        rec = sb("rec", [P, 16])
        st6 = sb("st6", [P, NT, 6])
        mv = sb("mv", [P, NT * 2])
        rstd = sb("rstd", [P, NT])
        y_sb = sb("y_sb", [P, 4 * D])
        hid = sb("hid", [P, 2, 4 * P])
        hga = sb("hga", [P, 2, 4 * P])
        o_n, ot, qt = hid[:, 0, :], hid[:, 1, :], hga[:, 0, :]
        hh = sb("hh", [P, 2, 4 * P], F16)
        hl = sb("hl", [P, 2, 4 * P], F16)
        lg = sb("lg", [P, NT * E])
        gt = sb("gt", [P, 12, NT * E])
        gs = sb("gs", [P, 12, NT])
        gi = sb("gi", [P, 2, NT], U32)
        gath = s_exp
        gath2 = p_exp
        xh = sb("xh", [P, 2, 2, D], F16)
        disp = sb("disp", [P, 2, 4 * P], F16)

        ps = ctx.enter_context(nc.psum_tensor("ps", [P, 8, 512], F32))

        ident = cst[:, C_ID:C_ID + P]
        tri = cst[:, C_TRI:C_TRI + P]
        ones = cst[:, C_ONE:C_ONE + P]
        iota = cst[:, C_IOTA:C_IOTA + SL]

        def xtile(t):
            return x_sb[:, bass.ds(t * D, D)] if not isinstance(t, int) else x_sb[:, t * D:(t + 1) * D]

        def cols(tensor, start, n):
            return tensor[:, bass.ds(start, n)] if not isinstance(start, int) else tensor[:, start:start + n]

        def free(eng, s, count):
            if not isinstance(count, int) or count > 0:
                eng.wait_ge(s, count)

        def met(eng):
            eng.sem_inc(sem("met"), 1)

        class Attention:

            def __init__(self, n, heads, dh, weights, mask_col, clip, bias):
                self.n, self.H, self.dh, self.weights = n, heads, dh, weights
                self.mask_col, self.clip, self.bias = mask_col, clip, bias
                self.inner = heads * dh
                self.nc = self.inner // P
                self.hpc = P // dh
                self.groups = heads // 4
                self.w = min(4, self.hpc) * CK
                self.per = self.hpc * CK // self.w
                self.banks = self.nc * self.per
                self.hb = self.w // CK
                self.scale = float(dh) ** -0.5
                flat = arena[:, :, :, :].rearrange("p a b c -> p (a b c)").bitcast(F32)
                nk = NB * heads * CK
                nv = NB * heads * (dh + 1)
                self.km = flat[:, 0:nk]
                self.v = flat[0:CK, nk:nk + nv]
                self.pt = flat[0:CK, nk + nv:nk + nv + heads * P]
                self.ctx_t = stage[0:CR, 0, 0:2 * NB * CK].rearrange("p (k n) -> p k n", k=2)
                i = self.inner
                self.wq = aw[:, 0:DC * i].rearrange("p (k n) -> p k n", k=DC)
                self.wk = aw[0:CR, DC * i:DC * i + 2 * i].rearrange("p (k n) -> p k n", k=2)
                self.wv = aw[0:CR, DC * i + 2 * i:DC * i + 4 * i].rearrange("p (k n) -> p k n", k=2)
                self.wo = aw[:, DC * i + 4 * i:DC * i + 4 * i + self.nc * D].rearrange("p (k n) -> p k n", k=self.nc)

            def s(self, name):
                return sem(f"att{self.n}_{name}")

        att = [
            Attention(0, 16, 16, (wq0, wk0, wv0, wo0), C_HM0, True, True),
            Attention(1, 8, 64, (wq1, wk1, wv1, wo1), C_HM1, False, False),
        ]
        for a in att:
            for name in ("w", "k", "km", "v", "vs", "ones", "xn", "xt", "xts", "q", "qs", "sc", "clip", "max", "sub",
                         "p", "pt", "pts", "pv", "rec", "on", "ot", "ots", "pr", "pb", "x"):
                a.s(name)
        for n in range(4):
            for name in ("st", "mv", "ve", "sq", "rs"):
                sem(f"ln{n}_{name}")

        def ln_stats_vector(eng, n, wait_x):
            wait_x()
            for t in range(NT):
                eng.bn_stats(st6[:, t, :], xtile(t)).then_inc(sem(f"ln{n}_st"), 1)
            for t in range(NT):
                eng.wait_ge(sem(f"ln{n}_st"), t + 1)
                eng.bn_aggr(mv[:, 2 * t:2 * t + 2], st6[:, t, :]).then_inc(sem(f"ln{n}_mv"), 1)
            eng.wait_ge(sem(f"ln{n}_mv"), NT)
            eng.tensor_scalar(rstd[:, :], mv[:, 1:2 * NT:2], EPS, None, ALU.add).then_inc(sem(f"ln{n}_ve"), 1)
            eng.wait_ge(sem(f"ln{n}_sq"), 1)
            eng.reciprocal(rstd[:, :], rstd[:, :]).then_inc(sem(f"ln{n}_rs"), 1)
            eng.wait_ge(sem(f"ln{n}_rs"), 1)

        def ln_stats_scalar(eng, n):
            eng.wait_ge(sem(f"ln{n}_ve"), 1)
            eng.activation(rstd[:, :], rstd[:, :], ACT.Sqrt).then_inc(sem(f"ln{n}_sq"), 1)

        def normalize(eng, dst, t):
            return eng.tensor_scalar(dst, xtile(t), cols(mv, t * 2, 1), cols(rstd, t, 1), ALU.subtract, ALU.mult)

        def att_loads(eng, a):
            for dst, src in zip((a.wq, a.wk, a.wv, a.wo), a.weights):
                eng.dma_start(dst, src).then_inc(a.s("w"), 16)
            eng.dma_start(a.ctx_t, ctx_t).then_inc(a.s("w"), 16)

        def att_kv_tensor(eng, a):
            half = NB * CK // 2
            eng.wait_ge(a.s("w"), 80)
            for c in range(a.nc):
                if c:
                    eng.wait_ge(a.s("km"), c * a.hpc)
                for h in range(2):
                    for k in range(2):
                        mm = eng.matmul(ps[:, h, 0:half], a.wk[:, k, c * P:(c + 1) * P],
                                        a.ctx_t[:, k, h * half:(h + 1) * half], start=(k == 0), stop=(k == 1))
                mm.then_inc(a.s("k"), 1)
            for b in range(NB):
                if b >= 2:
                    eng.wait_ge(a.s("vs"), b - 1)
                for k in range(2):
                    mm = eng.matmul(ps[0:CK, 2 + b % 2, 0:a.inner], a.ctx_t[:, k, b * CK:(b + 1) * CK],
                                    a.wv[:, k, :], start=(k == 0), stop=(k == 1))
                mm.then_inc(a.s("v"), 1)

        def att_kv_vector(eng, a):
            km = a.km.rearrange("p (b h n) -> p b h n", b=NB, h=a.H)
            for c in range(a.nc):
                eng.wait_ge(a.s("k"), c + 1)
                for j in range(a.hpc):
                    for h in range(2):
                        dst = km[:, h * NB // 2:(h + 1) * NB // 2, c * a.hpc + j, :]
                        src = ps[:, h, 0:NB * CK // 2].rearrange("p (b n) -> p b n", n=CK)
                        m = cst[:, a.mask_col + j:a.mask_col + j + 1]
                        if a.bias:
                            ins = eng.tensor_scalar(dst, src, vec[:, V_BK + c:V_BK + c + 1], m, ALU.add, ALU.mult)
                        else:
                            ins = eng.tensor_scalar(dst, src, m, None, ALU.mult)
                    ins.then_inc(a.s("km"), 1)
            for b in range(NB):
                eng.wait_ge(a.s("v"), b + 1)
                dst = a.v.rearrange("p (b h n) -> p b h n", b=NB, h=a.H)[:, b, :, 0:a.dh]
                src = ps[0:CK, 2 + b % 2, 0:a.inner].rearrange("p (h n) -> p h n", n=a.dh)
                if a.bias:
                    bv = vec[0:CK, V_BV:V_BV + a.inner].rearrange("p (h n) -> p h n", n=a.dh)
                    eng.tensor_tensor(dst, src, bv, ALU.add).then_inc(a.s("vs"), 1)
                else:
                    eng.tensor_copy(dst, src).then_inc(a.s("vs"), 1)

        def pipelined(eng, front, back):
            def batch(i):
                front(i, 1)
                back(i, 0)
                front(i + 1, 0)
                back(i, 1)

            front(0, 0)
            batch(0)
            with eng.Fori(1, NB - 1) as i:
                batch(i)
            front(NB - 1, 1)
            back(NB - 1, 0)
            back(NB - 1, 1)

        def per_batch(eng, body):
            body(0)
            with eng.Fori(1, NB) as i:
                body(i)

        def att_tensor(eng, a):
            def front(i, u):
                t = i * 2 + u
                eng.wait_ge(a.s("xn"), t + 1)
                for c in range(DC):
                    mm = eng.transpose(ps[:, 4, c * P:(c + 1) * P], xn[:, 0, c * P:(c + 1) * P], ident)
                mm.then_inc(a.s("xt"), 1)
                eng.wait_ge(a.s("xts"), t + 1)
                free(eng, a.s("pb"), t - 1)
                for c in range(a.nc):
                    for k in range(DC):
                        mm = eng.matmul(ps[:, 5, c * P:(c + 1) * P], a.wq[:, k, c * P:(c + 1) * P],
                                        xnt[:, 0, k * P:(k + 1) * P], start=(k == 0), stop=(k == DC - 1))
                mm.then_inc(a.s("q"), 1)
                eng.wait_ge(a.s("qs"), (t + 1) * a.nc)
                free(eng, a.s("clip"), t)
                for c in range(a.nc):
                    for h in range(a.per):
                        mm = eng.matmul(ps[:, c * a.per + h, 0:a.w], qt[:, c * P:(c + 1) * P],
                                        cols(a.km, i * (a.H * CK) + (c * a.per + h) * a.w, a.w),
                                        start=True, stop=True)
                mm.then_inc(a.s("sc"), 1)

            def back(i, u):
                t = i * 2 + u
                eng.wait_ge(a.s("p"), t + 1)
                for g in range(a.groups):
                    if g >= 2:
                        eng.wait_ge(a.s("pts"), t * a.groups + g - 1)
                    else:
                        free(eng, a.s("pts"), t * a.groups)
                    for j in range(4):
                        h = 4 * g + j
                        mm = eng.transpose(ps[0:CK, 6 + g % 2, j * P:(j + 1) * P], p_exp[:, h * CK:(h + 1) * CK], ident)
                    mm.then_inc(a.s("pt"), 1)
                nv = a.dh + 1
                free(eng, a.s("pb"), t)
                for g in range(a.groups):
                    eng.wait_ge(a.s("pts"), t * a.groups + g + 1)
                    for j in range(4):
                        h = 4 * g + j
                        hb = 4 if a.n else 16
                        mm = eng.matmul(ps[:, 4 + h // hb, (h % hb) * nv:(h % hb + 1) * nv], a.pt[:, h * P:(h + 1) * P],
                                        cols(a.v, i * (a.H * nv) + h * nv, nv), start=True, stop=True)
                mm.then_inc(a.s("pv"), 1)
                eng.wait_ge(a.s("on"), t + 1)
                for c in range(a.nc):
                    mm = eng.transpose(ps[:, 4, c * P:(c + 1) * P], o_n[:, c * P:(c + 1) * P], ident)
                mm.then_inc(a.s("ot"), 1)
                eng.wait_ge(a.s("ots"), t + 1)
                for c in range(a.nc):
                    mm = eng.matmul(ps[:, 5, 0:D], ot[:, c * P:(c + 1) * P], a.wo[:, c, :],
                                    start=(c == 0), stop=(c == a.nc - 1))
                mm.then_inc(a.s("pr"), 1)

            eng.wait_ge(a.s("km"), a.H)
            eng.wait_ge(a.s("vs"), NB)
            eng.wait_ge(a.s("ones"), 1)
            pipelined(eng, front, back)

        def att_vector(eng, a):
            H = a.H
            s3 = s_exp[:, 0:H * CK].rearrange("p (h n) -> p h n", n=CK)

            def front(i, u):
                t = i * 2 + u
                free(eng, a.s("xt"), t)
                normalize(eng, xn[:, 0, :], t).then_inc(a.s("xn"), 1)
                eng.wait_ge(a.s("sc"), t + 1)
                free(eng, a.s("p"), t)
                s4 = ps[:, 0:a.banks, 0:a.w]
                sx = s_exp[:, 0:H * CK].rearrange("p (k n) -> p k n", k=a.banks)
                lim = CLAMP / a.scale
                if a.clip:
                    eng.tensor_scalar(sx, s4, lim, -lim, ALU.min, ALU.max).then_inc(a.s("clip"), 1)
                    eng.wait_ge(a.s("clip"), t + 1)
                    eng.reduce_max(red[:, 0:H], s3, AX).then_inc(a.s("max"), 1)
                    eng.wait_ge(a.s("max"), t + 1)
                    eng.tensor_tensor(s3, s3, red[:, 0:H].unsqueeze(2).to_broadcast([P, H, CK]),
                                      ALU.subtract).then_inc(a.s("sub"), 1)
                else:
                    s4 = ps[:, 0:a.banks, 0:a.w].rearrange("p k (h n) -> p k h n", n=CK)
                    sx = s_exp[:, 0:H * CK].rearrange("p (k h n) -> p k h n", k=a.banks, n=CK)
                    r4 = red[:, 0:H].rearrange("p (k h) -> p k h", k=a.banks)
                    eng.reduce_max(r4, s4, AX).then_inc(a.s("max"), 1)
                    eng.wait_ge(a.s("max"), t + 1)
                    for k in range(a.banks):
                        ins = eng.tensor_tensor(sx[:, k], s4[:, k], r4[:, k].unsqueeze(2).to_broadcast([P, a.hb, CK]),
                                                ALU.subtract)
                    ins.then_inc(a.s("clip"), 1)

            def back(i, u):
                t = i * 2 + u
                nv = a.dh + 1
                eng.wait_ge(a.s("pv"), t + 1)
                hb = 4 if a.n else 16
                nb = H // hb
                for k in range(nb):
                    pv = ps[:, 4 + k, 0:hb * nv].rearrange("p (h n) -> p h n", n=nv)
                    ins = eng.reciprocal(rec[:, k * hb:(k + 1) * hb], pv[:, :, a.dh])
                ins.then_inc(a.s("rec"), 1)
                eng.wait_ge(a.s("rec"), t + 1)
                for k in range(nb):
                    pv = ps[:, 4 + k, 0:hb * nv].rearrange("p (h n) -> p h n", n=nv)
                    dst = o_n[:, k * hb * a.dh:(k + 1) * hb * a.dh].rearrange("p (h n) -> p h n", n=a.dh)
                    ins = eng.tensor_tensor(dst, pv[:, :, 0:a.dh],
                                            rec[:, k * hb:(k + 1) * hb].unsqueeze(2).to_broadcast([P, hb, a.dh]), ALU.mult)
                ins.then_inc(a.s("on"), 1)
                eng.wait_ge(a.s("pr"), t + 1)
                vb = V_BO1 if a.n else V_BO0
                eng.tensor_tensor(xn[:, 1, :], ps[:, 5, 0:D], vec[:, vb:vb + D], ALU.add).then_inc(a.s("pb"), 1)
                eng.wait_ge(a.s("pb"), t + 1)
                eng.tensor_tensor(xtile(t), xtile(t), xn[:, 1, :], ALU.add).then_inc(a.s("x"), 1)

            pipelined(eng, front, back)
            eng.wait_ge(a.s("x"), NT)

        def att_scalar(eng, a):
            def evacuate(i, u):
                t = i * 2 + u
                eng.wait_ge(a.s("xt"), t + 1)
                free(eng, a.s("q"), t)
                eng.activation(xnt[:, 0, :], ps[:, 4, 0:D], ACT.Copy).then_inc(a.s("xts"), 1)
                eng.wait_ge(a.s("q"), t + 1)
                free(eng, a.s("sc"), t)
                for c in range(a.nc):
                    if a.bias:
                        eng.activation(qt[:, c * P:(c + 1) * P], ps[:, 5, c * P:(c + 1) * P], ACT.Identity,
                                       bias=vec[:, V_BQ + c:V_BQ + c + 1]).then_inc(a.s("qs"), 1)
                if not a.bias:
                    eng.activation(qt[:, 0:a.inner], ps[:, 5, 0:a.inner], ACT.Copy).then_inc(a.s("qs"), a.nc)

            def exponential(i, u):
                t = i * 2 + u
                eng.wait_ge(a.s("sub" if a.clip else "clip"), t + 1)
                free(eng, a.s("pt"), t * a.groups)
                eng.activation(p_exp[:, 0:a.H * CK], s_exp[:, 0:a.H * CK], ACT.Exp, scale=a.scale).then_inc(a.s("p"), 1)

            def turned(i, u):
                t = i * 2 + u
                for g in range(a.groups):
                    eng.wait_ge(a.s("pt"), t * a.groups + g + 1)
                    free(eng, a.s("pv"), t)
                    eng.activation(a.pt[:, g * 4 * P:(g + 1) * 4 * P], ps[0:CK, 6 + g % 2, :], ACT.Copy)\
                       .then_inc(a.s("pts"), 1)

            def output(i, u):
                t = i * 2 + u
                eng.wait_ge(a.s("ot"), t + 1)
                free(eng, a.s("pr"), t)
                eng.activation(ot[:, 0:a.inner], ps[:, 4, 0:a.inner], ACT.Copy).then_inc(a.s("ots"), 1)

            def step(i, u, j, v):
                evacuate(j, v)
                turned(i, u)
                exponential(j, v)
                output(i, u)

            evacuate(0, 0)
            exponential(0, 0)
            step(0, 0, 0, 1)
            step(0, 1, 1, 0)
            with eng.Fori(1, NB - 1) as i:
                step(i, 0, i, 1)
                step(i, 1, i + 1, 0)
            step(NB - 1, 0, NB - 1, 1)
            turned(NB - 1, 1)
            output(NB - 1, 1)

        for n in range(2):
            for name in ("xn", "t", "xf", "hi", "lo", "l", "lb", "g"):
                sem(f"rt{n}_{name}")

        def route_vector(eng, n):
            def tile(i, u):
                t = i * 2 + u
                free(eng, sem(f"rt{n}_t"), i * 2)
                normalize(eng, xn[:, u, :], t).then_inc(sem(f"rt{n}_xn"), 1)

            def rest(i, u):
                t = i * 2 + u
                if n == 0:
                    eng.wait_ge(sem(f"rt{n}_hi"), t + 1)
                    for c in range(DC):
                        ins = eng.scalar_tensor_tensor(out=cols(xt[:, 1, c, :], t * P, P), in0=ps[:, 4 + u, c * P:(c + 1) * P],
                                                       scalar=XS, in1=cols(xt[:, 0, c, :], t * P, P),
                                                       op0=ALU.mult, op1=ALU.subtract)
                    ins.then_inc(sem(f"rt{n}_lo"), 1)
                eng.wait_ge(sem(f"rt{n}_l"), t + 1)
                if n == 0:
                    eng.tensor_tensor(cols(lg, t * E, E), ps[:, 6 + u, 0:E], vec[:, V_BR:V_BR + E],
                                      ALU.add).then_inc(sem(f"rt{n}_lb"), 1)
                else:
                    eng.tensor_copy(cols(lg, t * E, E), ps[:, 6 + u, 0:E]).then_inc(sem(f"rt{n}_lb"), 1)

            def body(i):
                tile(i, 0)
                tile(i, 1)
                rest(i, 0)
                rest(i, 1)

            per_batch(eng, body)
            eng.wait_ge(sem(f"rt{n}_lb"), NT)

        def route_tensor(eng, n):
            wr = vec[:, (V_WR1 if n else V_WR0):(V_WR1 if n else V_WR0) + DC * E].rearrange("p (k e) -> p k e", k=DC)
            eng.wait_ge(att[n].s("x"), NT)
            def body(i):
                for u in range(2):
                    t = i * 2 + u
                    eng.wait_ge(sem(f"rt{n}_xn"), t + 1)
                    if n == 0:
                        free(eng, sem(f"rt{n}_lo"), i * 2)
                    free(eng, sem(f"rt{n}_xf"), i * 2)
                    for c in range(DC):
                        mm = eng.transpose(ps[:, 4 + u, c * P:(c + 1) * P], xn[:, u, c * P:(c + 1) * P], ident)
                    mm.then_inc(sem(f"rt{n}_t"), 1)
                for u in range(2):
                    t = i * 2 + u
                    eng.wait_ge(sem(f"rt{n}_xf"), t + 1)
                    free(eng, sem(f"rt{n}_lb"), i * 2)
                    for c in range(DC):
                        mm = eng.matmul(ps[:, 6 + u, 0:E], xnt[:, u, c * P:(c + 1) * P], wr[:, c, :],
                                        start=(c == 0), stop=(c == DC - 1))
                    mm.then_inc(sem(f"rt{n}_l"), 1)

            per_batch(eng, body)

        def route_scalar(eng, n):
            def body(i):
                for u in range(2):
                    t = i * 2 + u
                    eng.wait_ge(sem(f"rt{n}_t"), t + 1)
                    free(eng, sem(f"rt{n}_l"), i * 2)
                    eng.activation(xnt[:, u, :], ps[:, 4 + u, 0:D], ACT.Copy).then_inc(sem(f"rt{n}_xf"), 1)
                    if n == 0:
                        for c in range(DC):
                            ins = eng.activation(cols(xt[:, 0, c, :], t * P, P), ps[:, 4 + u, c * P:(c + 1) * P],
                                                 ACT.Copy, scale=XS)
                        ins.then_inc(sem(f"rt{n}_hi"), 1)

            per_batch(eng, body)

        def bcast(ap):
            return ap.unsqueeze(2).to_broadcast([P, NT, E])

        def g3(k):
            return gt[:, k, :].rearrange("p (t e) -> p t e", e=E)

        rev3 = cst[:, C_REV:C_REV + NT * E].rearrange("p (t e) -> p t e", e=E)
        row3 = cst[:, C_ROW:C_ROW + NT * E].rearrange("p (t e) -> p t e", e=E)
        col3 = cst[:, C_COL:C_COL + NT * E].rearrange("p (t e) -> p t e", e=E)
        lg3 = lg[:, :].rearrange("p (t e) -> p t e", e=E)

        class Chain:

            def __init__(self, eng, name):
                self.eng, self.sem, self.n = eng, sem(name), 0

            def __call__(self, ins):
                self.n += 1
                ins.then_inc(self.sem, 1)
                self.eng.wait_ge(self.sem, self.n)

        def first_max(eng, ch, values, top, tmp, one_hot):
            ch(eng.reduce_max(top, values, AX))
            ch(eng.tensor_tensor(tmp, values, bcast(top), ALU.is_equal))
            ch(eng.tensor_tensor(tmp, tmp, rev3, ALU.mult))
            ch(eng.reduce_max(gs[:, 11, :], tmp, AX))
            ch(eng.tensor_tensor(one_hot, tmp, bcast(gs[:, 11, :]), ALU.is_equal))

        sem("oht"), sem("ohts"), sem("b2"), sem("f0_yx")

        def gate0_vector(eng):
            ch = Chain(eng, "gate0")
            first_max(eng, ch, lg3, gs[:, 0, :], g3(0), g3(1))
            ch(eng.tensor_scalar(gt[:, 2, :], gt[:, 1, :], 1.0 / (WS * HS0), None, ALU.mult))
            for t in range(NT):
                eng.wait_ge(sem("b2"), t + 1)
                eng.tensor_tensor(xtile(t), xtile(t), ps[:, 2 + t % 2, 0:D], ALU.add).then_inc(sem("f0_yx"), 1)
            eng.wait_ge(sem("f0_yx"), NT)

        GATE0_STEPS = 6

        def gate0_tensor(eng):
            eng.wait_ge(sem("gate0"), GATE0_STEPS - 1)
            for t in range(NT):
                if t >= 2:
                    eng.wait_ge(sem("ohts"), t - 1)
                eng.transpose(ps[0:E, t % 2, 0:P], gt[:, 1, t * E:(t + 1) * E], ident).then_inc(sem("oht"), 1)
                if t >= 2:
                    eng.wait_ge(sem("f0_yx"), t - 1)
                eng.wait_ge(sem("ohts"), t + 1)
                eng.matmul(ps[:, 2 + t % 2, 0:D], xnt[0:E, 0, (t % 2) * P:(t % 2 + 1) * P], b2_sb[:, :],
                           start=True, stop=True).then_inc(sem("b2"), 1)

        def gate0_scalar(eng):
            for t in range(NT):
                eng.wait_ge(sem("oht"), t + 1)
                if t >= 2:
                    eng.wait_ge(sem("b2"), t - 1)
                eng.activation(xnt[0:E, 0, (t % 2) * P:(t % 2 + 1) * P], ps[0:E, t % 2, 0:P], ACT.Copy)\
                   .then_inc(sem("ohts"), 1)

        sem("gmax"), sem("gexp"), sem("p1"), sem("m1k"), sem("p2"), sem("gdone")

        def gate1_vector(eng):
            ch = Chain(eng, "gate1")
            bc = bcast
            ch(eng.reduce_max(gs[:, 0, :], lg3, AX))
            eng.tensor_tensor(g3(0), lg3, bc(gs[:, 0, :]), ALU.subtract).then_inc(sem("gmax"), 1)
            eng.wait_ge(sem("gexp"), 1)
            ch(eng.reduce_sum(gs[:, 1, :], g3(1), AX))
            ch(eng.reciprocal(gs[:, 1, :], gs[:, 1, :]))
            ch(eng.tensor_tensor(g3(2), g3(1), bc(gs[:, 1, :]), ALU.mult))
            first_max(eng, ch, g3(2), gs[:, 2, :], g3(0), g3(3))
            ch(eng.tensor_scalar(gt[:, 1, :], gt[:, 3, :], -1.0, 1.0, ALU.mult, ALU.add))
            ch(eng.tensor_tensor(g3(1), g3(1), g3(2), ALU.mult))
            first_max(eng, ch, g3(1), gs[:, 3, :], g3(0), g3(4))
            assert ch.n == 16

            def kept(bank, m, dst):
                for par in range(2):
                    src = ps[:, bank + par, 0:NB * E].rearrange("p (g e) -> p g e", e=E)
                    ch(eng.tensor_copy(gt[:, dst, :].rearrange("p (g u e) -> p g u e", u=2, e=E)[:, :, par, :], src))
                ch(eng.tensor_scalar(gt[:, 0, :], gt[:, dst, :], float(CAP), None, ALU.is_lt))
                ch(eng.tensor_tensor(gt[:, m, :], gt[:, m, :], gt[:, 0, :], ALU.mult))

            eng.wait_ge(sem("p1"), 1)
            kept(0, 3, 5)
            eng.sem_inc(sem("m1k"), 1)
            eng.wait_ge(sem("p2"), 1)
            kept(2, 4, 6)
            for c, (m, pos) in enumerate(((3, 5), (4, 6))):
                ch(eng.reduce_sum(gs[:, 4, :], g3(m), AX))
                ch(eng.tensor_tensor(gs[:, 2 + c, :], gs[:, 2 + c, :], gs[:, 4, :], ALU.mult))
                ch(eng.tensor_tensor(g3(0), g3(pos), row3, ALU.add))
                ch(eng.tensor_tensor(g3(0), g3(0), g3(m), ALU.mult))
                ch(eng.reduce_sum(gs[:, 5, :], g3(0), AX))
                ch(eng.tensor_copy(gi[:, c, :], gs[:, 5, :]))
                ch(eng.tensor_tensor(g3(0), g3(pos), col3, ALU.add))
                ch(eng.tensor_tensor(g3(0), g3(0), g3(m), ALU.mult))
                ch(eng.reduce_sum(gs[:, 6, :], g3(0), AX))
                ch(eng.tensor_scalar(gs[:, 7 + c, :], gs[:, 6, :], -1.0, None, ALU.add))
            eng.sem_inc(sem("gdone"), 1)

        def gate1_tensor(eng):
            def view(k, par):
                return gt[:, k, :].rearrange("p (g u e) -> p g u e", u=2, e=E)[:, :, par, :]

            def o(b):
                return ps[:, b, 0:NB * E].rearrange("p (g e) -> p g e", e=E)

            eng.wait_ge(sem("gate1"), 16)
            eng.matmul(o(0), tri, view(3, 0), start=True, stop=True)
            eng.matmul(o(1), ones, view(3, 0), start=True, stop=False)
            eng.matmul(o(1), tri, view(3, 1), start=False, stop=True).then_inc(sem("p1"), 1)
            eng.wait_ge(sem("m1k"), 1)
            eng.matmul(o(2), ones, view(3, 0), start=True, stop=False)
            eng.matmul(o(2), ones, view(3, 1), start=False, stop=False)
            eng.matmul(o(2), tri, view(4, 0), start=False, stop=True)
            eng.matmul(o(3), ones, view(3, 0), start=True, stop=False)
            eng.matmul(o(3), ones, view(3, 1), start=False, stop=False)
            eng.matmul(o(3), ones, view(4, 0), start=False, stop=False)
            eng.matmul(o(3), tri, view(4, 1), start=False, stop=True).then_inc(sem("p2"), 1)

        def gate1_scalar(eng):
            eng.wait_ge(sem("gmax"), 1)
            eng.activation(gt[:, 1, :], gt[:, 0, :], ACT.Exp).then_inc(sem("gexp"), 1)

        sem("dxn"), sem("dxh"), sem("dxl"), sem("dd1"), sem("dd"), sem("dmm"), sem("dhi"), sem("dlo")

        def dispatch_vector(eng):
            def body(g):
                free(eng, sem("dmm"), g)
                for u in range(2):
                    t = g * 2 + u
                    normalize(eng, xn[:, u, :], t).then_inc(sem("dxn"), 1)
                    eng.tensor_scalar(disp[:, u, :], iota, cols(gs[:, 7, :], t, 1), None, ALU.is_equal).then_inc(sem("dd1"), 1)
                for u in range(2):
                    t = g * 2 + u
                    eng.wait_ge(sem("dxn"), t + 1)
                    eng.tensor_copy(xh[:, 0, u, :], xn[:, u, :]).then_inc(sem("dxh"), 1)
                    eng.wait_ge(sem("dxh"), t + 1)
                    eng.tensor_tensor(xh[:, 1, u, :], xn[:, u, :], xh[:, 0, u, :], ALU.subtract).then_inc(sem("dxl"), 1)
                    eng.wait_ge(sem("dd1"), t + 1)
                    eng.scalar_tensor_tensor(out=disp[:, u, :], in0=iota, scalar=cols(gs[:, 8, :], t, 1),
                                             in1=disp[:, u, :], op0=ALU.is_equal, op1=ALU.add).then_inc(sem("dd"), 1)
                eng.wait_ge(sem("dmm"), g + 1)
                for c in range(DC):
                    ins = eng.tensor_copy(cols(xt[:, 1, c, :], g * SL, SL), ps[:, 2 + c, :])
                ins.then_inc(sem("dlo"), 1)

            per_batch(eng, body)

        def dispatch_scalar(eng):
            def body(g):
                eng.wait_ge(sem("dmm"), g + 1)
                met(eng)
                for c in range(DC):
                    ins = eng.activation(cols(xt[:, 0, c, :], g * SL, SL), ps[:, c, :], ACT.Copy)
                ins.then_inc(sem("dhi"), 1)

            per_batch(eng, body)

        def dispatch_tensor(eng):
            eng.wait_ge(sem("gdone"), 1)
            def body(g):
                eng.wait_ge(sem("dd"), (g + 1) * 2)
                eng.wait_ge(sem("dxl"), (g + 1) * 2)
                free(eng, sem("dhi"), g)
                free(eng, sem("dlo"), g)
                for part in range(2):
                    for c in range(DC):
                        for u in range(2):
                            mm = eng.matmul(ps[:, 2 * part + c, :], xh[:, part, u, c * P:(c + 1) * P], disp[:, u, :],
                                            start=(u == 0), stop=(u == 1))
                mm.then_inc(sem("dmm"), 1)

            per_batch(eng, body)

        def flat_w(par, part):
            return arena[:, par, part, :]

        PIECES = [
            [(f0w1, DC * F0, 0), (f0w2, FC0 * D, DC * F0)],
            [(f1w0, DC * F1, 0), (f1w1, DC * F1, DC * F1), (f1wo, FC1 * D, 2 * DC * F1)],
        ]
        for n in range(2):
            for name in ("st0", "st1", "wsc", "whi", "w", "h", "b", "g", "m", "hi", "lo", "y", "yx"):
                sem(f"f{n}_{name}")
        UNITS = [4 * FC0, FC1]
        FIRST_E = E // 2

        def weights_loads(eng, n):
            np_ = len(PIECES[n])

            def pair(i, first):
                for k in range(2 * np_):
                    e, (src, size, _) = i * 2 + k // np_, PIECES[n][k % np_]
                    piece = i * (2 * np_) + k
                    if not (first and k < 2):
                        eng.wait_ge(sem(f"f{n}_w"), piece - 1)
                    s = sem(f"f{n}_st{k % 2}")
                    if n == 1 and k % np_ == 2:
                        full = (FC1 - 1) * D
                        srcm = src[bass.ds(e, 1), 0:(FC1 - 1) * P, :] if not isinstance(e, int) else src[e:e + 1, 0:(FC1 - 1) * P, :]
                        eng.dma_start(stage[:, k % 2, 0:full].rearrange("p (k n) -> p k n", n=D),
                                      srcm.rearrange("e (k p) n -> p (e k) n", p=P)).then_inc(s, 16)
                        srct = src[bass.ds(e, 1), (FC1 - 1) * P:F1, :] if not isinstance(e, int) else src[e:e + 1, (FC1 - 1) * P:F1, :]
                        eng.dma_start(stage[0:FT1, k % 2, full:full + D], srct.rearrange("e p n -> p (e n)")).then_inc(s, 16)
                    else:
                        width = src.shape[2]
                        s_ = src[bass.ds(e, 1)] if not isinstance(e, int) else src[e:e + 1]
                        eng.dma_start(stage[:, k % 2, 0:size].rearrange("p (k n) -> p k n", n=width),
                                      s_.rearrange("e (k p) n -> p (e k) n", p=P)).then_inc(s, 16)

            if n == 0:
                eng.wait_ge(att[0].s("vs"), NB)
            pair(0, True)
            with eng.Fori(1, FIRST_E) as i:
                pair(i, False)

        def staged(n, i, k):
            np_ = len(PIECES[n])
            per = [sum(32 if (n == 1 and q % np_ == 2) else 16 for q in range(s, 2 * np_, 2)) for s in range(2)]
            mine = sum(32 if (n == 1 and q % np_ == 2) else 16 for q in range(k % 2, k + 1, 2))
            return i * per[k % 2] + mine

        def weights_split(eng, n):
            np_ = len(PIECES[n])

            def pair(i, first):
                for k in range(2 * np_):
                    par, q = k // np_, k % np_
                    _, size, at = PIECES[n][q]
                    eng.wait_ge(sem(f"f{n}_st{k % 2}"), staged(n, i, k))
                    if q == 0 and not first:
                        eng.wait_ge(sem(f"f{n}_y"), i * (2 * UNITS[n]) + (par - 1) * UNITS[n])
                    piece = i * (2 * np_) + k
                    spans = [(0, size, P)]
                    if n == 1 and q == 2:
                        spans = [(0, size - D, P), (size - D, size, FT1)]
                    extra = (i * 2 + par + (q == 2)) if n else 0
                    met(eng)
                    for lo, hi, rows in spans:
                        st = stage[0:rows, k % 2, lo:hi]
                        eng.tensor_scalar(st, st, WS, None, ALU.mult).then_inc(sem(f"f{n}_wsc"), 1)
                    eng.wait_ge(sem(f"f{n}_wsc"), piece + 1 + extra)
                    met(eng)
                    for lo, hi, rows in spans:
                        eng.tensor_copy(flat_w(par, 0)[0:rows, at + lo:at + hi], stage[0:rows, k % 2, lo:hi])\
                           .then_inc(sem(f"f{n}_whi"), 1)
                    eng.wait_ge(sem(f"f{n}_whi"), piece + 1 + extra)
                    met(eng)
                    for lo, hi, rows in spans:
                        ins = eng.tensor_tensor(flat_w(par, 1)[0:rows, at + lo:at + hi], stage[0:rows, k % 2, lo:hi],
                                                flat_w(par, 0)[0:rows, at + lo:at + hi], ALU.subtract)
                    ins.then_inc(sem(f"f{n}_w"), 1)

            eng.wait_ge(att[n].s("x"), NT)
            pair(0, True)
            with eng.Fori(1, FIRST_E) as i:
                pair(i, False)

        def three(eng, out_ap, a, b, first, last):
            eng.matmul(out_ap, a[0], b[0], start=first, stop=False)
            eng.matmul(out_ap, a[0], b[1], start=False, stop=False)
            return eng.matmul(out_ap, a[1], b[0], start=False, stop=last)

        def ffn0_tensor(eng):
            def hidden(i, k):
                par, r = divmod(k, UNITS[0])
                n, f = divmod(r, FC0)
                if r == 0:
                    eng.wait_ge(sem("f0_w"), i * 4 + par * 2 + 1)
                if k >= 2:
                    eng.wait_ge(sem("f0_g"), i * (2 * UNITS[0]) + k - 1)
                w = [flat_w(par, s)[:, 0:DC * F0].rearrange("p (c n) -> p c n", c=DC) for s in range(2)]
                for c in range(DC):
                    mm = three(eng, ps[:, k % 2, :], [w[s][:, c, f * P:(f + 1) * P] for s in range(2)],
                               [xt[:, s, c, n * 4 * P:(n + 1) * 4 * P] for s in range(2)], c == 0, c == DC - 1)
                mm.then_inc(sem("f0_h"), 1)

            def output(i, k):
                par, r = divmod(k, UNITS[0])
                n, f = divmod(r, FC0)
                eng.wait_ge(sem("f0_lo"), i * (2 * UNITS[0]) + k + 1)
                if r == 0:
                    eng.wait_ge(sem("f0_w"), i * 4 + par * 2 + 2)
                if f == 0:
                    eng.wait_ge(sem("f0_yx"), i * (2 * NT) + (NT + par * NT + n * 4))
                w = [flat_w(par, s)[:, DC * F0 + f * D:DC * F0 + (f + 1) * D] for s in range(2)]
                for j in range(4):
                    mm = three(eng, ps[:, 4 + j, 0:D], [(hh, hl)[s][:, k % 2, j * P:(j + 1) * P] for s in range(2)],
                               w, f == 0, f == FC0 - 1)
                mm.then_inc(sem("f0_y"), 1)

            eng.wait_ge(sem("rt0_lo"), NT)
            eng.wait_ge(sem("f0_yx"), NT)
            with eng.Fori(0, FIRST_E) as i:
                for k in range(2 * UNITS[0]):
                    hidden(i, k)
                    if k:
                        output(i, k - 1)
                output(i, 2 * UNITS[0] - 1)

        def ffn0_scalar(eng):
            with eng.Fori(0, FIRST_E) as i:
                base = i * (2 * UNITS[0])
                for k in range(2 * UNITS[0]):
                    par, r = divmod(k, UNITS[0])
                    f = r % FC0
                    eng.wait_ge(sem("f0_h"), base + k + 1)
                    if k >= 2:
                        eng.wait_ge(sem("f0_lo"), base + k - 1)
                    met(eng)
                    eng.activation(hid[:, k % 2, :], ps[:, k % 2, :], ACT.Gelu,
                                   bias=cols(vec, i * (2 * FC0) + V_B1 + par * FC0 + f, 1),
                                   scale=1.0 / (WS * XS)).then_inc(sem("f0_g"), 1)
                    eng.wait_ge(sem("f0_g"), base + k + 1)
                    if k >= 2:
                        eng.wait_ge(sem("f0_y"), base + k - 1)
                    eng.activation(hh[:, k % 2, :], hid[:, k % 2, :], ACT.Copy, scale=HS0).then_inc(sem("f0_hi"), 1)

        def ffn0_vector(eng):
            with eng.Fori(0, FIRST_E) as i:
                base = i * (2 * UNITS[0])
                for k in range(2 * UNITS[0]):
                    par, r = divmod(k, UNITS[0])
                    n, f = divmod(r, FC0)
                    eng.wait_ge(sem("f0_hi"), base + k + 1)
                    eng.scalar_tensor_tensor(out=hl[:, k % 2, :], in0=hid[:, k % 2, :], scalar=HS0, in1=hh[:, k % 2, :],
                                             op0=ALU.mult, op1=ALU.subtract).then_inc(sem("f0_lo"), 1)
                    if f == FC0 - 1:
                        eng.wait_ge(sem("f0_y"), base + k + 1)
                        for j in range(4):
                            t = 4 * n + j
                            eng.scalar_tensor_tensor(out=xtile(t), in0=ps[:, 4 + j, 0:D],
                                                     scalar=cols(gt[:, 2, :], i * 2 + (t * E + par), 1),
                                                     in1=xtile(t), op0=ALU.mult, op1=ALU.add).then_inc(sem("f0_yx"), 1)
            eng.wait_ge(sem("f0_yx"), (E + 1) * NT)

        def ffn1_tensor(eng):
            U = UNITS[1]

            def rows(k):
                return FT1 if k % U == FC1 - 1 else P

            def hidden(i, k):
                par, f = divmod(k, U)
                m = rows(k)
                if k >= 2:
                    eng.wait_ge(sem("f1_m"), i * (2 * U) + k - 1)
                for which in range(2):
                    if f == 0:
                        eng.wait_ge(sem("f1_w"), i * 6 + par * 3 + which + 1)
                    w = [flat_w(par, s)[:, which * DC * F1:(which + 1) * DC * F1].rearrange("p (c n) -> p c n", c=DC)
                         for s in range(2)]
                    for c in range(DC):
                        xe = [xt[:, s, c, :].rearrange("p (g e n) -> p g e n", g=NB, e=E) for s in range(2)]
                        e_sel = [v[:, :, bass.ds(i * 2 + par, 1), :].rearrange("p g e n -> p g (e n)") for v in xe]
                        mm = three(eng, ps[0:m, 2 * which + k % 2, :].rearrange("p (g n) -> p g n", g=NB),
                                   [w[s][:, c, f * P:f * P + m] for s in range(2)], e_sel, c == 0, c == DC - 1)
                    mm.then_inc(sem("f1_b" if which else "f1_h"), 1)

            def output(i, k):
                par, f = divmod(k, U)
                m = rows(k)
                eng.wait_ge(sem("f1_lo"), i * (2 * U) + k + 1)
                if f == 0:
                    eng.wait_ge(sem("f1_w"), i * 6 + par * 3 + 3)
                    eng.wait_ge(sem("f1_yx"), i * 2 + (par + 1))
                at = 2 * DC * F1 + f * D
                w = [flat_w(par, s)[0:m, at:at + D] for s in range(2)]
                for j in range(4):
                    mm = three(eng, ps[:, 4 + j, 0:D], [(hh, hl)[s][0:m, k % 2, j * P:(j + 1) * P] for s in range(2)],
                               w, f == 0, f == FC1 - 1)
                mm.then_inc(sem("f1_y"), 1)

            eng.wait_ge(sem("dhi"), NB)
            eng.wait_ge(sem("dlo"), NB)
            with eng.Fori(0, FIRST_E) as i:
                for k in range(2 * U):
                    hidden(i, k)
                    if k:
                        output(i, k - 1)
                output(i, 2 * U - 1)

        def ffn1_scalar(eng):
            U = UNITS[1]
            eng.sem_inc(sem("f1_yx"), 1)
            eng.sem_inc(sem("f1_out"), 16)
            with eng.Fori(0, FIRST_E) as i:
                base = i * (2 * U)
                for k in range(2 * U):
                    par, f = divmod(k, U)
                    m = FT1 if f == FC1 - 1 else P
                    eng.wait_ge(sem("f1_h"), base + k + 1)
                    if k >= 2:
                        eng.wait_ge(sem("f1_m"), base + k - 1)
                    eng.activation(hga[0:m, k % 2, :], ps[0:m, k % 2, :], ACT.Gelu_apprx_tanh,
                                   scale=1.0 / WS).then_inc(sem("f1_g"), 1)
                    eng.wait_ge(sem("f1_m"), base + k + 1)
                    if k >= 2:
                        eng.wait_ge(sem("f1_y"), base + k - 1)
                    eng.activation(hh[0:m, k % 2, :], hid[0:m, k % 2, :], ACT.Copy).then_inc(sem("f1_hi"), 1)
                    if f == FC1 - 1:
                        eng.wait_ge(sem("f1_y"), base + k + 1)
                        eng.wait_ge(sem("f1_out"), i * 32 + (par + 1) * 16)
                        eng.activation(y_sb[:, :].rearrange("p (j n) -> p j n", n=D), ps[:, 4:8, 0:D], ACT.Copy,
                                       scale=1.0 / (WS * HS1)).then_inc(sem("f1_yx"), 1)
                        eng.wait_ge(sem("f1_yx"), i * 2 + (par + 2))
                        dst = y_dram.rearrange("(e j p) n -> e p j n", e=E, p=P)[bass.ds(i * 2 + par, 1)]
                        eng.dma_start(dst.rearrange("e p j n -> p (e j) n"), y_sb[:, :].rearrange("p (j n) -> p j n", n=D))\
                           .then_inc(sem("f1_out"), 16)

        def ffn1_vector(eng):
            U = UNITS[1]
            with eng.Fori(0, FIRST_E) as i:
                base = i * (2 * U)
                for k in range(2 * U):
                    f = k % U
                    m = FT1 if f == FC1 - 1 else P
                    eng.wait_ge(sem("f1_b"), base + k + 1)
                    eng.wait_ge(sem("f1_g"), base + k + 1)
                    if k >= 2:
                        eng.wait_ge(sem("f1_lo"), base + k - 1)
                    eng.scalar_tensor_tensor(out=hid[0:m, k % 2, :], in0=ps[0:m, 2 + k % 2, :], scalar=HS1 / WS,
                                             in1=hga[0:m, k % 2, :], op0=ALU.mult, op1=ALU.mult).then_inc(sem("f1_m"), 1)
                    eng.wait_ge(sem("f1_hi"), base + k + 1)
                    eng.tensor_tensor(hl[0:m, k % 2, :], hid[0:m, k % 2, :], hh[0:m, k % 2, :],
                                      ALU.subtract).then_inc(sem("f1_lo"), 1)

        sem("f1_out")

        for r in range(4):
            sem(f"ga{r}"), sem(f"gb{r}")
        sem("cx1"), sem("cx"), sem("xout")

        def gather_pool(eng):
            eng.wait_ge(sem("f1_out"), 16 * (E + 1))
            for t in range(NT):
                r = t % 4
                if t >= 4:
                    eng.wait_ge(sem("cx"), t - 3)
                for c, (buf, s) in enumerate(((gath, f"ga{r}"), (gath2, f"gb{r}"))):
                    eng.indirect_dma_start(out=buf[:, r * D:(r + 1) * D], out_offset=None, in_=y_dram,
                                           in_offset=bass.IndirectOffsetOnAxis(ap=gi[:, c, t:t + 1], axis=0))\
                       .then_inc(sem(s), 16)

        def combine_vector(eng):
            for t in range(NT):
                r = t % 4
                eng.wait_ge(sem(f"ga{r}"), 16 * (t // 4 + 1))
                eng.scalar_tensor_tensor(out=xtile(t), in0=gath[:, r * D:(r + 1) * D], scalar=gs[:, 2, t:t + 1],
                                         in1=xtile(t), op0=ALU.mult, op1=ALU.add).then_inc(sem("cx1"), 1)
                eng.wait_ge(sem(f"gb{r}"), 16 * (t // 4 + 1))
                eng.wait_ge(sem("cx1"), t + 1)
                eng.scalar_tensor_tensor(out=xtile(t), in0=gath2[:, r * D:(r + 1) * D], scalar=gs[:, 3, t:t + 1],
                                         in1=xtile(t), op0=ALU.mult, op1=ALU.add).then_inc(sem("cx"), 1)

        def x_stores(eng):
            o = out.rearrange("b (u p) n -> p (b u) n", p=P)
            for t in range(0, NT, 4):
                eng.wait_ge(sem("cx"), t + 4)
                eng.dma_start(o[:, t:t + 4, :], x_sb[:, t * D:(t + 4) * D].rearrange("p (t n) -> p t n", n=D))\
                   .then_inc(sem("xout"), 16)
            eng.wait_ge(sem("xout"), 16 * (NT // 4))

        sem("load"), sem("xload")
        for n in range(2):
            sem(f"xc{n}")

        block = ctx.enter_context(nc.Block())

        @block.sync
        def _(sp):
            xv = x.rearrange("b (u p) n -> p (b u) n", p=P)
            for t in range(0, NT, 4):
                sp.dma_start(x_sb[:, t * D:(t + 4) * D].rearrange("p (t n) -> p t n", n=D), xv[:, t:t + 4, :])\
                  .then_inc(sem("xload"), 16)
            sp.dma_start(cst[:, :], consts).then_inc(sem("load"), 16)
            sp.dma_start(vec[:, :], vecs).then_inc(sem("load"), 16)
            sp.dma_start(b2_sb[:, :], b2).then_inc(sem("load"), 16)
            att_loads(sp, att[0])
            weights_loads(sp, 0)
            sp.wait_ge(sem("f0_w"), 2 * E)
            att_loads(sp, att[1])
            sp.wait_ge(att[1].s("vs"), NB)
            weights_loads(sp, 1)
            x_stores(sp)

        @block.gpsimd
        def _(pool):
            for n in range(2):
                a = att[n]
                if n:
                    pool.wait_ge(sem("f0_y"), E * UNITS[0])
                v = a.v.rearrange("p (b h n) -> p b h n", b=NB, h=a.H)
                pool.memset(v[:, :, :, a.dh], 1.0).then_inc(a.s("ones"), 1)
                weights_split(pool, n)
            gather_pool(pool)

        @block.scalar
        def _(act):
            act.wait_ge(sem("load"), 48)
            ln_stats_scalar(act, 0)
            att_scalar(act, att[0])
            ln_stats_scalar(act, 1)
            route_scalar(act, 0)
            gate0_scalar(act)
            ffn0_scalar(act)
            ln_stats_scalar(act, 2)
            att_scalar(act, att[1])
            ln_stats_scalar(act, 3)
            route_scalar(act, 1)
            gate1_scalar(act)
            dispatch_scalar(act)
            ffn1_scalar(act)

        @block.vector
        def _(dve):
            ln_stats_vector(dve, 0, lambda: dve.wait_ge(sem("xload"), 16 * (NT // 4)))
            dve.wait_ge(sem("load"), 48)
            att_kv_vector(dve, att[0])
            att_vector(dve, att[0])
            ln_stats_vector(dve, 1, lambda: dve.wait_ge(att[0].s("x"), NT))
            route_vector(dve, 0)
            gate0_vector(dve)
            ffn0_vector(dve)
            ln_stats_vector(dve, 2, lambda: dve.wait_ge(sem("f0_yx"), (E + 1) * NT))
            att_kv_vector(dve, att[1])
            att_vector(dve, att[1])
            ln_stats_vector(dve, 3, lambda: dve.wait_ge(att[1].s("x"), NT))
            route_vector(dve, 1)
            gate1_vector(dve)
            dispatch_vector(dve)
            ffn1_vector(dve)
            combine_vector(dve)

        @block.tensor
        def _(pe):
            pe.wait_ge(sem("load"), 48)
            att_kv_tensor(pe, att[0])
            att_tensor(pe, att[0])
            route_tensor(pe, 0)
            gate0_tensor(pe)
            ffn0_tensor(pe)
            pe.wait_ge(sem("f0_yx"), (E + 1) * NT)
            att_kv_tensor(pe, att[1])
            att_tensor(pe, att[1])
            route_tensor(pe, 1)
            gate1_tensor(pe)
            dispatch_tensor(pe)
            ffn1_tensor(pe)


def kernel(**inputs):
    import numpy as np
    import concourse.bacc as bacc
    from concourse.bass_utils import run_bass_kernel_spmd

    g = {k: np.ascontiguousarray(v) for k, v in inputs.items()}

    def chunks(w, rows):
        return np.ascontiguousarray(w.reshape(w.shape[0] // rows, rows, w.shape[1]).transpose(1, 0, 2))

    def cols(v):
        return v.reshape(-1, P).T

    def wide(v):
        return np.broadcast_to(v, (P, v.shape[-1]))

    p = np.arange(P)
    t, e = np.arange(NT)[:, None], np.arange(E)[None, :]
    consts = np.concatenate([
        p[:, None] == p[None, :],
        p[:, None] < p[None, :],
        np.ones((P, P)),
        wide(np.arange(SL)[None]),
        wide((np.zeros((NT, 1)) + (E - e)).reshape(1, -1)),
        wide((e * SL + (t // TPB) * CAP).reshape(1, -1)),
        wide((e * CAP + 1 + 0 * t).reshape(1, -1)),
        p[:, None] // 16 == np.arange(8)[None],
        p[:, None] // 64 == np.arange(2)[None],
    ], axis=1).astype(np.float32)
    vecs = np.ascontiguousarray(np.concatenate([
        cols(g["L0_xattn_bq"]), cols(g["L0_xattn_bk"]), cols(g["L0_ffn_b1"].reshape(-1)),
        wide(g["L0_xattn_bv"]), wide(g["L0_xattn_bo"]), wide(g["L1_xattn_bo"]), wide(g["L0_ffn_br"]),
        chunks(g["L0_ffn_wr"], P).reshape(P, -1), chunks(g["L1_ffn_router_w"], P).reshape(P, -1),
    ], axis=1))
    assert consts.shape[1] == C_END and vecs.shape[1] == V_END
    ctx_t = chunks(np.ascontiguousarray(g["ctx_768"].reshape(NB * CK, CC).T), CR)
    arrays = {
        "x": g["x"], "ctx_t": ctx_t, "consts": consts, "vecs": vecs, "b2": g["L0_ffn_b2"],
        "wq0": chunks(g["L0_xattn_Wq"], P), "wk0": chunks(g["L0_xattn_Wk"], CR),
        "wv0": chunks(g["L0_xattn_Wv"], CR), "wo0": chunks(g["L0_xattn_Wo"], P),
        "wq1": chunks(g["L1_xattn_Wq"], P), "wk1": chunks(g["L1_xattn_Wk"], CR),
        "wv1": chunks(g["L1_xattn_Wv"], CR), "wo1": chunks(g["L1_xattn_Wo"], P),
        "f0w1": g["L0_ffn_w1"], "f0w2": g["L0_ffn_w2"],
        "f1w0": g["L1_ffn_w0_kernel"], "f1w1": g["L1_ffn_w1_kernel"], "f1wo": g["L1_ffn_wo_kernel"],
    }
    nc = bacc.Bacc("TRN2", target_bir_lowering=False, num_devices=1)
    args = [nc.dram_tensor(f"in_{k}", a.shape, mybir.dt.from_np(a.dtype), kind="ExternalInput").ap()
            for k, a in arrays.items()]
    out = nc.dram_tensor("out_x", (NB, TPB * P, D), F32, kind="ExternalOutput").ap()
    build(nc, *args, out)
    r = run_bass_kernel_spmd(nc, [{f"in_{k}": a for k, a in arrays.items()}], core_ids=[0])
    return r.results[0]["out_x"]
```

```python
from contextlib import ExitStack

import concourse.bass as bass
from concourse import mybir

F32 = mybir.dt.float32
F16 = mybir.dt.float16
U32 = mybir.dt.uint32
ALU = mybir.AluOpType
ACT = mybir.ActivationFunctionType
AX = mybir.AxisListType.X

P = 128
NB = 8
TPB = 2
NT = NB * TPB
D = 256
DC = D // P
CK = 77
CC = 192
CR = 96
E = 8
F0 = 1024
FC0 = F0 // P
F1 = 1368
FC1 = (F1 + P - 1) // P
FT1 = F1 - (FC1 - 1) * P
CAP = 64
SL = NB * CAP
ST = 256
SLT = NT * P // ST + E - 1
EPS = 1e-5
CLAMP = 10000.0

WS = 128.0
XS = 64.0
HS0 = 8.0
HS1 = 1.0 / 32

C_ID, C_TRI, C_ONE, C_REV, C_ROW, C_J, C_K, C_TOK, C_HM0, C_HM1 = 0, 128, 256, 384, 512, 640, 768, 832, 848, 856
C_END = 858
V_BQ, V_BK, V_BV, V_BO0, V_BO1, V_BR, V_WR0, V_WR1 = 0, 2, 4, 260, 516, 772, 780, 796
V_END = 812


def build(nc, x, ctx_t, consts, vecs, b1c, b2w, wq0, wk0, wv0, wo0, wq1, wk1, wv1, wo1, f0w1, f0w2, f1w0, f1w1, f1wo, out):
    slots0 = nc.dram_tensor("slots0", (SLT * ST, D), F32, kind="Internal").ap()
    slots1 = nc.dram_tensor("slots1", (E * SL + 2 * NT * P, D), F32, kind="Internal").ap()
    y0 = nc.dram_tensor("y0_rows", (SLT * ST, D), F32, kind="Internal").ap()
    y1 = nc.dram_tensor("y1_rows", (E * SL, D), F32, kind="Internal").ap()
    ctx = ExitStack()
    with ctx:
        def sb(name, shape, dt=F32):
            return ctx.enter_context(nc.sbuf_tensor(name, shape, dt))

        sems = {}

        def sem(name):
            if name not in sems:
                sems[name] = ctx.enter_context(nc.semaphore(name))
            return sems[name]

        x_sb = sb("x_sb", [P, NT * D])
        cst = sb("cst", [P, C_END])
        vec = sb("vec", [P, V_END])
        aw = sb("aw", [P, 16 * D])
        xt = sb("xt", [P, 2, 2, DC * SL], F16)
        xns = sb("xns", [P, NT * D])
        xs = sb("xs", [P, 2, 2 * D])
        xs4 = xs[:, :, :].rearrange("p a n -> p (a n)")
        b1t = sb("b1t", [P, 2, FC0])
        b2t = sb("b2t", [P, 2, D])
        texp = sb("texp", [P, NT], U32)
        si = sb("si", [P, 2, NT], U32)
        stage = sb("stage", [P, 2, FC1 * D])
        W1 = 2 * DC * F1 + FC1 * D
        arena = sb("arena", [P, 2, 2, W1], F16)
        s_exp = sb("s_exp", [P, 16 * CK])
        p_exp = sb("p_exp", [P, 16 * CK])
        xn = sb("xn", [P, 2, D])
        xnt = sb("xnt", [P, 2, D])
        red = sb("red", [P, 16])
        rec = sb("rec", [P, 16])
        st6 = sb("st6", [P, NT, 6])
        mv = sb("mv", [P, NT * 2])
        rstd = sb("rstd", [P, NT])
        y_sb = sb("y_sb", [P, 4 * D])
        hid = sb("hid", [P, 2, 4 * P])
        hga = sb("hga", [P, 2, 4 * P])
        o_n, ot, qt = hid[:, 0, :], hid[:, 1, :], hga[:, 0, :]
        hh = sb("hh", [P, 2, 4 * P], F16)
        hl = sb("hl", [P, 2, 4 * P], F16)
        lg = sb("lg", [P, NT * E])
        gt = sb("gt", [P, 12, NT * E])
        gs = sb("gs", [P, 12, NT])
        gi = sb("gi", [P, 2, NT], U32)
        ps = ctx.enter_context(nc.psum_tensor("ps", [P, 8, 512], F32))

        ident = cst[:, C_ID:C_ID + P]
        tri = cst[:, C_TRI:C_TRI + P]
        ones = cst[:, C_ONE:C_ONE + P]

        def xtile(t):
            return x_sb[:, bass.ds(t * D, D)] if not isinstance(t, int) else x_sb[:, t * D:(t + 1) * D]

        def cols(tensor, start, n):
            return tensor[:, bass.ds(start, n)] if not isinstance(start, int) else tensor[:, start:start + n]

        def free(eng, s, count):
            if not isinstance(count, int) or count > 0:
                eng.wait_ge(s, count)

        class Attention:

            def __init__(self, n, heads, dh, weights, mask_col, clip, bias):
                self.n, self.H, self.dh, self.weights = n, heads, dh, weights
                self.mask_col, self.clip, self.bias = mask_col, clip, bias
                self.inner = heads * dh
                self.nc = self.inner // P
                self.hpc = P // dh
                self.groups = heads // 4
                self.w = min(4, self.hpc) * CK
                self.per = self.hpc * CK // self.w
                self.banks = self.nc * self.per
                self.hb = self.w // CK
                self.scale = float(dh) ** -0.5
                flat = arena[:, :, :, :].rearrange("p a b c -> p (a b c)").bitcast(F32)
                nk = NB * heads * CK
                nv = NB * heads * (dh + 1)
                self.km = flat[:, 0:nk]
                self.v = flat[0:CK, nk:nk + nv]
                self.pt = flat[0:CK, nk + nv:nk + nv + heads * P]
                self.ctx_t = stage[0:CR, 0, 0:2 * NB * CK].rearrange("p (k n) -> p k n", k=2)
                i = self.inner
                self.wq = aw[:, 0:DC * i].rearrange("p (k n) -> p k n", k=DC)
                self.wk = aw[0:CR, DC * i:DC * i + 2 * i].rearrange("p (k n) -> p k n", k=2)
                self.wv = aw[0:CR, DC * i + 2 * i:DC * i + 4 * i].rearrange("p (k n) -> p k n", k=2)
                self.wo = aw[:, DC * i + 4 * i:DC * i + 4 * i + self.nc * D].rearrange("p (k n) -> p k n", k=self.nc)

            def s(self, name):
                return sem(f"att{self.n}_{name}")

        att = [
            Attention(0, 16, 16, (wq0, wk0, wv0, wo0), C_HM0, True, True),
            Attention(1, 8, 64, (wq1, wk1, wv1, wo1), C_HM1, False, False),
        ]
        for a in att:
            for name in ("w", "k", "km", "v", "vs", "ones", "xn", "xt", "xts", "q", "qs", "sc", "clip", "max", "sub",
                         "p", "pt", "pts", "pv", "rec", "on", "ot", "ots", "pr", "pb", "x"):
                a.s(name)
        for n in range(4):
            for name in ("st", "mv", "ve", "sq", "rs"):
                sem(f"ln{n}_{name}")

        def ln_stats_vector(eng, n, wait_x):
            wait_x()
            for t in range(NT):
                eng.bn_stats(st6[:, t, :], xtile(t)).then_inc(sem(f"ln{n}_st"), 1)
            for t in range(NT):
                eng.wait_ge(sem(f"ln{n}_st"), t + 1)
                eng.bn_aggr(mv[:, 2 * t:2 * t + 2], st6[:, t, :]).then_inc(sem(f"ln{n}_mv"), 1)
            eng.wait_ge(sem(f"ln{n}_mv"), NT)
            eng.tensor_scalar(rstd[:, :], mv[:, 1:2 * NT:2], EPS, None, ALU.add).then_inc(sem(f"ln{n}_ve"), 1)
            eng.wait_ge(sem(f"ln{n}_sq"), 1)
            eng.reciprocal(rstd[:, :], rstd[:, :]).then_inc(sem(f"ln{n}_rs"), 1)
            eng.wait_ge(sem(f"ln{n}_rs"), 1)

        def ln_stats_scalar(eng, n):
            eng.wait_ge(sem(f"ln{n}_ve"), 1)
            eng.activation(rstd[:, :], rstd[:, :], ACT.Sqrt).then_inc(sem(f"ln{n}_sq"), 1)

        def normalize(eng, dst, t):
            return eng.tensor_scalar(dst, xtile(t), cols(mv, t * 2, 1), cols(rstd, t, 1), ALU.subtract, ALU.mult)

        def att_loads(eng, a):
            for dst, src in zip((a.wq, a.wk, a.wv, a.wo), a.weights):
                eng.dma_start(dst, src).then_inc(a.s("w"), 16)
            eng.dma_start(a.ctx_t, ctx_t).then_inc(a.s("w"), 16)

        def att_kv_tensor(eng, a):
            half = NB * CK // 2
            eng.wait_ge(a.s("w"), 80)
            for c in range(a.nc):
                if c:
                    eng.wait_ge(a.s("km"), c * a.hpc)
                for h in range(2):
                    for k in range(2):
                        mm = eng.matmul(ps[:, h, 0:half], a.wk[:, k, c * P:(c + 1) * P],
                                        a.ctx_t[:, k, h * half:(h + 1) * half], start=(k == 0), stop=(k == 1))
                mm.then_inc(a.s("k"), 1)
            for b in range(NB):
                if b >= 2:
                    eng.wait_ge(a.s("vs"), b - 1)
                for k in range(2):
                    mm = eng.matmul(ps[0:CK, 2 + b % 2, 0:a.inner], a.ctx_t[:, k, b * CK:(b + 1) * CK],
                                    a.wv[:, k, :], start=(k == 0), stop=(k == 1))
                mm.then_inc(a.s("v"), 1)

        def att_kv_vector(eng, a):
            km = a.km.rearrange("p (b h n) -> p b h n", b=NB, h=a.H)
            for c in range(a.nc):
                eng.wait_ge(a.s("k"), c + 1)
                for j in range(a.hpc):
                    for h in range(2):
                        dst = km[:, h * NB // 2:(h + 1) * NB // 2, c * a.hpc + j, :]
                        src = ps[:, h, 0:NB * CK // 2].rearrange("p (b n) -> p b n", n=CK)
                        m = cst[:, a.mask_col + j:a.mask_col + j + 1]
                        if a.bias:
                            ins = eng.tensor_scalar(dst, src, vec[:, V_BK + c:V_BK + c + 1], m, ALU.add, ALU.mult)
                        else:
                            ins = eng.tensor_scalar(dst, src, m, None, ALU.mult)
                    ins.then_inc(a.s("km"), 1)
            for b in range(NB):
                eng.wait_ge(a.s("v"), b + 1)
                dst = a.v.rearrange("p (b h n) -> p b h n", b=NB, h=a.H)[:, b, :, 0:a.dh]
                src = ps[0:CK, 2 + b % 2, 0:a.inner].rearrange("p (h n) -> p h n", n=a.dh)
                if a.bias:
                    bv = vec[0:CK, V_BV:V_BV + a.inner].rearrange("p (h n) -> p h n", n=a.dh)
                    eng.tensor_tensor(dst, src, bv, ALU.add).then_inc(a.s("vs"), 1)
                else:
                    eng.tensor_copy(dst, src).then_inc(a.s("vs"), 1)

        def pipelined(eng, front, back):
            def batch(i):
                front(i, 1)
                back(i, 0)
                front(i + 1, 0)
                back(i, 1)

            front(0, 0)
            batch(0)
            with eng.Fori(1, NB - 1) as i:
                batch(i)
            front(NB - 1, 1)
            back(NB - 1, 0)
            back(NB - 1, 1)

        def per_batch(eng, body):
            body(0)
            with eng.Fori(1, NB) as i:
                body(i)

        def att_tensor(eng, a):
            def front(i, u):
                t = i * 2 + u
                eng.wait_ge(a.s("xn"), t + 1)
                for c in range(DC):
                    mm = eng.transpose(ps[:, 4, c * P:(c + 1) * P], xn[:, 0, c * P:(c + 1) * P], ident)
                mm.then_inc(a.s("xt"), 1)
                eng.wait_ge(a.s("xts"), t + 1)
                free(eng, a.s("pb"), t - 1)
                for c in range(a.nc):
                    for k in range(DC):
                        mm = eng.matmul(ps[:, 5, c * P:(c + 1) * P], a.wq[:, k, c * P:(c + 1) * P],
                                        xnt[:, 0, k * P:(k + 1) * P], start=(k == 0), stop=(k == DC - 1))
                mm.then_inc(a.s("q"), 1)
                eng.wait_ge(a.s("qs"), (t + 1) * a.nc)
                free(eng, a.s("clip"), t)
                for c in range(a.nc):
                    for h in range(a.per):
                        mm = eng.matmul(ps[:, c * a.per + h, 0:a.w], qt[:, c * P:(c + 1) * P],
                                        cols(a.km, i * (a.H * CK) + (c * a.per + h) * a.w, a.w),
                                        start=True, stop=True)
                mm.then_inc(a.s("sc"), 1)

            def back(i, u):
                t = i * 2 + u
                eng.wait_ge(a.s("p"), t + 1)
                for g in range(a.groups):
                    if g >= 2:
                        eng.wait_ge(a.s("pts"), t * a.groups + g - 1)
                    else:
                        free(eng, a.s("pts"), t * a.groups)
                    for j in range(4):
                        h = 4 * g + j
                        mm = eng.transpose(ps[0:CK, 6 + g % 2, j * P:(j + 1) * P], p_exp[:, h * CK:(h + 1) * CK], ident)
                    mm.then_inc(a.s("pt"), 1)
                nv = a.dh + 1
                free(eng, a.s("pb"), t)
                for g in range(a.groups):
                    eng.wait_ge(a.s("pts"), t * a.groups + g + 1)
                    for j in range(4):
                        h = 4 * g + j
                        hb = 4 if a.n else 16
                        mm = eng.matmul(ps[:, 4 + h // hb, (h % hb) * nv:(h % hb + 1) * nv], a.pt[:, h * P:(h + 1) * P],
                                        cols(a.v, i * (a.H * nv) + h * nv, nv), start=True, stop=True)
                mm.then_inc(a.s("pv"), 1)
                eng.wait_ge(a.s("on"), t + 1)
                for c in range(a.nc):
                    mm = eng.transpose(ps[:, 4, c * P:(c + 1) * P], o_n[:, c * P:(c + 1) * P], ident)
                mm.then_inc(a.s("ot"), 1)
                eng.wait_ge(a.s("ots"), t + 1)
                for c in range(a.nc):
                    mm = eng.matmul(ps[:, 5, 0:D], ot[:, c * P:(c + 1) * P], a.wo[:, c, :],
                                    start=(c == 0), stop=(c == a.nc - 1))
                mm.then_inc(a.s("pr"), 1)

            eng.wait_ge(a.s("km"), a.H)
            eng.wait_ge(a.s("vs"), NB)
            eng.wait_ge(a.s("ones"), 1)
            pipelined(eng, front, back)

        def att_vector(eng, a):
            H = a.H
            s3 = s_exp[:, 0:H * CK].rearrange("p (h n) -> p h n", n=CK)

            def front(i, u):
                t = i * 2 + u
                free(eng, a.s("xt"), t)
                normalize(eng, xn[:, 0, :], t).then_inc(a.s("xn"), 1)
                eng.wait_ge(a.s("sc"), t + 1)
                free(eng, a.s("p"), t)
                s4 = ps[:, 0:a.banks, 0:a.w]
                sx = s_exp[:, 0:H * CK].rearrange("p (k n) -> p k n", k=a.banks)
                lim = CLAMP / a.scale
                if a.clip:
                    eng.tensor_scalar(sx, s4, lim, -lim, ALU.min, ALU.max).then_inc(a.s("clip"), 1)
                    eng.wait_ge(a.s("clip"), t + 1)
                    eng.reduce_max(red[:, 0:H], s3, AX).then_inc(a.s("max"), 1)
                    eng.wait_ge(a.s("max"), t + 1)
                    eng.tensor_tensor(s3, s3, red[:, 0:H].unsqueeze(2).to_broadcast([P, H, CK]),
                                      ALU.subtract).then_inc(a.s("sub"), 1)
                else:
                    s4 = ps[:, 0:a.banks, 0:a.w].rearrange("p k (h n) -> p k h n", n=CK)
                    sx = s_exp[:, 0:H * CK].rearrange("p (k h n) -> p k h n", k=a.banks, n=CK)
                    r4 = red[:, 0:H].rearrange("p (k h) -> p k h", k=a.banks)
                    eng.reduce_max(r4, s4, AX).then_inc(a.s("max"), 1)
                    eng.wait_ge(a.s("max"), t + 1)
                    for k in range(a.banks):
                        ins = eng.tensor_tensor(sx[:, k], s4[:, k], r4[:, k].unsqueeze(2).to_broadcast([P, a.hb, CK]),
                                                ALU.subtract)
                    ins.then_inc(a.s("clip"), 1)

            def back(i, u):
                t = i * 2 + u
                nv = a.dh + 1
                eng.wait_ge(a.s("pv"), t + 1)
                hb = 4 if a.n else 16
                nb = H // hb
                for k in range(nb):
                    pv = ps[:, 4 + k, 0:hb * nv].rearrange("p (h n) -> p h n", n=nv)
                    ins = eng.reciprocal(rec[:, k * hb:(k + 1) * hb], pv[:, :, a.dh])
                ins.then_inc(a.s("rec"), 1)
                eng.wait_ge(a.s("rec"), t + 1)
                for k in range(nb):
                    pv = ps[:, 4 + k, 0:hb * nv].rearrange("p (h n) -> p h n", n=nv)
                    dst = o_n[:, k * hb * a.dh:(k + 1) * hb * a.dh].rearrange("p (h n) -> p h n", n=a.dh)
                    ins = eng.tensor_tensor(dst, pv[:, :, 0:a.dh],
                                            rec[:, k * hb:(k + 1) * hb].unsqueeze(2).to_broadcast([P, hb, a.dh]), ALU.mult)
                ins.then_inc(a.s("on"), 1)
                eng.wait_ge(a.s("pr"), t + 1)
                vb = V_BO1 if a.n else V_BO0
                eng.tensor_tensor(xn[:, 1, :], ps[:, 5, 0:D], vec[:, vb:vb + D], ALU.add).then_inc(a.s("pb"), 1)
                eng.wait_ge(a.s("pb"), t + 1)
                eng.tensor_tensor(xtile(t), xtile(t), xn[:, 1, :], ALU.add).then_inc(a.s("x"), 1)

            pipelined(eng, front, back)
            eng.wait_ge(a.s("x"), NT)

        def att_scalar(eng, a):
            def evacuate(i, u):
                t = i * 2 + u
                eng.wait_ge(a.s("xt"), t + 1)
                free(eng, a.s("q"), t)
                eng.activation(xnt[:, 0, :], ps[:, 4, 0:D], ACT.Copy).then_inc(a.s("xts"), 1)
                eng.wait_ge(a.s("q"), t + 1)
                free(eng, a.s("sc"), t)
                for c in range(a.nc):
                    if a.bias:
                        eng.activation(qt[:, c * P:(c + 1) * P], ps[:, 5, c * P:(c + 1) * P], ACT.Identity,
                                       bias=vec[:, V_BQ + c:V_BQ + c + 1]).then_inc(a.s("qs"), 1)
                if not a.bias:
                    eng.activation(qt[:, 0:a.inner], ps[:, 5, 0:a.inner], ACT.Copy).then_inc(a.s("qs"), a.nc)

            def exponential(i, u):
                t = i * 2 + u
                eng.wait_ge(a.s("sub" if a.clip else "clip"), t + 1)
                free(eng, a.s("pt"), t * a.groups)
                eng.activation(p_exp[:, 0:a.H * CK], s_exp[:, 0:a.H * CK], ACT.Exp, scale=a.scale).then_inc(a.s("p"), 1)

            def turned(i, u):
                t = i * 2 + u
                for g in range(a.groups):
                    eng.wait_ge(a.s("pt"), t * a.groups + g + 1)
                    free(eng, a.s("pv"), t)
                    eng.activation(a.pt[:, g * 4 * P:(g + 1) * 4 * P], ps[0:CK, 6 + g % 2, :], ACT.Copy)\
                       .then_inc(a.s("pts"), 1)

            def output(i, u):
                t = i * 2 + u
                eng.wait_ge(a.s("ot"), t + 1)
                free(eng, a.s("pr"), t)
                eng.activation(ot[:, 0:a.inner], ps[:, 4, 0:a.inner], ACT.Copy).then_inc(a.s("ots"), 1)

            def step(i, u, j, v):
                evacuate(j, v)
                turned(i, u)
                exponential(j, v)
                output(i, u)

            evacuate(0, 0)
            exponential(0, 0)
            step(0, 0, 0, 1)
            step(0, 1, 1, 0)
            with eng.Fori(1, NB - 1) as i:
                step(i, 0, i, 1)
                step(i, 1, i + 1, 0)
            step(NB - 1, 0, NB - 1, 1)
            turned(NB - 1, 1)
            output(NB - 1, 1)

        for n in range(2):
            for name in ("xn", "t", "xf", "l", "lb", "sc"):
                sem(f"rt{n}_{name}")

        def route_vector(eng, n):
            for t in range(NT):
                normalize(eng, xns[:, t * D:(t + 1) * D], t).then_inc(sem(f"rt{n}_xn"), 1)
            for t in range(NT):
                eng.wait_ge(sem(f"rt{n}_l"), t + 1)
                dst, src = lg[:, t * E:(t + 1) * E], ps[:, 6 + t % 2, 0:E]
                if n == 0:
                    ins = eng.tensor_tensor(dst, src, vec[:, V_BR:V_BR + E], ALU.add)
                else:
                    ins = eng.tensor_copy(dst, src)
                ins.then_inc(sem(f"rt{n}_lb"), 1)
            eng.wait_ge(sem(f"rt{n}_lb"), NT)

        def route_tensor(eng, n):
            at = V_WR1 if n else V_WR0
            wr = vec[:, at:at + DC * E].rearrange("p (k e) -> p k e", k=DC)
            eng.wait_ge(att[n].s("x"), NT)

            def turn(t):
                eng.wait_ge(sem(f"rt{n}_xn"), t + 1)
                free(eng, sem(f"rt{n}_xf"), t - 1)
                for c in range(DC):
                    mm = eng.transpose(ps[:, 4 + t % 2, c * P:(c + 1) * P], xns[:, t * D + c * P:t * D + (c + 1) * P],
                                       ident)
                mm.then_inc(sem(f"rt{n}_t"), 1)

            turn(0)
            for t in range(NT):
                if t + 1 < NT:
                    turn(t + 1)
                eng.wait_ge(sem(f"rt{n}_xf"), t + 1)
                free(eng, sem(f"rt{n}_lb"), t - 1)
                for c in range(DC):
                    mm = eng.matmul(ps[:, 6 + t % 2, 0:E], xnt[:, t % 2, c * P:(c + 1) * P], wr[:, c, :],
                                    start=(c == 0), stop=(c == DC - 1))
                mm.then_inc(sem(f"rt{n}_l"), 1)

        def route_scalar(eng, n):
            for t in range(NT):
                eng.wait_ge(sem(f"rt{n}_t"), t + 1)
                free(eng, sem(f"rt{n}_l"), t - 1)
                eng.activation(xnt[:, t % 2, :], ps[:, 4 + t % 2, 0:D], ACT.Copy).then_inc(sem(f"rt{n}_xf"), 1)

        def bcast(ap):
            return ap.unsqueeze(2).to_broadcast([P, NT, E])

        def over_t(ap):
            return ap.unsqueeze(1).to_broadcast([P, NT, E])

        def g3(k):
            return gt[:, k, :].rearrange("p (t e) -> p t e", e=E)

        def c3(at):
            return cst[:, at:at + NT * E].rearrange("p (t e) -> p t e", e=E)

        rev3, row3 = c3(C_REV), c3(C_ROW)
        lg3 = lg[:, :].rearrange("p (t e) -> p t e", e=E)

        class Chain:

            def __init__(self, eng, name):
                self.eng, self.sem, self.n = eng, sem(name), 0

            def __call__(self, ins):
                self.n += 1
                ins.then_inc(self.sem, 1)
                self.eng.wait_ge(self.sem, self.n)

        def first_max(eng, ch, values, top, tmp, one_hot):
            ch(eng.reduce_max(top, values, AX))
            ch(eng.tensor_tensor(tmp, values, bcast(top), ALU.is_equal))
            ch(eng.tensor_tensor(tmp, tmp, rev3, ALU.mult))
            ch(eng.reduce_max(gs[:, 11, :], tmp, AX))
            ch(eng.tensor_tensor(one_hot, tmp, bcast(gs[:, 11, :]), ALU.is_equal))

        def prefix(eng, ch, src, ping, pong, width, block):
            step = block
            while step < width:
                ch(eng.tensor_copy(ping[:, 0:step], src[:, 0:step]))
                ch(eng.tensor_tensor(ping[:, step:width], src[:, step:width], src[:, 0:width - step], ALU.add))
                src, ping, pong = ping, pong, ping
                step *= 2
            return src

        sem("rank"), sem("route0"), sem("oh0")

        def gate0_vector(eng):
            ch = Chain(eng, "gate0")
            first_max(eng, ch, lg3, gs[:, 0, :], g3(0), g3(1))
            eng.sem_inc(sem("oh0"), 1)
            eng.wait_ge(sem("rank"), 1)
            ch(eng.tensor_copy(gt[:, 2, :], ps[:, 1, 0:NT * E]))
            upto = prefix(eng, ch, gt[:, 2, :], gt[:, 3, :], gt[:, 4, :], NT * E, E)
            count = upto[:, (NT - 1) * E:NT * E]
            tiles = gt[:, 6, 0:E]
            cmp = gt[:, 0, 0:NB * E].rearrange("p (e k) -> p e k", e=E)
            kk = cst[:, C_K:C_K + NB * E].rearrange("p (e k) -> p e k", e=E)
            ch(eng.tensor_tensor(cmp, count.unsqueeze(2).to_broadcast([P, E, NB]), kk, ALU.is_gt))
            ch(eng.reduce_sum(tiles, cmp, AX))
            ends = prefix(eng, ch, tiles, gt[:, 7, 0:E], gt[:, 7, E:2 * E], E, 1)
            base = gt[:, 7, 2 * E:3 * E]
            ch(eng.tensor_tensor(base, ends, tiles, ALU.subtract))
            ch(eng.tensor_scalar(base, base, float(ST), None, ALU.mult))
            ch(eng.tensor_tensor(gt[:, 5, :], ps[:, 0, 0:NT * E], upto, ALU.add))
            ch(eng.tensor_tensor(gt[:, 5, :], gt[:, 5, :], gt[:, 2, :], ALU.subtract))
            ch(eng.tensor_tensor(g3(5), g3(5), over_t(base), ALU.add))
            ch(eng.tensor_tensor(g3(5), g3(5), g3(1), ALU.mult))
            ch(eng.reduce_sum(gs[:, 5, :], g3(5), AX))
            ch(eng.tensor_copy(gi[:, 0, :], gs[:, 5, :]))
            ch(eng.tensor_tensor(g3(0), c3(C_J), over_t(ends), ALU.is_ge))
            ch(eng.reduce_sum(gs[:, 6, :], g3(0), AX))
            ch(eng.tensor_scalar(texp[:, :], gs[:, 6, :], float(E - 1), None, ALU.min))
            eng.sem_inc(sem("route0"), 1)

        def gate0_tensor(eng):
            eng.wait_ge(sem("oh0"), 1)
            eng.matmul(ps[:, 0, 0:NT * E], tri, gt[:, 1, :], start=True, stop=True)
            eng.matmul(ps[:, 1, 0:NT * E], ones, gt[:, 1, :], start=True, stop=True).then_inc(sem("rank"), 1)

        sem("gmax"), sem("gexp"), sem("oh1"), sem("p1"), sem("m1k"), sem("p2"), sem("route1")

        def gate1_vector(eng):
            ch = Chain(eng, "gate1")
            ch(eng.reduce_max(gs[:, 0, :], lg3, AX))
            eng.tensor_tensor(g3(0), lg3, bcast(gs[:, 0, :]), ALU.subtract).then_inc(sem("gmax"), 1)
            eng.wait_ge(sem("gexp"), 1)
            ch(eng.reduce_sum(gs[:, 1, :], g3(1), AX))
            ch(eng.reciprocal(gs[:, 1, :], gs[:, 1, :]))
            ch(eng.tensor_tensor(g3(2), g3(1), bcast(gs[:, 1, :]), ALU.mult))
            first_max(eng, ch, g3(2), gs[:, 2, :], g3(0), g3(3))
            ch(eng.tensor_scalar(gt[:, 1, :], gt[:, 3, :], -1.0, 1.0, ALU.mult, ALU.add))
            ch(eng.tensor_tensor(g3(1), g3(1), g3(2), ALU.mult))
            first_max(eng, ch, g3(1), gs[:, 3, :], g3(0), g3(4))
            eng.sem_inc(sem("oh1"), 1)

            def kept(bank, m, dst):
                for par in range(2):
                    src = ps[:, bank + par, 0:NB * E].rearrange("p (g e) -> p g e", e=E)
                    ch(eng.tensor_copy(gt[:, dst, :].rearrange("p (g u e) -> p g u e", u=2, e=E)[:, :, par, :], src))
                ch(eng.tensor_scalar(gt[:, 0, :], gt[:, dst, :], float(CAP), None, ALU.is_lt))
                ch(eng.tensor_tensor(gt[:, m, :], gt[:, m, :], gt[:, 0, :], ALU.mult))

            eng.wait_ge(sem("p1"), 1)
            kept(0, 3, 5)
            eng.sem_inc(sem("m1k"), 1)
            eng.wait_ge(sem("p2"), 1)
            kept(2, 4, 6)
            for c, (m, pos) in enumerate(((3, 5), (4, 6))):
                ch(eng.tensor_tensor(g3(0), g3(pos), row3, ALU.add))
                ch(eng.tensor_tensor(g3(0), g3(0), g3(m), ALU.mult))
                ch(eng.reduce_sum(gs[:, 5, :], g3(0), AX))
                ch(eng.reduce_sum(gs[:, 4, :], g3(m), AX))
                ch(eng.tensor_scalar(gs[:, 6, :], gs[:, 4, :], -1.0, 1.0, ALU.mult, ALU.add))
                ch(eng.tensor_scalar(gs[:, 7, :], cst[:, C_TOK:C_TOK + NT], float(E * SL + c * NT * P), None, ALU.add))
                ch(eng.tensor_tensor(gs[:, 7, :], gs[:, 7, :], gs[:, 6, :], ALU.mult))
                ch(eng.tensor_tensor(gs[:, 7, :], gs[:, 7, :], gs[:, 5, :], ALU.add))
                ch(eng.tensor_copy(si[:, c, :], gs[:, 7, :]))
                ch(eng.tensor_copy(gi[:, c, :], gs[:, 5, :]))
                ch(eng.tensor_tensor(gs[:, 2 + c, :], gs[:, 2 + c, :], gs[:, 4, :], ALU.mult))
            eng.sem_inc(sem("route1"), 1)

        def gate1_tensor(eng):
            def view(k, par):
                return gt[:, k, :].rearrange("p (g u e) -> p g u e", u=2, e=E)[:, :, par, :]

            def o(b):
                return ps[:, b, 0:NB * E].rearrange("p (g e) -> p g e", e=E)

            eng.wait_ge(sem("oh1"), 1)
            eng.matmul(o(0), tri, view(3, 0), start=True, stop=True)
            eng.matmul(o(1), ones, view(3, 0), start=True, stop=False)
            eng.matmul(o(1), tri, view(3, 1), start=False, stop=True).then_inc(sem("p1"), 1)
            eng.wait_ge(sem("m1k"), 1)
            eng.matmul(o(2), ones, view(3, 0), start=True, stop=False)
            eng.matmul(o(2), ones, view(3, 1), start=False, stop=False)
            eng.matmul(o(2), tri, view(4, 0), start=False, stop=True)
            eng.matmul(o(3), ones, view(3, 0), start=True, stop=False)
            eng.matmul(o(3), ones, view(3, 1), start=False, stop=False)
            eng.matmul(o(3), ones, view(4, 0), start=False, stop=False)
            eng.matmul(o(3), tri, view(4, 1), start=False, stop=True).then_inc(sem("p2"), 1)

        def gate1_scalar(eng):
            eng.wait_ge(sem("gmax"), 1)
            eng.activation(gt[:, 1, :], gt[:, 0, :], ACT.Exp).then_inc(sem("gexp"), 1)

        sem("zeros"), sem("zfill"), sem("scat0"), sem("scat1")
        for r in range(4):
            sem(f"back0_{r}"), sem(f"back1_{r}"), sem(f"back2_{r}")
        sem("add1"), sem("add2"), sem("add0")

        def scatter_pool(eng, n):
            eng.wait_ge(sem("zfill"), 32)
            eng.wait_ge(sem(f"route{n}"), 1)
            for t in range(NT):
                for c in range(n + 1):
                    idx = si[:, c, t:t + 1] if n else gi[:, c, t:t + 1]
                    eng.indirect_dma_start(out=(slots0, slots1)[n], out_offset=bass.IndirectOffsetOnAxis(ap=idx, axis=0),
                                           in_=xns[:, t * D:(t + 1) * D], in_offset=None).then_inc(sem(f"scat{n}"), 16)

        def gather_pool(eng, which, rows, index, buf):
            for t in range(NT):
                eng.indirect_dma_start(out=buf[:, t * D:(t + 1) * D], out_offset=None, in_=rows,
                                       in_offset=bass.IndirectOffsetOnAxis(ap=index[:, t:t + 1], axis=0))\
                   .then_inc(sem(f"back{which}_{t // 4}"), 16)

        for n in range(2):
            for name in ("wh", "wl", "tr", "xhi", "xlo", "h", "b", "g", "m", "hi", "lo", "y", "yx", "out"):
                sem(f"f{n}_{name}")
        for p in range(2):
            sem(f"f0_dw{p}"), sem(f"f0_db{p}"), sem(f"f0_dx{p}"), sem(f"f1_st{p}")
        sem("f1_tail"), sem("f1_dx")

        def flat_w(par, part):
            return arena[:, par, part, :]

        def three(eng, out_ap, a, b, first, last, shared=False):
            eng.matmul(out_ap, a[0], b[0], start=first, stop=False, skip_group_check=shared)
            eng.matmul(out_ap, a[0], b[1], start=False, stop=False, skip_group_check=shared)
            return eng.matmul(out_ap, a[1], b[0], start=False, stop=last, skip_group_check=shared)

        def steps(eng, n, units, pairs, single, step):
            step(0, 0)
            last = pairs - 1
            with eng.Fori(0, last) as i:
                for k in range(1, 2 * units + 1):
                    step(i, k)
            for k in range(1, (3 if single else 2) * units):
                step(last, k)
            return last

        U0 = FC0 // 2
        DW = DC * F0
        fl32 = arena[:, :, :, :].rearrange("p a b c -> p (a b c)")
        wsp0 = [[fl32[:, (2 * p + s) * 2 * DW:(2 * p + s + 1) * 2 * DW] for s in range(2)] for p in range(2)]
        st0 = [fl32[:, 8 * DW + p * 4 * DW:8 * DW + (p + 1) * 4 * DW].bitcast(F32) for p in range(2)]

        def ffn0_loads(eng):
            def weights(j, par):
                e = eng.value_load(texp[0:1, bass.ds(j, 1)] if not isinstance(j, int) else texp[0:1, j:j + 1],
                                   min_val=0, max_val=E - 1)
                for src, at, width in ((f0w1, 0, F0), (f0w2, DW, D)):
                    eng.dma_start(st0[par][:, at:at + DW].rearrange("p (k n) -> p k n", n=width),
                                  src[bass.ds(e, 1)].rearrange("e (k p) n -> p (e k) n", p=P))\
                       .then_inc(sem(f"f0_dw{par}"), 16)
                return e

            def biases(e, par):
                eng.dma_start(b1t[:, par, :], b1c[bass.ds(e, 1)].rearrange("e p f -> p (e f)")).then_inc(sem(f"f0_db{par}"), 16)
                eng.dma_start(b2t[:, par, :], b2w[bass.ds(e, 1)].rearrange("e p n -> p (e n)")).then_inc(sem(f"f0_db{par}"), 16)

            def tokens(j, par):
                src = slots0.rearrange("(j s p) n -> j p s n", j=SLT, p=P)
                src = src[j:j + 1] if isinstance(j, int) else src[bass.ds(j, 1)]
                eng.dma_start(xs[:, par, :].rearrange("p (s n) -> p s n", s=2), src.rearrange("j p s n -> p (j s) n"))\
                   .then_inc(sem(f"f0_dx{par}"), 16)

            def store(j, par):
                eng.wait_ge(sem("f0_yx"), j + 3)
                dst = y0.rearrange("(j s p) n -> j p s n", j=SLT, p=P)
                dst = dst[j:j + 1] if isinstance(j, int) else dst[bass.ds(j, 1)]
                eng.dma_start(dst.rearrange("j p s n -> p (j s) n"), y_sb[:, par * 2 * D:(par + 1) * 2 * D]
                              .rearrange("p (s n) -> p s n", s=2)).then_inc(sem("f0_out"), 16)

            def tile(j, par):
                eng.wait_ge(sem("f0_wl"), j * U0 + U0)
                e = weights(j + 2, par)
                eng.wait_ge(sem("f0_tr"), j + 1)
                tokens(j + 2, par)
                store(j, par)
                biases(e, par)

            eng.wait_ge(sem("route0"), 1)
            e0 = weights(0, 0)
            e1 = weights(1, 1)
            biases(e0, 0)
            biases(e1, 1)
            eng.wait_ge(sem("scat0"), 16 * NT)
            tokens(0, 0)
            tokens(1, 1)
            with eng.Fori(0, (SLT - 3) // 2) as i:
                tile(i * 2, 0)
                tile(i * 2 + 1, 1)
            tile(SLT - 3, 0)
            store(SLT - 2, 1)
            store(SLT - 1, 0)

        def half(k):
            return k // U0 % 2, k % U0

        def more(i, k):
            return not (isinstance(i, int) and i == SLT // 2 - 1 and k >= 2 * U0)

        def ffn0_tensor(eng):
            def turn(j, landed, par):
                eng.wait_ge(sem(f"f0_dx{par}"), landed)
                free(eng, sem("f0_xlo"), j)
                for s in range(2):
                    for c in range(DC):
                        mm = eng.transpose(ps[:, 2, c * ST + s * P:c * ST + (s + 1) * P],
                                           xs[:, par, s * D + c * P:s * D + (c + 1) * P], ident)
                mm.then_inc(sem("f0_tr"), 1)

            def hidden(i, k):
                par, r = half(k)
                u, j = i * (2 * U0) + k, i * 2 + k // U0
                if r == 0:
                    eng.wait_ge(sem("f0_wl"), j * U0 + U0 // 2)
                    eng.wait_ge(sem("f0_xlo"), j + 1)
                free(eng, sem("f0_g"), u)
                w = [wsp0[par][s][:, 0:DW].rearrange("p (c n) -> p c n", c=DC) for s in range(2)]
                for q in range(2):
                    f = 2 * r + q
                    for c in range(DC):
                        mm = three(eng, ps[:, k % 2, q * ST:(q + 1) * ST], [w[s][:, c, f * P:(f + 1) * P] for s in range(2)],
                                   [xt[:, par, s, c * ST:(c + 1) * ST] for s in range(2)], c == 0, c == DC - 1)
                mm.then_inc(sem("f0_h"), 1)

            def output(i, k):
                par, r = half(k)
                u, j = i * (2 * U0) + k, i * 2 + k // U0
                eng.wait_ge(sem("f0_lo"), u + 2)
                if r == 0:
                    eng.wait_ge(sem("f0_wl"), j * U0 + U0)
                    eng.wait_ge(sem("f0_yx"), j + 1)
                for s in range(2):
                    for q in range(2):
                        f = 2 * r + q
                        mm = three(eng, ps[:, 4 + 2 * par + s, 0:D],
                                   [(hh, hl)[h][:, k % 2, q * ST + s * P:q * ST + (s + 1) * P] for h in range(2)],
                                   [wsp0[par][h][:, DW + f * D:DW + (f + 1) * D] for h in range(2)],
                                   f == 0, f == FC0 - 1)
                mm.then_inc(sem("f0_y"), 1)

            def step(i, k):
                hidden(i, k)
                if k:
                    output(i, k - 1)
                par, r = half(k)
                if r == 1 and more(i, k):
                    turn(i * 2 + k // U0 + 1, i * 16 + 16 * ((k // U0 + 1) // 2 + 1), 1 - par)

            eng.sem_inc(sem("f0_y"), 1)
            turn(0, 16, 0)
            last = steps(eng, 0, U0, SLT // 2, True, step)
            output(last, 3 * U0 - 1)

        def ffn0_slices(r):
            return r * (2 * DW // U0), (r + 1) * (2 * DW // U0)

        def ffn0_scalar(eng):
            def weights_hi(par, r):
                a, b = ffn0_slices(r)
                eng.activation(wsp0[par][0][:, a:b], st0[par][:, a:b], ACT.Copy, scale=WS).then_inc(sem("f0_wh"), 1)

            def tokens_hi(j, par):
                eng.wait_ge(sem("f0_tr"), j + 1)
                eng.activation(xt[:, par, 0, 0:DC * ST], ps[:, 2, :], ACT.Copy, scale=XS).then_inc(sem("f0_xhi"), 1)

            def step(i, k):
                par, r = half(k)
                u, j = i * (2 * U0) + k, i * 2 + k // U0
                eng.wait_ge(sem("f0_h"), u + 1)
                free(eng, sem("f0_lo"), u)
                if r == 0:
                    eng.wait_ge(sem(f"f0_db{par}"), i * 32 + 32 * (k // U0 // 2 + 1))
                for q in range(2):
                    ins = eng.activation(hid[:, k % 2, q * ST:(q + 1) * ST], ps[:, k % 2, q * ST:(q + 1) * ST], ACT.Gelu,
                                         bias=b1t[:, par, 2 * r + q:2 * r + q + 1], scale=1.0 / (WS * XS))
                ins.then_inc(sem("f0_g"), 1)
                eng.wait_ge(sem("f0_g"), u + 2)
                free(eng, sem("f0_y"), u)
                eng.activation(hh[:, k % 2, :], hid[:, k % 2, :], ACT.Copy, scale=HS0).then_inc(sem("f0_hi"), 1)
                if not more(i, k):
                    return
                if r == 0:
                    eng.wait_ge(sem(f"f0_dw{1 - par}"), i * 32 + 32 * ((k // U0 + 1) // 2 + 1))
                    free(eng, sem("f0_y"), j * U0 + 1 if not isinstance(j, int) or j else 0)
                weights_hi(1 - par, r)
                if r == 1:
                    tokens_hi(j + 1, 1 - par)

            eng.wait_ge(sem("f0_dw0"), 32)
            for r in range(U0):
                weights_hi(0, r)
            tokens_hi(0, 0)
            eng.sem_inc(sem("f0_g"), 1)
            steps(eng, 0, U0, SLT // 2, True, step)

        def ffn0_vector(eng):
            def weights_lo(par, r, count):
                a, b = ffn0_slices(r)
                eng.wait_ge(sem("f0_wh"), count)
                eng.scalar_tensor_tensor(out=wsp0[par][1][:, a:b], in0=st0[par][:, a:b], scalar=WS,
                                         in1=wsp0[par][0][:, a:b], op0=ALU.mult, op1=ALU.subtract).then_inc(sem("f0_wl"), 1)

            def tokens_lo(j, par):
                eng.wait_ge(sem("f0_xhi"), j + 1)
                eng.scalar_tensor_tensor(out=xt[:, par, 1, 0:DC * ST], in0=ps[:, 2, :], scalar=XS,
                                         in1=xt[:, par, 0, 0:DC * ST], op0=ALU.mult, op1=ALU.subtract)\
                   .then_inc(sem("f0_xlo"), 1)

            def result(i, k):
                par = (k // U0 - 1) % 2
                u, j = i * (2 * U0) + (k - 1), i * 2 + (k // U0 - 1)
                eng.wait_ge(sem("f0_y"), u + 2)
                eng.wait_ge(sem("f0_out"), (j + 1) * 16)
                eng.wait_ge(sem(f"f0_db{par}"), i * 32 + 32 * ((k // U0 - 1) // 2 + 1))
                for s in range(2):
                    ins = eng.scalar_tensor_tensor(out=y_sb[:, (par * 2 + s) * D:(par * 2 + s + 1) * D],
                                                   in0=ps[:, 4 + 2 * par + s, 0:D], scalar=1.0 / (WS * HS0),
                                                   in1=b2t[:, par, :], op0=ALU.mult, op1=ALU.add)
                ins.then_inc(sem("f0_yx"), 1)

            def step(i, k):
                par, r = half(k)
                u, j = i * (2 * U0) + k, i * 2 + k // U0
                eng.wait_ge(sem("f0_hi"), u + 1)
                eng.scalar_tensor_tensor(out=hl[:, k % 2, :], in0=hid[:, k % 2, :], scalar=HS0, in1=hh[:, k % 2, :],
                                         op0=ALU.mult, op1=ALU.subtract).then_inc(sem("f0_lo"), 1)
                if more(i, k):
                    weights_lo(1 - par, r, j * U0 + (U0 + r + 1))
                    if r == 1:
                        tokens_lo(j + 1, 1 - par)
                if k and r == 0:
                    result(i, k)

            eng.sem_inc(sem("f0_lo"), 1)
            eng.sem_inc(sem("f0_yx"), 2)
            eng.sem_inc(sem("f0_out"), 32)
            for r in range(U0):
                weights_lo(0, r, r + 1)
            tokens_lo(0, 0)
            last = steps(eng, 0, U0, SLT // 2, True, step)
            result(last, 3 * U0)

        def ffn0_add(eng):
            for t in range(NT):
                if t % 4 == 0:
                    eng.wait_ge(sem(f"back0_{t // 4}"), 64)
                eng.tensor_tensor(xtile(t), xtile(t), xns[:, t * D:(t + 1) * D], ALU.add).then_inc(sem("add0"), 1)

        U1 = FC1
        PIECE = [(0, DC * F1), (DC * F1, DC * F1), (2 * DC * F1, FC1 * D)]
        DONE = [4, 8, 11]
        MAIN = (FC1 - 1) * D

        def ffn1_slice(f):
            if f < 8:
                w = DC * F1 // 4
                return f // 4, P, f % 4 * w, (f % 4 + 1) * w
            if f < 10:
                return 2, P, (f - 8) * MAIN // 2, (f - 7) * MAIN // 2
            return 2, FT1, MAIN, MAIN + D

        def ffn1_loads(eng):
            def piece(i, k):
                q, e = k % 3, i * 2 + k // 3
                src = (f1w0, f1w1, f1wo)[q]
                src = src[e:e + 1] if isinstance(e, int) else src[bass.ds(e, 1)]
                if k >= 2:
                    eng.wait_ge(sem("f1_wl"), i * (2 * U1) + ((k - 2) // 3 * U1 + DONE[(k - 2) % 3]))
                elif not isinstance(i, int):
                    eng.wait_ge(sem("f1_wl"), i * (2 * U1) + (DONE[k + 1] - U1))
                if q < 2:
                    eng.dma_start(stage[:, k % 2, 0:DC * F1].rearrange("p (k n) -> p k n", n=F1),
                                  src.rearrange("e (k p) n -> p (e k) n", p=P)).then_inc(sem(f"f1_st{k % 2}"), 16)
                else:
                    eng.dma_start(stage[:, k % 2, 0:MAIN].rearrange("p (k n) -> p k n", n=D),
                                  src[:, 0:F1 - FT1, :].rearrange("e (k p) n -> p (e k) n", p=P))\
                       .then_inc(sem(f"f1_st{k % 2}"), 16)
                    eng.dma_start(stage[0:FT1, k % 2, MAIN:MAIN + D], src[:, F1 - FT1:F1, :].rearrange("e p n -> p (e n)"))\
                       .then_inc(sem("f1_tail"), 16)

            for k in range(6):
                piece(0, k)
            with eng.Fori(1, E // 2) as i:
                for k in range(6):
                    piece(i, k)

        def ffn1_tensor(eng):
            def turn(e, landed):
                eng.wait_ge(sem("f1_dx"), landed)
                free(eng, sem("f1_xlo"), e)
                for c in range(DC):
                    for s in range(4):
                        mm = eng.transpose(ps[:, 6 + c, s * P:(s + 1) * P], xs4[:, s * D + c * P:s * D + (c + 1) * P], ident)
                mm.then_inc(sem("f1_tr"), 1)

            def hidden(i, k):
                par, f = k // U1 % 2, k % U1
                m = FT1 if f == FC1 - 1 else P
                u, e = i * (2 * U1) + k, i * 2 + k // U1
                free(eng, sem("f1_m"), u)
                for which in range(2):
                    if f == 0:
                        eng.wait_ge(sem("f1_wl"), e * U1 + DONE[which])
                        if which == 0:
                            eng.wait_ge(sem("f1_xlo"), e + 1)
                    w = [flat_w(par, s)[:, which * DC * F1:(which + 1) * DC * F1].rearrange("p (c n) -> p c n", c=DC)
                         for s in range(2)]
                    for c in range(DC):
                        mm = three(eng, ps[0:m, 2 * which + k % 2, :], [w[s][:, c, f * P:f * P + m] for s in range(2)],
                                   [xt[:, par, s, c * SL:(c + 1) * SL] for s in range(2)], c == 0, c == DC - 1)
                    mm.then_inc(sem("f1_b" if which else "f1_h"), 1)

            def output(i, k):
                par, f = k // U1 % 2, k % U1
                m = FT1 if f == FC1 - 1 else P
                u, e = i * (2 * U1) + k, i * 2 + k // U1
                eng.wait_ge(sem("f1_lo"), u + 2)
                if f == 0:
                    eng.wait_ge(sem("f1_wl"), e * U1 + U1)
                    eng.wait_ge(sem("f1_yx"), e + 1)
                at = 2 * DC * F1 + f * D
                for j in range(4):
                    mm = three(eng, ps[:, 4 + j // 2, j % 2 * D:(j % 2 + 1) * D],
                               [(hh, hl)[s][0:m, k % 2, j * P:(j + 1) * P] for s in range(2)],
                               [flat_w(par, s)[0:m, at:at + D] for s in range(2)],
                               f == 0 and j % 2 == 0, f == FC1 - 1, shared=True)
                mm.then_inc(sem("f1_y"), 1)

            def step(i, k):
                hidden(i, k)
                if k:
                    output(i, k - 1)
                if k % U1 == 6 and not (isinstance(i, int) and i == E // 2 - 1 and k > U1):
                    turn(i * 2 + k // U1 + 1, i * 32 + 16 * (k // U1 + 2))

            eng.sem_inc(sem("f1_y"), 1)
            turn(0, 16)
            last = steps(eng, 1, U1, E // 2, False, step)
            output(last, 2 * U1 - 1)

        def ffn1_scalar(eng):
            def weights_hi(par, f, stbuf):
                q, rows, a, b = ffn1_slice(f)
                at = PIECE[q][0]
                eng.activation(flat_w(par, 0)[0:rows, at + a:at + b], stage[0:rows, stbuf, a:b], ACT.Copy, scale=WS)\
                   .then_inc(sem("f1_wh"), 1)

            def tokens(e):
                src = slots1[0:E * SL, :].rearrange("(e s p) n -> e p s n", e=E, p=P)
                src = src[e:e + 1] if isinstance(e, int) else src[bass.ds(e, 1)]
                eng.dma_start(xs4[:, :].rearrange("p (s n) -> p s n", s=4), src.rearrange("e p s n -> p (e s) n"))\
                   .then_inc(sem("f1_dx"), 16)

            def tokens_hi(e, par):
                eng.wait_ge(sem("f1_tr"), e + 1)
                eng.activation(xt[:, par, 0, :].rearrange("p (c n) -> p c n", c=DC), ps[:, 6:8, :], ACT.Copy)\
                   .then_inc(sem("f1_xhi"), 1)

            def result(i, k):
                e = i * 2 + (k // U1 - 1)
                eng.wait_ge(sem("f1_y"), i * (2 * U1) + (k + 1))
                eng.wait_ge(sem("f1_out"), e * 16 + 16)
                eng.activation(y_sb[:, :].rearrange("p (j n) -> p j n", j=2), ps[:, 4:6, :], ACT.Copy,
                               scale=1.0 / (WS * HS1)).then_inc(sem("f1_yx"), 1)
                eng.wait_ge(sem("f1_yx"), e + 2)
                dst = y1.rearrange("(e j p) n -> e p j n", e=E, p=P)
                dst = dst[e:e + 1] if isinstance(e, int) else dst[bass.ds(e, 1)]
                eng.dma_start(dst.rearrange("e p j n -> p (e j) n"), y_sb[:, :].rearrange("p (j n) -> p j n", n=D))\
                   .then_inc(sem("f1_out"), 16)

            def step(i, k):
                par, f = k // U1 % 2, k % U1
                m = FT1 if f == FC1 - 1 else P
                u, e = i * (2 * U1) + k, i * 2 + k // U1
                follows = not (isinstance(i, int) and i == E // 2 - 1 and k >= U1)
                eng.wait_ge(sem("f1_h"), u + 1)
                free(eng, sem("f1_m"), u)
                eng.activation(hga[0:m, k % 2, :], ps[0:m, k % 2, :], ACT.Gelu_apprx_tanh,
                               scale=1.0 / WS).then_inc(sem("f1_g"), 1)
                if follows:
                    q = ffn1_slice(f)[0]
                    piece = 3 * (k // U1 + 1) + q
                    if f in (0, 4, 8):
                        eng.wait_ge(sem(f"f1_st{piece % 2}"), i * 48 + 16 * (piece // 2 + 1))
                    if f == 10:
                        eng.wait_ge(sem("f1_tail"), i * 32 + 16 * (k // U1 + 2))
                    if f == 0:
                        free(eng, sem("f1_y"), e * U1 + 1 if not isinstance(e, int) or e else 0)
                        eng.wait_ge(sem("f1_tr"), e + 1)
                        tokens(e + 1)
                    weights_hi(1 - par, f, piece % 2)
                    if f == 7:
                        tokens_hi(e + 1, 1 - par)
                eng.wait_ge(sem("f1_m"), u + 2)
                free(eng, sem("f1_y"), u)
                eng.activation(hh[0:m, k % 2, :], hid[0:m, k % 2, :], ACT.Copy).then_inc(sem("f1_hi"), 1)
                if k and f == 0:
                    result(i, k)

            eng.sem_inc(sem("f1_yx"), 1)
            eng.sem_inc(sem("f1_out"), 16)
            for f in range(U1):
                q = ffn1_slice(f)[0]
                if f in (0, 4, 8):
                    eng.wait_ge(sem(f"f1_st{q % 2}"), 16 * (q // 2 + 1))
                if f == 10:
                    eng.wait_ge(sem("f1_tail"), 16)
                weights_hi(0, f, q % 2)
            eng.wait_ge(sem("scat1"), 32 * NT)
            tokens(0)
            tokens_hi(0, 0)
            last = steps(eng, 1, U1, E // 2, False, step)
            result(last, 2 * U1)

        def ffn1_vector(eng):
            def weights_lo(par, f, stbuf, count):
                q, rows, a, b = ffn1_slice(f)
                at = PIECE[q][0]
                eng.wait_ge(sem("f1_wh"), count)
                eng.scalar_tensor_tensor(out=flat_w(par, 1)[0:rows, at + a:at + b], in0=stage[0:rows, stbuf, a:b],
                                         scalar=WS, in1=flat_w(par, 0)[0:rows, at + a:at + b],
                                         op0=ALU.mult, op1=ALU.subtract).then_inc(sem("f1_wl"), 1)

            def tokens_lo(e, par):
                eng.wait_ge(sem("f1_xhi"), e + 1)
                eng.tensor_tensor(xt[:, par, 1, :].rearrange("p (c n) -> p c n", c=DC), ps[:, 6:8, :],
                                  xt[:, par, 0, :].rearrange("p (c n) -> p c n", c=DC), ALU.subtract)\
                   .then_inc(sem("f1_xlo"), 1)

            def step(i, k):
                par, f = k // U1 % 2, k % U1
                m = FT1 if f == FC1 - 1 else P
                u, e = i * (2 * U1) + k, i * 2 + k // U1
                eng.wait_ge(sem("f1_b"), u + 1)
                eng.wait_ge(sem("f1_g"), u + 1)
                free(eng, sem("f1_lo"), u)
                eng.scalar_tensor_tensor(out=hid[0:m, k % 2, :], in0=ps[0:m, 2 + k % 2, :], scalar=HS1 / WS,
                                         in1=hga[0:m, k % 2, :], op0=ALU.mult, op1=ALU.mult).then_inc(sem("f1_m"), 1)
                if not (isinstance(i, int) and i == E // 2 - 1 and k >= U1):
                    piece = 3 * (k // U1 + 1) + ffn1_slice(f)[0]
                    weights_lo(1 - par, f, piece % 2, e * U1 + (U1 + f + 1))
                    if f == 7:
                        tokens_lo(e + 1, 1 - par)
                eng.wait_ge(sem("f1_hi"), u + 1)
                eng.tensor_tensor(hl[0:m, k % 2, :], hid[0:m, k % 2, :], hh[0:m, k % 2, :],
                                  ALU.subtract).then_inc(sem("f1_lo"), 1)

            eng.sem_inc(sem("f1_m"), 1)
            eng.sem_inc(sem("f1_lo"), 1)
            for f in range(U1):
                weights_lo(0, f, ffn1_slice(f)[0] % 2, f + 1)
            tokens_lo(0, 0)
            steps(eng, 1, U1, E // 2, False, step)

        back2 = arena[:, :, :, :].rearrange("p a b c -> p (a b c)").bitcast(F32)[:, 0:NT * D]

        def ffn1_add(eng):
            for t in range(NT):
                if t % 4 == 0:
                    eng.wait_ge(sem(f"back1_{t // 4}"), 64)
                eng.scalar_tensor_tensor(out=xtile(t), in0=xns[:, t * D:(t + 1) * D], scalar=gs[:, 2, t:t + 1],
                                         in1=xtile(t), op0=ALU.mult, op1=ALU.add).then_inc(sem("add1"), 1)
                if t % 4 == 0:
                    eng.wait_ge(sem(f"back2_{t // 4}"), 64)
                eng.wait_ge(sem("add1"), t + 1)
                eng.scalar_tensor_tensor(out=xtile(t), in0=back2[:, t * D:(t + 1) * D], scalar=gs[:, 3, t:t + 1],
                                         in1=xtile(t), op0=ALU.mult, op1=ALU.add).then_inc(sem("add2"), 1)

        def x_stores(eng):
            o = out.rearrange("b (u p) n -> p (b u) n", p=P)
            for t in range(0, NT, 4):
                eng.wait_ge(sem("add2"), t + 4)
                eng.dma_start(o[:, t:t + 4, :], x_sb[:, t * D:(t + 4) * D].rearrange("p (t n) -> p t n", n=D))\
                   .then_inc(sem("xout"), 16)
            eng.wait_ge(sem("xout"), 16 * (NT // 4))

        sem("load"), sem("xload"), sem("xout")

        block = ctx.enter_context(nc.Block())

        @block.sync
        def _(sp):
            xv = x.rearrange("b (u p) n -> p (b u) n", p=P)
            for t in range(0, NT, 4):
                sp.dma_start(x_sb[:, t * D:(t + 4) * D].rearrange("p (t n) -> p t n", n=D), xv[:, t:t + 4, :])\
                  .then_inc(sem("xload"), 16)
            sp.dma_start(cst[:, :], consts).then_inc(sem("load"), 16)
            sp.dma_start(vec[:, :], vecs).then_inc(sem("load"), 16)
            att_loads(sp, att[0])
            sp.wait_ge(sem("zeros"), 1)
            for rows in (slots0, slots1[0:E * SL, :]):
                n = rows.shape[0] // P
                sp.dma_start(rows.rearrange("(k p) n -> p k n", p=P), y_sb[:, 0:D].unsqueeze(1).to_broadcast([P, n, D]))\
                  .then_inc(sem("zfill"), 16)
            ffn0_loads(sp)
            sp.wait_ge(att[0].s("x"), NT)
            att_loads(sp, att[1])
            sp.wait_ge(att[1].s("vs"), NB)
            ffn1_loads(sp)
            x_stores(sp)
            for name, count in (("f0_out", 16 * SLT + 32), ("f1_out", 16 * E + 16), ("scat0", 16 * NT), ("scat1", 32 * NT)):
                sp.wait_ge(sem(name), count)

        @block.gpsimd
        def _(pool):
            pool.memset(y_sb[:, 0:D], 0.0).then_inc(sem("zeros"), 1)
            for n in range(2):
                a = att[n]
                v = a.v.rearrange("p (b h n) -> p b h n", b=NB, h=a.H)
                if n:
                    pool.wait_ge(sem("f0_y"), SLT * U0 + 1)
                pool.memset(v[:, :, :, a.dh], 1.0).then_inc(a.s("ones"), 1)
                scatter_pool(pool, n)
                if n == 0:
                    pool.wait_ge(sem("f0_out"), 16 * SLT + 32)
                    gather_pool(pool, 0, y0, gi[:, 0, :], xns)
            pool.wait_ge(sem("f1_out"), 16 * E + 16)
            gather_pool(pool, 1, y1, gi[:, 0, :], xns)
            gather_pool(pool, 2, y1, gi[:, 1, :], back2)

        @block.scalar
        def _(act):
            act.wait_ge(sem("load"), 32)
            ln_stats_scalar(act, 0)
            att_scalar(act, att[0])
            ln_stats_scalar(act, 1)
            route_scalar(act, 0)
            ffn0_scalar(act)
            ln_stats_scalar(act, 2)
            att_scalar(act, att[1])
            ln_stats_scalar(act, 3)
            route_scalar(act, 1)
            gate1_scalar(act)
            ffn1_scalar(act)

        @block.vector
        def _(dve):
            ln_stats_vector(dve, 0, lambda: dve.wait_ge(sem("xload"), 16 * (NT // 4)))
            dve.wait_ge(sem("load"), 32)
            att_kv_vector(dve, att[0])
            att_vector(dve, att[0])
            ln_stats_vector(dve, 1, lambda: dve.wait_ge(att[0].s("x"), NT))
            route_vector(dve, 0)
            gate0_vector(dve)
            ffn0_vector(dve)
            ffn0_add(dve)
            ln_stats_vector(dve, 2, lambda: dve.wait_ge(sem("add0"), NT))
            att_kv_vector(dve, att[1])
            att_vector(dve, att[1])
            ln_stats_vector(dve, 3, lambda: dve.wait_ge(att[1].s("x"), NT))
            route_vector(dve, 1)
            gate1_vector(dve)
            ffn1_vector(dve)
            ffn1_add(dve)

        @block.tensor
        def _(pe):
            pe.wait_ge(sem("load"), 32)
            att_kv_tensor(pe, att[0])
            att_tensor(pe, att[0])
            route_tensor(pe, 0)
            gate0_tensor(pe)
            ffn0_tensor(pe)
            pe.wait_ge(sem("f0_yx"), SLT + 2)
            att_kv_tensor(pe, att[1])
            att_tensor(pe, att[1])
            route_tensor(pe, 1)
            gate1_tensor(pe)
            ffn1_tensor(pe)


def kernel(**inputs):
    import numpy as np
    import concourse.bacc as bacc
    from concourse.bass_utils import run_bass_kernel_spmd

    g = {k: np.ascontiguousarray(v) for k, v in inputs.items()}

    def chunks(w, rows):
        return np.ascontiguousarray(w.reshape(w.shape[0] // rows, rows, w.shape[1]).transpose(1, 0, 2))

    def cols(v):
        return v.reshape(-1, P).T

    def wide(v):
        return np.broadcast_to(v, (P, v.shape[-1]))

    p = np.arange(P)
    t, e = np.arange(NT)[:, None], np.arange(E)[None, :]
    consts = np.concatenate([
        p[:, None] == p[None, :],
        p[:, None] < p[None, :],
        np.ones((P, P)),
        wide((np.zeros((NT, 1)) + (E - e)).reshape(1, -1)),
        wide((e * SL + (t // TPB) * CAP).reshape(1, -1)),
        wide((t + 0 * e).reshape(1, -1)),
        wide((0 * e.T + ST * e).reshape(1, -1)),
        t.T * P + p[:, None],
        p[:, None] // 16 == np.arange(8)[None],
        p[:, None] // 64 == np.arange(2)[None],
    ], axis=1).astype(np.float32)
    vecs = np.ascontiguousarray(np.concatenate([
        cols(g["L0_xattn_bq"]), cols(g["L0_xattn_bk"]),
        wide(g["L0_xattn_bv"]), wide(g["L0_xattn_bo"]), wide(g["L1_xattn_bo"]), wide(g["L0_ffn_br"]),
        chunks(g["L0_ffn_wr"], P).reshape(P, -1), chunks(g["L1_ffn_router_w"], P).reshape(P, -1),
    ], axis=1))
    assert consts.shape[1] == C_END and vecs.shape[1] == V_END
    ctx_t = chunks(np.ascontiguousarray(g["ctx_768"].reshape(NB * CK, CC).T), CR)
    arrays = {
        "x": g["x"], "ctx_t": ctx_t, "consts": consts, "vecs": vecs, 
        "b1c": np.ascontiguousarray(g["L0_ffn_b1"].reshape(E, FC0, P).transpose(0, 2, 1)),
        "b2w": np.ascontiguousarray(np.broadcast_to(g["L0_ffn_b2"][:, None], (E, P, D))),
        "wq0": chunks(g["L0_xattn_Wq"], P), "wk0": chunks(g["L0_xattn_Wk"], CR),
        "wv0": chunks(g["L0_xattn_Wv"], CR), "wo0": chunks(g["L0_xattn_Wo"], P),
        "wq1": chunks(g["L1_xattn_Wq"], P), "wk1": chunks(g["L1_xattn_Wk"], CR),
        "wv1": chunks(g["L1_xattn_Wv"], CR), "wo1": chunks(g["L1_xattn_Wo"], P),
        "f0w1": g["L0_ffn_w1"], "f0w2": g["L0_ffn_w2"],
        "f1w0": g["L1_ffn_w0_kernel"], "f1w1": g["L1_ffn_w1_kernel"], "f1wo": g["L1_ffn_wo_kernel"],
    }
    nc = bacc.Bacc("TRN2", target_bir_lowering=False, num_devices=1)
    args = [nc.dram_tensor(f"in_{k}", a.shape, mybir.dt.from_np(a.dtype), kind="ExternalInput").ap()
            for k, a in arrays.items()]
    out = nc.dram_tensor("out_x", (NB, TPB * P, D), F32, kind="ExternalOutput").ap()
    build(nc, *args, out)
    r = run_bass_kernel_spmd(nc, [{f"in_{k}": a for k, a in arrays.items()}], core_ids=[0])
    return r.results[0]["out_x"]
```

```python
from contextlib import ExitStack

import concourse.bass as bass
from concourse import mybir

F32 = mybir.dt.float32
F16 = mybir.dt.float16
U32 = mybir.dt.uint32
ALU = mybir.AluOpType
ACT = mybir.ActivationFunctionType
AX = mybir.AxisListType.X

P = 128
NB = 8
TPB = 2
NT = NB * TPB
D = 256
DC = D // P
CK = 77
CC = 192
CR = 96
E = 8
F0 = 1024
FC0 = F0 // P
F1 = 1368
FC1 = (F1 + P - 1) // P
FT1 = F1 - (FC1 - 1) * P
CAP = 64
SL = NB * CAP
ST = 256
SLT = NT * P // ST + E - 1
EPS = 1e-5
CLAMP = 10000.0

WS = 128.0
XS = 64.0
QS = 4.0
VS = 8.0
PS = 1024.0
OS = 8.0
HS0 = 8.0
HS1 = 1.0 / 32

C_ID, C_TRI, C_ONE, C_REV, C_ROW, C_J, C_K, C_TOK, C_HM0, C_HM1 = 0, 128, 256, 384, 512, 640, 768, 832, 848, 856
C_END = 858
V_BQ, V_BK, V_BV, V_BO0, V_BO1, V_BR, V_WR0, V_WR1 = 0, 2, 4, 260, 516, 772, 780, 796
V_END = 812


def build(nc, x, ctx_t, consts, vecs, b1c, b2w, wq0, wk0, wv0, wo0, wq1, wk1, wv1, wo1, f0w1, f0w2, f1w0, f1w1, f1wo, out):
    slots0 = nc.dram_tensor("slots0", (SLT * ST, D), F32, kind="Internal").ap()
    slots1 = nc.dram_tensor("slots1", (E * SL + 2 * NT * P, D), F32, kind="Internal").ap()
    y0 = nc.dram_tensor("y0_rows", (SLT * ST, D), F32, kind="Internal").ap()
    y1 = nc.dram_tensor("y1_rows", (E * SL, D), F32, kind="Internal").ap()
    ctx = ExitStack()
    with ctx:
        def sb(name, shape, dt=F32):
            return ctx.enter_context(nc.sbuf_tensor(name, shape, dt))

        sems = {}

        def sem(name):
            if name not in sems:
                sems[name] = ctx.enter_context(nc.semaphore(name))
            return sems[name]

        x_sb = sb("x_sb", [P, NT * D])
        cst = sb("cst", [P, C_END])
        vec = sb("vec", [P, V_END])
        aw = sb("aw", [P, 16 * D])
        xt = sb("xt", [P, 2, 2, DC * SL], F16)
        xns = sb("xns", [P, NT * D])
        xs = sb("xs", [P, 2, 2 * D])
        xs4 = xs[:, :, :].rearrange("p a n -> p (a n)")
        b1t = sb("b1t", [P, 2, FC0])
        b2t = sb("b2t", [P, 2, D])
        texp = sb("texp", [P, NT], U32)
        si = sb("si", [P, 2, NT], U32)
        stage = sb("stage", [P, 2, FC1 * D])
        W1 = 2 * DC * F1 + FC1 * D
        arena = sb("arena", [P, 2, 2, W1], F16)
        s_exp = sb("s_exp", [P, 16 * CK])
        p_exp = sb("p_exp", [P, 16 * CK])
        xnt = sb("xnt", [P, 4, 2, D], F16)
        red = sb("red", [P, 16])
        rec = sb("rec", [P, 16])
        wrs = sb("wrs", [P, 2, 2, DC * E], F16)
        st6 = sb("st6", [P, NT, 6])
        mv = sb("mv", [P, NT * 2])
        rstd = sb("rstd", [P, NT])
        y_sb = sb("y_sb", [P, 4 * D])
        hid = sb("hid", [P, 2, 4 * P])
        hga = sb("hga", [P, 2, 4 * P])
        o_n, qf = hid[:, 0, :], hga[:, 0, :]
        py = hga[:, 1, :]
        xn = sb("xn", [P, 2, D])
        bvs = sb("bvs", [1, 3, D], F16)
        bqk = sb("bqk", [P, 4])
        hh = sb("hh", [P, 2, 4 * P], F16)
        hl = sb("hl", [P, 2, 4 * P], F16)
        lg = sb("lg", [P, NT * E])
        gt = sb("gt", [P, 12, NT * E])
        gs = sb("gs", [P, 12, NT])
        gi = sb("gi", [P, 2, NT], U32)
        ps = ctx.enter_context(nc.psum_tensor("ps", [P, 8, 512], F32))

        ident = cst[:, C_ID:C_ID + P]
        tri = cst[:, C_TRI:C_TRI + P]
        ones = cst[:, C_ONE:C_ONE + P]

        def xtile(t):
            return x_sb[:, bass.ds(t * D, D)] if not isinstance(t, int) else x_sb[:, t * D:(t + 1) * D]

        def cols(tensor, start, n):
            return tensor[:, bass.ds(start, n)] if not isinstance(start, int) else tensor[:, start:start + n]

        def free(eng, s, count):
            if not isinstance(count, int) or count > 0:
                eng.wait_ge(s, count)

        def three(eng, out_ap, a, b, first, last, shared=False):
            eng.matmul(out_ap, a[0], b[0], start=first, stop=False, skip_group_check=shared)
            eng.matmul(out_ap, a[0], b[1], start=False, stop=False, skip_group_check=shared)
            return eng.matmul(out_ap, a[1], b[0], start=False, stop=last, skip_group_check=shared)

        class Attention:

            def __init__(self, n, heads, dh, weights, mask_col, clip, bias):
                self.n, self.H, self.dh, self.weights = n, heads, dh, weights
                self.mask_col, self.clip, self.bias = mask_col, clip, bias
                self.inner = heads * dh
                self.nc = self.inner // P
                self.hpc = P // dh
                self.groups = heads // 4
                self.w = min(4, self.hpc) * CK
                self.per = self.hpc * CK // self.w
                self.ppb = n + 1
                self.banks = self.nc * self.per // self.ppb
                self.hb = 4 if n else 16
                self.pvb = 2 if n else 6
                self.scale = float(dh) ** -0.5
                flat = arena[:, :, :, :].rearrange("p a b c -> p (a b c)").bitcast(F32)
                nk = NB * heads * CK
                nv = NB * heads * (dh + 1)
                half = arena[:, :, :, :].rearrange("p a b c -> p (a b c)")
                self.kms = [half[:, s * nk:(s + 1) * nk] for s in range(2)]
                self.vs = [half[0:CK, 2 * nk + s * nv:2 * nk + (s + 1) * nv] for s in range(2)]
                at = 2 * (nk + nv)
                self.pts = [half[0:CK, at + s * heads * P:at + (s + 1) * heads * P] for s in range(2)]
                self.ctx_t = stage[0:CR, 0, 0:2 * NB * CK].rearrange("p (k n) -> p k n", k=2)
                i = self.inner
                at = nk + nv + heads * P
                end = at + 2 * DC * i
                self.kf = [flat[:, end + c * NB * CK:end + (c + 1) * NB * CK] for c in range(2)]

                def pair(tensor, rows, start, k, n):
                    return [tensor[0:rows, start + s * k * n:start + (s + 1) * k * n].rearrange("p (k n) -> p k n", k=k)
                            for s in range(2)]

                self.ctx_s = pair(s_exp[:, :].bitcast(F16), CR, 0, 2, NB * CK)
                self.wks = pair(hga[:, :, :].rearrange("p a n -> p (a n)").bitcast(F16), CR, 0, 2, i)
                self.wvs = pair(hid[:, :, :].rearrange("p a n -> p (a n)").bitcast(F16), CR, 0, 2, i)
                self.wqs = pair(half, P, 2 * at, DC, i)
                self.wos = pair(half, P, 2 * at + 2 * DC * i, self.nc, D)
                self.wq = aw[:, 0:DC * i].rearrange("p (k n) -> p k n", k=DC)
                self.wk = aw[0:CR, DC * i:DC * i + 2 * i].rearrange("p (k n) -> p k n", k=2)
                self.wv = aw[0:CR, DC * i + 2 * i:DC * i + 4 * i].rearrange("p (k n) -> p k n", k=2)
                self.wo = aw[:, DC * i + 4 * i:DC * i + 4 * i + self.nc * D].rearrange("p (k n) -> p k n", k=self.nc)

                self.splits = ((self.ctx_t, self.ctx_s, XS), (self.wk, self.wks, WS), (self.wv, self.wvs, WS),
                               (self.wq, self.wqs, WS), (self.wo, self.wos, WS))

            def s(self, name):
                return sem(f"att{self.n}_{name}")

        att = [
            Attention(0, 16, 16, (wk0, wv0, wq0, wo0), C_HM0, True, True),
            Attention(1, 8, 64, (wk1, wv1, wq1, wo1), C_HM1, False, False),
        ]
        for a in att:
            for name in ("w", "wh", "wl", "k", "kf", "kh", "km", "v", "vh", "vs", "ones", "xn", "xb", "xt", "xh", "xl", "q",
                         "qh", "ql", "sc", "max", "p", "pt", "ph", "pts", "pv", "rec", "on", "ot", "oh", "ol",
                         "pr", "py", "x") + (("qf", "sub", "neg") if a.clip else ("sub",)):
                a.s(name)
        sem("bias"), sem("wrh"), sem("wrl")
        for name in ("st", "mv", "ve", "sq", "rs"):
            sem(f"ln_{name}")

        def ln_tile(eng, n, t, done):
            eng.wait_ge(done, t + 1)
            dst = st6[:, t:t + 1, :] if isinstance(t, int) else st6[:, bass.ds(t, 1), :]
            eng.bn_stats(dst.rearrange("p a n -> p (a n)"), xtile(t)).then_inc(sem("ln_st"), 1)

        def ln_aggregate(eng, n, t):
            eng.wait_ge(sem("ln_st"), t + (n * NT + 1))
            src = st6[:, t:t + 1, :] if isinstance(t, int) else st6[:, bass.ds(t, 1), :]
            eng.bn_aggr(cols(mv, t * 2, 2), src.rearrange("p a n -> p (a n)")).then_inc(sem("ln_mv"), 1)

        def ln_finish_vector(eng, n):
            ln_variance(eng, n)
            ln_invert(eng, n)

        def ln_variance(eng, n):
            eng.wait_ge(sem("ln_mv"), (n + 1) * NT)
            eng.tensor_scalar(rstd[:, :], mv[:, 1:2 * NT:2], EPS, None, ALU.add).then_inc(sem("ln_ve"), 1)

        def ln_invert(eng, n):
            eng.wait_ge(sem("ln_sq"), n + 1)
            eng.reciprocal(rstd[:, :], rstd[:, :]).then_inc(sem("ln_rs"), 1)
            eng.wait_ge(sem("ln_rs"), n + 1)

        def ln_stats_scalar(eng, n):
            eng.wait_ge(sem("ln_ve"), n + 1)
            eng.activation(rstd[:, :], rstd[:, :], ACT.Sqrt).then_inc(sem("ln_sq"), 1)

        def normalize(eng, dst, t):
            return eng.tensor_scalar(dst, xtile(t), cols(mv, t * 2, 1), cols(rstd, t, 1), ALU.subtract, ALU.mult)

        def att_loads(eng, a):
            eng.dma_start(a.ctx_t, ctx_t).then_inc(a.s("w"), 16)
            for dst, src in zip((a.wk, a.wv, a.wq, a.wo), a.weights):
                eng.dma_start(dst, src).then_inc(a.s("w"), 16)

        def att_kv_tensor(eng, a):
            half = NB * CK // 2

            def keys(c):
                if c >= 2:
                    eng.wait_ge(a.s("kf"), c - 1)
                for h in range(2):
                    for k in range(2):
                        mm = three(eng, ps[:, 6 * (c % 2) + h, 0:half], [w[:, k, c * P:(c + 1) * P] for w in a.wks],
                                   [w[:, k, h * half:(h + 1) * half] for w in a.ctx_s], k == 0, k == 1)
                mm.then_inc(a.s("k"), 1)

            eng.wait_ge(a.s("wl"), 2)
            keys(0)
            keys(1)
            eng.wait_ge(a.s("wl"), 3)
            if a.bias:
                eng.wait_ge(sem("bias"), 2)
            for b in range(NB):
                if b >= 4:
                    eng.wait_ge(a.s("vs"), b - 3)
                dst = ps[0:CK, 2 + b % 4, 0:a.inner]
                for k in range(2):
                    mm = three(eng, dst, [w[:, k, b * CK:(b + 1) * CK] for w in a.ctx_s],
                               [w[:, k, :] for w in a.wvs], k == 0, k == 1 and not a.bias)
                if a.bias:
                    for s in range(2):
                        mm = eng.matmul(dst, bvs[0:1, 2, 0:CK], bvs[0:1, s, :], start=False, stop=(s == 1))
                mm.then_inc(a.s("v"), 1)
            for c in range(2, a.nc):
                keys(c)

        def att_split_scalar(eng, a):
            eng.wait_ge(a.s("w"), 80)
            for src, dst, scale in a.splits:
                eng.activation(dst[0], src, ACT.Copy, scale=scale).then_inc(a.s("wh"), 1)

        def att_split_vector(eng, a):
            if a.bias:
                eng.memset(bvs[:, 2, :], XS)
                eng.tensor_scalar(bqk[:, :], vec[:, V_BQ:V_BQ + 4], QS, None, ALU.mult)
                bv = vec[0:1, V_BV:V_BV + D]
                eng.tensor_scalar(bvs[:, 0, :], bv, WS, None, ALU.mult).then_inc(sem("bias"), 1)
                eng.wait_ge(sem("bias"), 1)
                eng.scalar_tensor_tensor(out=bvs[:, 1, :], in0=bv, scalar=WS, in1=bvs[:, 0, :], op0=ALU.mult,
                                         op1=ALU.subtract).then_inc(sem("bias"), 1)
            for n, (src, dst, scale) in enumerate(a.splits):
                eng.wait_ge(a.s("wh"), n + 1)
                eng.scalar_tensor_tensor(out=dst[1], in0=src, scalar=scale, in1=dst[0], op0=ALU.mult,
                                         op1=ALU.subtract).then_inc(a.s("wl"), 1)

        def value_views(a, b):
            dst = [v.rearrange("p (b h n) -> p b h n", b=NB, h=a.H)[:, b, :, 0:a.dh] for v in a.vs]
            return dst, ps[0:CK, 2 + b % 4, 0:a.inner].rearrange("p (h n) -> p h n", n=a.dh)

        def att_kv_scalar(eng, a, chunks):
            kmh = a.kms[0].rearrange("p (b h n) -> p b h n", b=NB, h=a.H)
            for c in chunks:
                eng.wait_ge(a.s("k"), c + 1)
                if c >= 2:
                    eng.wait_ge(a.s("km"), (c - 1) * a.hpc)
                src = ps[:, 6 * (c % 2):6 * (c % 2) + 2, 0:NB * CK // 2]
                dst = a.kf[c % 2].rearrange("p (h n) -> p h n", h=2)
                if a.bias:
                    ins = eng.activation(dst, src, ACT.Identity, bias=bqk[:, 2 + c:3 + c], scale=QS / (WS * XS))
                else:
                    ins = eng.activation(dst, src, ACT.Copy, scale=QS / (WS * XS))
                ins.then_inc(a.s("kf"), 1)
                for j in range(NB if c == 1 else a.hpc):
                    if j == 0:
                        eng.wait_ge(a.s("kf"), c + 1)
                    if j < a.hpc:
                        eng.activation(kmh[:, :, c * a.hpc + j, :], a.kf[c % 2].rearrange("p (b n) -> p b n", b=NB), ACT.Copy,
                                       scale=cst[:, a.mask_col + j:a.mask_col + j + 1]).then_inc(a.s("kh"), 1)
                    if c == 1:
                        dst, src = value_views(a, j)
                        eng.wait_ge(a.s("v"), j + 1)
                        eng.activation(dst[0], src, ACT.Copy, scale=VS / (WS * XS)).then_inc(a.s("vh"), 1)

        def att_kv_vector(eng, a, chunks):
            kmh, kml = (k.rearrange("p (b h n) -> p b h n", b=NB, h=a.H) for k in a.kms)
            for c in chunks:
                for j in range(NB if c == 1 else a.hpc):
                    if j < a.hpc:
                        h = c * a.hpc + j
                        eng.wait_ge(a.s("kh"), h + 1)
                        eng.scalar_tensor_tensor(out=kml[:, :, h, :], in0=a.kf[c % 2].rearrange("p (b n) -> p b n", b=NB),
                                                 scalar=cst[:, a.mask_col + j:a.mask_col + j + 1], in1=kmh[:, :, h, :],
                                                 op0=ALU.mult, op1=ALU.subtract).then_inc(a.s("km"), 1)
                    if c == 1:
                        dst, src = value_views(a, j)
                        eng.wait_ge(a.s("vh"), j + 1)
                        eng.scalar_tensor_tensor(out=dst[1], in0=src, scalar=VS / (WS * XS), in1=dst[0], op0=ALU.mult,
                                                 op1=ALU.subtract).then_inc(a.s("vs"), 1)

        def att_prepare_pool(eng, a):
            vb = V_BO1 if a.n else V_BO0
            eng.wait_ge(sem("ln_rs"), 2 * a.n + 1)
            lag = 2 * AHEAD
            for t in range(NT + lag):
                if t < NT:
                    if t >= 2:
                        eng.wait_ge(a.s("xt"), t - 1)
                    normalize(eng, xn[:, t % 2, :], t).then_inc(a.s("xn"), 1)
                    eng.wait_ge(a.s("xn"), t + 1)
                    eng.tensor_tensor(xtile(t), xtile(t), vec[:, vb:vb + D], ALU.add).then_inc(a.s("xb"), 1)
                if t >= lag:
                    v = t - lag
                    eng.wait_ge(a.s("py"), v + 1)
                    eng.wait_ge(a.s("xb"), v + 1)
                    eng.tensor_tensor(xtile(v), xtile(v), py[:, v % 2 * D:(v % 2 + 1) * D], ALU.add).then_inc(a.s("x"), 1)

        AHEAD = 3

        def over_tiles(eng, opening, parts):
            def step(i, u):
                for offset, part in opening if isinstance(i, int) and i < 0 else parts:
                    v = u + offset
                    if not isinstance(i, int) or 0 <= 2 * i + v < NT:
                        part(i + v // 2, v % 2)

            for s in range(-AHEAD, 4):
                step(s // 2, s % 2)
            with eng.Fori(2, (NT - AHEAD) // 2) as i:
                step(i, 0)
                step(i, 1)
            for s in range((NT - AHEAD) // 2 * 2, NT + 3):
                step(s // 2, s % 2)

        def ahead(t, n):
            return min(t + n, NT) if isinstance(t, int) else t + n

        def att_tensor(eng, a):
            G = a.groups

            def turn_x(i, u):
                t = i * 2 + u
                free(eng, a.s("pts"), t * G - 2 * G)
                eng.wait_ge(a.s("xn"), t + 1)
                for c in range(DC):
                    mm = eng.transpose(ps[:, 7, c * P:(c + 1) * P], xn[:, u, c * P:(c + 1) * P], ident)
                mm.then_inc(a.s("xt"), 1)

            def queries(i, u):
                t = i * 2 + u
                free(eng, a.s("ol"), t - 3)
                eng.wait_ge(a.s("xl"), t + 1)
                for c in range(a.nc):
                    for k in range(DC):
                        mm = three(eng, ps[:, 4, c * P:(c + 1) * P], [w[:, k, c * P:(c + 1) * P] for w in a.wqs],
                                   [xt[:, 0, s, k * P:(k + 1) * P] for s in range(2)], k == 0, k == DC - 1)
                mm.then_inc(a.s("q"), 1)

            def scores(i, u):
                t = i * 2 + u
                if isinstance(t, int) and t == 0:
                    eng.wait_ge(a.s("km"), a.H)
                eng.wait_ge(a.s("ql"), t + 1)
                free(eng, a.s("sub"), t)
                for c in range(a.nc):
                    for h in range(a.per):
                        m = c * a.per + h
                        mm = three(eng, ps[:, m // a.ppb, m % a.ppb * a.w:(m % a.ppb + 1) * a.w],
                                   [q[:, 0, c * P:(c + 1) * P] for q in (hh, hl)],
                                   [cols(k, i * (a.H * CK) + m * a.w, a.w) for k in a.kms], True, True)
                mm.then_inc(a.s("sc"), 1)

            def turn_p_first(i, u):
                turn_p(i, u, range(2))

            def turn_p_rest(i, u):
                turn_p(i, u, range(2, G))

            def turn_p(i, u, groups):
                t = i * 2 + u
                for g in groups:
                    if g == 0:
                        eng.wait_ge(a.s("p"), t + 1)
                        free(eng, a.s("on"), t)
                    if g == 1:
                        eng.wait_ge(a.s("xl"), ahead(t, AHEAD))
                    if g >= 2:
                        eng.wait_ge(a.s("pts"), t * G + (g - 1))
                    for j in range(4):
                        h = 4 * g + j
                        mm = eng.transpose(ps[0:CK, 6 + g % 2, j * P:(j + 1) * P], p_exp[:, h * CK:(h + 1) * CK], ident)
                    mm.then_inc(a.s("pt"), 1)

            def weighted(i, u):
                t, nv = i * 2 + u, a.dh + 1
                if isinstance(t, int) and t == 0:
                    eng.wait_ge(a.s("vs"), NB)
                    eng.wait_ge(a.s("ones"), 2)
                eng.wait_ge(a.s("pts"), t * G + G)
                for h in range(a.H):
                    mm = three(eng, ps[:, a.pvb + h // a.hb, (h % a.hb) * nv:(h % a.hb + 1) * nv],
                               [p[:, h * P:(h + 1) * P] for p in a.pts],
                               [cols(v, i * (a.H * nv) + h * nv, nv) for v in a.vs], True, True)
                mm.then_inc(a.s("pv"), 1)

            def turn_o(i, u):
                t = i * 2 + u
                eng.wait_ge(a.s("on"), t + 1)
                eng.wait_ge(a.s("ql"), ahead(t, 4))
                for c in range(a.nc):
                    mm = eng.transpose(ps[:, 4, c * P:(c + 1) * P], o_n[:, c * P:(c + 1) * P], ident)
                mm.then_inc(a.s("ot"), 1)

            def project(i, u):
                t = i * 2 + u
                eng.wait_ge(a.s("ol"), t + 1)
                free(eng, a.s("py"), t)
                for c in range(a.nc):
                    mm = three(eng, ps[:, 5, 0:D], [o[:, 1, c * P:(c + 1) * P] for o in (hh, hl)],
                               [w[:, c, :] for w in a.wos], c == 0, c == a.nc - 1)
                mm.then_inc(a.s("pr"), 1)

            eng.wait_ge(a.s("wl"), len(a.splits))
            eng.wait_ge(a.s("vs"), NB)
            eng.wait_ge(a.s("kf"), a.nc)
            opening = ((2, queries), (3, turn_x), (2, scores))
            if a.n == 0:
                steady = ((2, queries), (-2, project), (0, turn_p_first), (0, turn_p_rest), (-1, turn_o), (2, scores),
                          (3, turn_x), (0, weighted))
            else:
                steady = ((2, queries), (0, turn_p_first), (-2, project), (3, turn_x), (-1, turn_o), (2, scores),
                          (0, weighted))
            over_tiles(eng, opening, steady)

        def att_vector(eng, a):
            H = a.H
            lim = CLAMP / a.scale * QS * QS

            def x_lo(i, u):
                t = i * 2 + u
                eng.wait_ge(a.s("xh"), t + 1)
                free(eng, a.s("q"), t)
                eng.scalar_tensor_tensor(out=xt[:, 0, 1, 0:D], in0=ps[:, 7, 0:D], scalar=XS, in1=xt[:, 0, 0, 0:D],
                                         op0=ALU.mult, op1=ALU.subtract).then_inc(a.s("xl"), 1)

            hpb = H // a.banks
            s4 = ps[:, 0:a.banks, 0:hpb * CK].rearrange("p k (h n) -> p k h n", n=CK)
            sx = s_exp[:, 0:H * CK].rearrange("p (k h n) -> p k h n", k=a.banks, n=CK)
            r4 = red[:, 0:H].rearrange("p (k h) -> p k h", k=a.banks)

            def maximum(i, u):
                t = i * 2 + u
                eng.wait_ge(a.s("sc"), t + 1)
                eng.reduce_max(r4, s4, AX).then_inc(a.s("max"), 1)

            def subtract(i, u):
                t = i * 2 + u
                if a.clip:
                    eng.wait_ge(a.s("max"), t * 2 + 1)
                    eng.tensor_scalar(red[:, 0:H], red[:, 0:H], lim, -lim, ALU.min, ALU.max).then_inc(a.s("max"), 1)
                    eng.wait_ge(a.s("max"), t * 2 + 2)
                else:
                    eng.wait_ge(a.s("max"), t + 1)
                free(eng, a.s("p"), t)
                m = r4.unsqueeze(3).to_broadcast([P, a.banks, hpb, CK])
                if a.clip:
                    ins = eng.scalar_tensor_tensor(out=sx, in0=s4, scalar=-lim, in1=m, op0=ALU.max, op1=ALU.subtract)
                else:
                    ins = eng.tensor_tensor(sx, s4, m, ALU.subtract)
                ins.then_inc(a.s("sub"), 1)

            def p_lo_first(i, u):
                p_lo(i, u, range(2))

            def p_lo_rest(i, u):
                p_lo(i, u, range(2, a.groups))

            def p_lo(i, u, groups):
                t = i * 2 + u
                for g in groups:
                    eng.wait_ge(a.s("ph"), t * a.groups + (g + 1))
                    cut = slice(g * 4 * P, (g + 1) * 4 * P)
                    eng.scalar_tensor_tensor(out=a.pts[1][:, cut], in0=ps[0:CK, 6 + g % 2, :], scalar=PS,
                                             in1=a.pts[0][:, cut], op0=ALU.mult, op1=ALU.subtract).then_inc(a.s("pts"), 1)

            def stats(i, u):
                ln_tile(eng, 2 * a.n + 1, i * 2 + u, a.s("x"))

            def q_lo(i, u):
                t = i * 2 + u
                eng.wait_ge(a.s("qh"), t + 1)
                free(eng, a.s("sc"), t)
                if a.bias:
                    ins = eng.tensor_tensor(hl[:, 0, 0:a.inner], qf[:, 0:a.inner], hh[:, 0, 0:a.inner], ALU.subtract)
                else:
                    ins = eng.scalar_tensor_tensor(out=hl[:, 0, 0:a.inner], in0=ps[:, 4, 0:a.inner], scalar=QS / (WS * XS),
                                                   in1=hh[:, 0, 0:a.inner], op0=ALU.mult, op1=ALU.subtract)
                ins.then_inc(a.s("ql"), 1)

            def average(i, u):
                t, nv = i * 2 + u, a.dh + 1
                eng.wait_ge(a.s("pv"), t + 1)
                free(eng, a.s("ot"), t)
                nb = H // a.hb
                pv = ps[:, a.pvb:a.pvb + nb, 0:a.hb * nv].rearrange("p k (h n) -> p k h n", n=nv)
                r3 = rec[:, 0:H].rearrange("p (k h) -> p k h", k=nb)
                dst = o_n[:, 0:a.inner].rearrange("p (k h n) -> p k h n", k=nb, n=a.dh)
                eng.reciprocal(r3, pv[:, :, :, a.dh]).then_inc(a.s("rec"), 1)
                eng.wait_ge(a.s("rec"), t + 1)
                eng.tensor_tensor(dst, pv[:, :, :, 0:a.dh], r3.unsqueeze(3).to_broadcast([P, nb, a.hb, a.dh]), ALU.mult)\
                   .then_inc(a.s("on"), 1)

            def o_lo(i, u):
                t = i * 2 + u
                eng.wait_ge(a.s("oh"), t + 1)
                free(eng, a.s("pr"), t)
                eng.scalar_tensor_tensor(out=hl[:, 1, 0:a.inner], in0=ps[:, 4, 0:a.inner], scalar=OS,
                                         in1=hh[:, 1, 0:a.inner], op0=ALU.mult, op1=ALU.subtract).then_inc(a.s("ol"), 1)

            opening = ((1, subtract), (2, q_lo), (3, x_lo), (2, maximum))
            if a.n == 0:
                steady = ((1, subtract), (0, p_lo_first), (2, q_lo), (0, p_lo_rest), (-3, stats),
                          (-1, o_lo), (2, maximum), (3, x_lo), (0, average))
            else:
                steady = ((1, subtract), (0, p_lo_first), (2, q_lo), (3, x_lo), (-3, stats),
                          (-1, o_lo), (2, maximum), (0, average))
            over_tiles(eng, opening, steady)
            for t in range(NT):
                ln_aggregate(eng, 2 * a.n + 1, t)

        def att_scalar(eng, a):
            def x_hi(i, u):
                t = i * 2 + u
                eng.wait_ge(a.s("xt"), t + 1)
                free(eng, a.s("q"), t)
                eng.activation(xt[:, 0, 0, 0:D], ps[:, 7, 0:D], ACT.Copy, scale=XS).then_inc(a.s("xh"), 1)

            def p_hi_first(i, u):
                p_hi(i, u, range(2))

            def p_hi_rest(i, u):
                p_hi(i, u, range(2, a.groups))

            def p_hi(i, u, groups):
                t = i * 2 + u
                for g in groups:
                    eng.wait_ge(a.s("pt"), t * a.groups + (g + 1))
                    free(eng, a.s("pv"), t)
                    eng.activation(a.pts[0][:, g * 4 * P:(g + 1) * 4 * P], ps[0:CK, 6 + g % 2, :], ACT.Copy, scale=PS)\
                       .then_inc(a.s("ph"), 1)

            def q_hi(i, u):
                t = i * 2 + u
                eng.wait_ge(a.s("q"), t + 1)
                if a.bias:
                    free(eng, a.s("ql"), t)
                    for c in range(a.nc):
                        ins = eng.activation(qf[:, c * P:(c + 1) * P], ps[:, 4, c * P:(c + 1) * P], ACT.Identity,
                                             bias=bqk[:, c:c + 1], scale=QS / (WS * XS))
                    ins.then_inc(a.s("qf"), 1)
                    eng.wait_ge(a.s("qf"), t + 1)
                free(eng, a.s("sc"), t)
                if a.bias:
                    ins = eng.activation(hh[:, 0, 0:a.inner], qf[:, 0:a.inner], ACT.Copy)
                else:
                    ins = eng.activation(hh[:, 0, 0:a.inner], ps[:, 4, 0:a.inner], ACT.Copy, scale=QS / (WS * XS))
                ins.then_inc(a.s("qh"), 1)

            def negate(i, u):
                t = i * 2 + u
                if a.clip:
                    eng.wait_ge(a.s("sub"), t + 1)
                    eng.activation(s_exp[:, 0:a.H * CK], s_exp[:, 0:a.H * CK], ACT.Relu, scale=-1.0).then_inc(a.s("neg"), 1)

            def exponential(i, u):
                t = i * 2 + u
                eng.wait_ge(a.s("neg" if a.clip else "sub"), t + 1)
                free(eng, a.s("pt"), t * a.groups)
                eng.activation(p_exp[:, 0:a.H * CK], s_exp[:, 0:a.H * CK], ACT.Exp,
                               scale=(-1.0 if a.clip else 1.0) * a.scale / (QS * QS)).then_inc(a.s("p"), 1)

            def evacuate(i, u):
                t = i * 2 + u
                eng.wait_ge(a.s("pr"), t + 1)
                free(eng, a.s("x"), t - 1)
                eng.activation(py[:, u * D:(u + 1) * D], ps[:, 5, 0:D], ACT.Copy, scale=1.0 / (WS * OS)).then_inc(a.s("py"), 1)

            def o_hi(i, u):
                t = i * 2 + u
                eng.wait_ge(a.s("ot"), t + 1)
                free(eng, a.s("pr"), t)
                eng.activation(hh[:, 1, 0:a.inner], ps[:, 4, 0:a.inner], ACT.Copy, scale=OS).then_inc(a.s("oh"), 1)

            opening = ((2, q_hi), (3, x_hi), (1, negate), (1, exponential))
            if a.n == 0:
                steady = ((2, q_hi), (-2, evacuate), (0, p_hi_first), (0, p_hi_rest), (-1, o_hi), (1, negate), (3, x_hi),
                          (1, exponential))
            else:
                steady = ((0, p_hi_first), (2, q_hi), (-2, evacuate), (3, x_hi), (-1, o_hi), (1, exponential))
            over_tiles(eng, opening, steady)

        for name in ("xn", "t", "xh", "xl", "l", "lb"):
            sem(f"rt_{name}")

        def wr(n):
            at = V_WR1 if n else V_WR0
            return vec[:, at:at + DC * E], [wrs[:, n, s, :] for s in range(2)]

        def wr_split_scalar(eng):
            for n in range(2):
                src, dst = wr(n)
                eng.activation(dst[0], src, ACT.Copy, scale=WS).then_inc(sem("wrh"), 1)

        def wr_split_vector(eng):
            for n in range(2):
                src, dst = wr(n)
                eng.wait_ge(sem("wrh"), n + 1)
                eng.scalar_tensor_tensor(out=dst[1], in0=src, scalar=WS, in1=dst[0], op0=ALU.mult, op1=ALU.subtract)\
                   .then_inc(sem("wrl"), 1)

        def route_vector(eng, n):
            normalize(eng, xns[:, 0:D], 0).then_inc(sem("rt_xn"), 1)
            normalize(eng, xns[:, D:2 * D], 1).then_inc(sem("rt_xn"), 1)
            for t in range(NT + 2):
                if t + 2 < NT:
                    normalize(eng, xns[:, (t + 2) * D:(t + 3) * D], t + 2).then_inc(sem("rt_xn"), 1)
                if t < NT:
                    eng.wait_ge(sem("rt_xh"), n * NT + t + 1)
                    eng.scalar_tensor_tensor(out=xnt[:, t % 4, 1, :], in0=ps[:, t % 4, 0:D], scalar=XS,
                                             in1=xnt[:, t % 4, 0, :], op0=ALU.mult, op1=ALU.subtract)\
                       .then_inc(sem("rt_xl"), 1)
                if t >= 2:
                    logits(eng, n, t - 2)
            eng.wait_ge(sem("rt_lb"), (n + 1) * NT)

        def logits(eng, n, t):
            eng.wait_ge(sem("rt_l"), n * NT + t + 1)
            dst, src = lg[:, t * E:(t + 1) * E], ps[:, 4 + t % 4, 0:E]
            if n == 0:
                ins = eng.scalar_tensor_tensor(out=dst, in0=src, scalar=1.0 / (WS * XS), in1=vec[:, V_BR:V_BR + E],
                                               op0=ALU.mult, op1=ALU.add)
            else:
                ins = eng.tensor_scalar(dst, src, 1.0 / (WS * XS), None, ALU.mult)
            ins.then_inc(sem("rt_lb"), 1)

        def route_tensor(eng, n):
            w = wr(n)[1]
            eng.wait_ge(att[n].s("x"), NT)

            def turn(t):
                eng.wait_ge(sem("rt_xn"), n * NT + t + 1)
                if t >= 4:
                    eng.wait_ge(sem("rt_xl"), n * NT + t - 3)
                for c in range(DC):
                    mm = eng.transpose(ps[:, t % 4, c * P:(c + 1) * P], xns[:, t * D + c * P:t * D + (c + 1) * P],
                                       ident)
                mm.then_inc(sem("rt_t"), 1)

            for t in range(3):
                turn(t)
            eng.wait_ge(sem("wrl"), 2)
            for t in range(NT):
                if t + 3 < NT:
                    turn(t + 3)
                eng.wait_ge(sem("rt_xl"), n * NT + t + 1)
                if t >= 4:
                    eng.wait_ge(sem("rt_lb"), n * NT + t - 3)
                for c in range(DC):
                    for s in range(4):
                        mm = eng.matmul(ps[:, 4 + t % 4, 0:E], xnt[:, t % 4, s // 2, c * P:(c + 1) * P],
                                        w[s % 2][:, c * E:(c + 1) * E], start=(c + s == 0), stop=(c == DC - 1 and s == 3))
                mm.then_inc(sem("rt_l"), 1)

        def route_scalar(eng, n):
            for t in range(NT):
                eng.wait_ge(sem("rt_t"), n * NT + t + 1)
                if t >= 4:
                    eng.wait_ge(sem("rt_l"), n * NT + t - 3)
                eng.activation(xnt[:, t % 4, 0, :], ps[:, t % 4, 0:D], ACT.Copy, scale=XS).then_inc(sem("rt_xh"), 1)

        def bcast(ap):
            return ap.unsqueeze(2).to_broadcast([P, NT, E])

        def over_t(ap):
            return ap.unsqueeze(1).to_broadcast([P, NT, E])

        def g3(k):
            return gt[:, k, :].rearrange("p (t e) -> p t e", e=E)

        def c3(at):
            return cst[:, at:at + NT * E].rearrange("p (t e) -> p t e", e=E)

        rev3, row3 = c3(C_REV), c3(C_ROW)
        lg3 = lg[:, :].rearrange("p (t e) -> p t e", e=E)

        class Chain:

            def __init__(self, eng, name):
                self.eng, self.sem, self.n = eng, sem(name), 0

            def __call__(self, ins):
                self.n += 1
                ins.then_inc(self.sem, 1)
                self.eng.wait_ge(self.sem, self.n)

        def first_max(eng, ch, values, top, tmp, one_hot):
            ch(eng.reduce_max(top, values, AX))
            ch(eng.tensor_tensor(tmp, values, bcast(top), ALU.is_equal))
            ch(eng.tensor_tensor(tmp, tmp, rev3, ALU.mult))
            ch(eng.reduce_max(gs[:, 11, :], tmp, AX))
            ch(eng.tensor_tensor(one_hot, tmp, bcast(gs[:, 11, :]), ALU.is_equal))

        def prefix(eng, ch, src, ping, pong, width, block):
            step = block
            while step < width:
                ch(eng.tensor_copy(ping[:, 0:step], src[:, 0:step]))
                ch(eng.tensor_tensor(ping[:, step:width], src[:, step:width], src[:, 0:width - step], ALU.add))
                src, ping, pong = ping, pong, ping
                step *= 2
            return src

        sem("rank"), sem("route0"), sem("oh0")

        def gate0_vector(eng):
            ch = Chain(eng, "gate0")
            first_max(eng, ch, lg3, gs[:, 0, :], g3(0), g3(1))
            eng.sem_inc(sem("oh0"), 1)
            eng.wait_ge(sem("rank"), 1)
            ch(eng.tensor_copy(gt[:, 2, :], ps[:, 1, 0:NT * E]))
            upto = prefix(eng, ch, gt[:, 2, :], gt[:, 3, :], gt[:, 4, :], NT * E, E)
            count = upto[:, (NT - 1) * E:NT * E]
            tiles = gt[:, 6, 0:E]
            cmp = gt[:, 0, 0:NB * E].rearrange("p (e k) -> p e k", e=E)
            kk = cst[:, C_K:C_K + NB * E].rearrange("p (e k) -> p e k", e=E)
            ch(eng.tensor_tensor(cmp, count.unsqueeze(2).to_broadcast([P, E, NB]), kk, ALU.is_gt))
            ch(eng.reduce_sum(tiles, cmp, AX))
            ends = prefix(eng, ch, tiles, gt[:, 7, 0:E], gt[:, 7, E:2 * E], E, 1)
            base = gt[:, 7, 2 * E:3 * E]
            ch(eng.tensor_tensor(base, ends, tiles, ALU.subtract))
            ch(eng.tensor_scalar(base, base, float(ST), None, ALU.mult))
            ch(eng.tensor_tensor(gt[:, 5, :], ps[:, 0, 0:NT * E], upto, ALU.add))
            ch(eng.tensor_tensor(gt[:, 5, :], gt[:, 5, :], gt[:, 2, :], ALU.subtract))
            ch(eng.tensor_tensor(g3(5), g3(5), over_t(base), ALU.add))
            ch(eng.tensor_tensor(g3(5), g3(5), g3(1), ALU.mult))
            ch(eng.reduce_sum(gs[:, 5, :], g3(5), AX))
            ch(eng.tensor_copy(gi[:, 0, :], gs[:, 5, :]))
            ch(eng.tensor_tensor(g3(0), c3(C_J), over_t(ends), ALU.is_ge))
            ch(eng.reduce_sum(gs[:, 6, :], g3(0), AX))
            ch(eng.tensor_scalar(texp[:, :], gs[:, 6, :], float(E - 1), None, ALU.min))
            eng.sem_inc(sem("route0"), 1)

        def gate0_tensor(eng):
            eng.wait_ge(sem("oh0"), 1)
            eng.matmul(ps[:, 0, 0:NT * E], tri, gt[:, 1, :], start=True, stop=True)
            eng.matmul(ps[:, 1, 0:NT * E], ones, gt[:, 1, :], start=True, stop=True).then_inc(sem("rank"), 1)

        sem("gmax"), sem("gexp"), sem("oh1"), sem("p1"), sem("m1k"), sem("p2"), sem("route1")

        def gate1_vector(eng):
            ch = Chain(eng, "gate1")
            ch(eng.reduce_max(gs[:, 0, :], lg3, AX))
            eng.tensor_tensor(g3(0), lg3, bcast(gs[:, 0, :]), ALU.subtract).then_inc(sem("gmax"), 1)
            eng.wait_ge(sem("gexp"), 1)
            ch(eng.reduce_sum(gs[:, 1, :], g3(1), AX))
            ch(eng.reciprocal(gs[:, 1, :], gs[:, 1, :]))
            ch(eng.tensor_tensor(g3(2), g3(1), bcast(gs[:, 1, :]), ALU.mult))
            first_max(eng, ch, g3(2), gs[:, 2, :], g3(0), g3(3))
            eng.sem_inc(sem("oh1"), 1)
            ch(eng.tensor_scalar(gt[:, 1, :], gt[:, 3, :], -1.0, 1.0, ALU.mult, ALU.add))
            ch(eng.tensor_tensor(g3(1), g3(1), g3(2), ALU.mult))

            def kept(bank, m, dst):
                for par in range(2):
                    src = ps[:, bank + par, 0:NB * E].rearrange("p (g e) -> p g e", e=E)
                    ch(eng.tensor_copy(gt[:, dst, :].rearrange("p (g u e) -> p g u e", u=2, e=E)[:, :, par, :], src))
                ch(eng.tensor_scalar(gt[:, 0, :], gt[:, dst, :], float(CAP), None, ALU.is_lt))
                ch(eng.tensor_tensor(gt[:, m, :], gt[:, m, :], gt[:, 0, :], ALU.mult))

            def place(c, m, pos):
                ch(eng.tensor_tensor(g3(0), g3(pos), row3, ALU.add))
                ch(eng.tensor_tensor(g3(0), g3(0), g3(m), ALU.mult))
                ch(eng.reduce_sum(gs[:, 5, :], g3(0), AX))
                ch(eng.reduce_sum(gs[:, 4, :], g3(m), AX))
                ch(eng.tensor_scalar(gs[:, 6, :], gs[:, 4, :], -1.0, 1.0, ALU.mult, ALU.add))
                ch(eng.tensor_scalar(gs[:, 7, :], cst[:, C_TOK:C_TOK + NT], float(E * SL + c * NT * P), None, ALU.add))
                ch(eng.tensor_tensor(gs[:, 7, :], gs[:, 7, :], gs[:, 6, :], ALU.mult))
                ch(eng.tensor_tensor(gs[:, 7, :], gs[:, 7, :], gs[:, 5, :], ALU.add))
                ch(eng.tensor_copy(si[:, c, :], gs[:, 7, :]))
                ch(eng.tensor_copy(gi[:, c, :], gs[:, 5, :]))
                ch(eng.tensor_tensor(gs[:, 2 + c, :], gs[:, 2 + c, :], gs[:, 4, :], ALU.mult))
                eng.sem_inc(sem("route1"), 1)

            eng.wait_ge(sem("p1"), 1)
            kept(0, 3, 5)
            place(0, 3, 5)
            first_max(eng, ch, g3(1), gs[:, 3, :], g3(0), g3(4))
            eng.sem_inc(sem("m1k"), 1)
            eng.wait_ge(sem("p2"), 1)
            kept(2, 4, 6)
            place(1, 4, 6)

        def gate1_tensor(eng):
            def view(k, par):
                return gt[:, k, :].rearrange("p (g u e) -> p g u e", u=2, e=E)[:, :, par, :]

            def o(b):
                return ps[:, b, 0:NB * E].rearrange("p (g e) -> p g e", e=E)

            eng.wait_ge(sem("oh1"), 1)
            eng.matmul(o(0), tri, view(3, 0), start=True, stop=True)
            eng.matmul(o(1), ones, view(3, 0), start=True, stop=False)
            eng.matmul(o(1), tri, view(3, 1), start=False, stop=True).then_inc(sem("p1"), 1)
            eng.wait_ge(sem("m1k"), 1)
            eng.matmul(o(2), ones, view(3, 0), start=True, stop=False)
            eng.matmul(o(2), ones, view(3, 1), start=False, stop=False)
            eng.matmul(o(2), tri, view(4, 0), start=False, stop=True)
            eng.matmul(o(3), ones, view(3, 0), start=True, stop=False)
            eng.matmul(o(3), ones, view(3, 1), start=False, stop=False)
            eng.matmul(o(3), ones, view(4, 0), start=False, stop=False)
            eng.matmul(o(3), tri, view(4, 1), start=False, stop=True).then_inc(sem("p2"), 1)

        def gate1_scalar(eng):
            eng.wait_ge(sem("gmax"), 1)
            eng.activation(gt[:, 1, :], gt[:, 0, :], ACT.Exp).then_inc(sem("gexp"), 1)

        sem("zeros"), sem("zfill"), sem("scat0"), sem("scat1")
        for r in range(4):
            sem(f"back0_{r}"), sem(f"back1_{r}"), sem(f"back2_{r}")
        sem("add1"), sem("add2"), sem("add0")

        def scatter_pool(eng, n):
            eng.wait_ge(sem("zfill"), 32)
            for c in range(n + 1):
                eng.wait_ge(sem(f"route{n}"), c + 1)
                for t in range(NT):
                    idx = si[:, c, t:t + 1] if n else gi[:, c, t:t + 1]
                    eng.indirect_dma_start(out=(slots0, slots1)[n], out_offset=bass.IndirectOffsetOnAxis(ap=idx, axis=0),
                                           in_=xns[:, t * D:(t + 1) * D], in_offset=None).then_inc(sem(f"scat{n}"), 16)

        def gather_pool(eng, which, rows, index, buf):
            for t in range(NT):
                eng.indirect_dma_start(out=buf[:, t * D:(t + 1) * D], out_offset=None, in_=rows,
                                       in_offset=bass.IndirectOffsetOnAxis(ap=index[:, t:t + 1], axis=0))\
                   .then_inc(sem(f"back{which}_{t // 4}"), 16)

        for n in range(2):
            for name in ("wh", "wl", "tr", "xhi", "xlo", "h", "g", "hi", "lo", "y", "yx", "out") + (("b", "m") if n else ()):
                sem(f"f{n}_{name}")
        for p in range(2):
            sem(f"f0_dw{p}"), sem(f"f0_db{p}"), sem(f"f0_dx{p}"), sem(f"f1_st{p}")
        sem("f1_tail"), sem("f1_dx")

        def flat_w(par, part):
            return arena[:, par, part, :]

        def steps(eng, units, pairs, single, step):
            step(0, 0)
            last = pairs - 1
            with eng.Fori(0, last) as i:
                for k in range(1, 2 * units + 1):
                    step(i, k)
            for k in range(1, (3 if single else 2) * units):
                step(last, k)
            return last

        U0 = FC0 // 2
        DW = DC * F0
        fl32 = arena[:, :, :, :].rearrange("p a b c -> p (a b c)")
        wsp0 = [[fl32[:, (2 * p + s) * 2 * DW:(2 * p + s + 1) * 2 * DW] for s in range(2)] for p in range(2)]
        st0 = [fl32[:, 8 * DW + p * 4 * DW:8 * DW + (p + 1) * 4 * DW].bitcast(F32) for p in range(2)]

        def ffn0_loads(eng):
            def expert(j):
                return eng.value_load(texp[0:1, bass.ds(j, 1)] if not isinstance(j, int) else texp[0:1, j:j + 1],
                                      min_val=0, max_val=E - 1)

            def weights(j, par):
                e = expert(j)
                for src, at, width in ((f0w1, 0, F0), (f0w2, DW, D)):
                    eng.dma_start(st0[par][:, at:at + DW].rearrange("p (k n) -> p k n", n=width),
                                  src[bass.ds(e, 1)].rearrange("e (k p) n -> p (e k) n", p=P))\
                       .then_inc(sem(f"f0_dw{par}"), 16)

            def biases(j, par):
                e = expert(j)
                eng.dma_start(b1t[:, par, :], b1c[bass.ds(e, 1)].rearrange("e p f -> p (e f)")).then_inc(sem(f"f0_db{par}"), 16)
                eng.dma_start(b2t[:, par, :], b2w[bass.ds(e, 1)].rearrange("e p n -> p (e n)")).then_inc(sem(f"f0_db{par}"), 16)

            def tokens(j, par):
                src = slots0.rearrange("(j s p) n -> j p s n", j=SLT, p=P)
                src = src[j:j + 1] if isinstance(j, int) else src[bass.ds(j, 1)]
                eng.dma_start(xs[:, par, :].rearrange("p (s n) -> p s n", s=2), src.rearrange("j p s n -> p (j s) n"))\
                   .then_inc(sem(f"f0_dx{par}"), 16)

            def store(j, par):
                eng.wait_ge(sem("f0_yx"), j + 3)
                dst = y0.rearrange("(j s p) n -> j p s n", j=SLT, p=P)
                dst = dst[j:j + 1] if isinstance(j, int) else dst[bass.ds(j, 1)]
                eng.dma_start(dst.rearrange("j p s n -> p (j s) n"), y_sb[:, par * 2 * D:(par + 1) * 2 * D]
                              .rearrange("p (s n) -> p s n", s=2)).then_inc(sem("f0_out"), 16)

            def tile(j, par):
                eng.wait_ge(sem("f0_wl"), j * U0 + U0)
                weights(j + 2, par)
                eng.wait_ge(sem("f0_tr"), j + 1)
                tokens(j + 2, par)

            def finish(j, par):
                store(j, par)
                biases(j + 2, par)

            eng.wait_ge(sem("route0"), 1)
            for j in range(2):
                weights(j, j)
                biases(j, j)
            eng.wait_ge(sem("scat0"), 16 * NT)
            tokens(0, 0)
            tokens(1, 1)
            tile(0, 0)
            with eng.Fori(0, (SLT - 3) // 2) as i:
                tile(i * 2 + 1, 1)
                finish(i * 2, 0)
                tile(i * 2 + 2, 0)
                finish(i * 2 + 1, 1)
            finish(SLT - 3, 0)
            store(SLT - 2, 1)
            store(SLT - 1, 0)

        def half(k):
            return k // U0 % 2, k % U0

        def more(i, k):
            return not (isinstance(i, int) and i == SLT // 2 - 1 and k >= 2 * U0)

        def ffn0_tensor(eng):
            def turn(j, landed, par):
                eng.wait_ge(sem(f"f0_dx{par}"), landed)
                free(eng, sem("f0_xlo"), j)
                for s in range(2):
                    for c in range(DC):
                        mm = eng.transpose(ps[:, 2, c * ST + s * P:c * ST + (s + 1) * P],
                                           xs[:, par, s * D + c * P:s * D + (c + 1) * P], ident)
                mm.then_inc(sem("f0_tr"), 1)

            def hidden(i, k):
                par, r = half(k)
                u, j = i * (2 * U0) + k, i * 2 + k // U0
                if r == 0:
                    eng.wait_ge(sem("f0_wl"), j * U0 + U0 // 2)
                    eng.wait_ge(sem("f0_xlo"), j + 1)
                free(eng, sem("f0_g"), u)
                w = [wsp0[par][s][:, 0:DW].rearrange("p (c n) -> p c n", c=DC) for s in range(2)]
                for q in range(2):
                    f = 2 * r + q
                    for c in range(DC):
                        mm = three(eng, ps[:, k % 2, q * ST:(q + 1) * ST], [w[s][:, c, f * P:(f + 1) * P] for s in range(2)],
                                   [xt[:, par, s, c * ST:(c + 1) * ST] for s in range(2)], c == 0, c == DC - 1)
                mm.then_inc(sem("f0_h"), 1)

            def output(i, k):
                par, r = half(k)
                u, j = i * (2 * U0) + k, i * 2 + k // U0
                eng.wait_ge(sem("f0_lo"), u + 2)
                if r == 0:
                    eng.wait_ge(sem("f0_wl"), j * U0 + U0)
                    eng.wait_ge(sem("f0_yx"), j + 1)
                for s in range(2):
                    for q in range(2):
                        f = 2 * r + q
                        mm = three(eng, ps[:, 4 + 2 * par + s, 0:D],
                                   [(hh, hl)[h][:, k % 2, q * ST + s * P:q * ST + (s + 1) * P] for h in range(2)],
                                   [wsp0[par][h][:, DW + f * D:DW + (f + 1) * D] for h in range(2)],
                                   f == 0, f == FC0 - 1)
                mm.then_inc(sem("f0_y"), 1)

            def step(i, k):
                hidden(i, k)
                if k:
                    output(i, k - 1)
                par, r = half(k)
                if r == 1 and more(i, k):
                    turn(i * 2 + k // U0 + 1, i * 16 + 16 * ((k // U0 + 1) // 2 + 1), 1 - par)

            eng.sem_inc(sem("f0_y"), 1)
            turn(0, 16, 0)
            last = steps(eng, U0, SLT // 2, True, step)
            output(last, 3 * U0 - 1)

        def ffn0_slices(r):
            return r * (2 * DW // U0), (r + 1) * (2 * DW // U0)

        def ffn0_scalar(eng):
            def weights_hi(par, r):
                a, b = ffn0_slices(r)
                eng.activation(wsp0[par][0][:, a:b], st0[par][:, a:b], ACT.Copy, scale=WS).then_inc(sem("f0_wh"), 1)

            def tokens_hi(j, par):
                eng.wait_ge(sem("f0_tr"), j + 1)
                eng.activation(xt[:, par, 0, 0:DC * ST], ps[:, 2, :], ACT.Copy, scale=XS).then_inc(sem("f0_xhi"), 1)

            def step(i, k):
                par, r = half(k)
                u, j = i * (2 * U0) + k, i * 2 + k // U0
                eng.wait_ge(sem("f0_h"), u + 1)
                free(eng, sem("f0_lo"), u)
                if r == 0:
                    eng.wait_ge(sem(f"f0_db{par}"), i * 32 + 32 * (k // U0 // 2 + 1))
                for q in range(2):
                    ins = eng.activation(hid[:, k % 2, q * ST:(q + 1) * ST], ps[:, k % 2, q * ST:(q + 1) * ST], ACT.Gelu,
                                         bias=b1t[:, par, 2 * r + q:2 * r + q + 1], scale=1.0 / (WS * XS))
                ins.then_inc(sem("f0_g"), 1)
                eng.wait_ge(sem("f0_g"), u + 2)
                free(eng, sem("f0_y"), u)
                eng.activation(hh[:, k % 2, :], hid[:, k % 2, :], ACT.Copy, scale=HS0).then_inc(sem("f0_hi"), 1)
                if not more(i, k):
                    return
                if r == 0:
                    eng.wait_ge(sem(f"f0_dw{1 - par}"), i * 32 + 32 * ((k // U0 + 1) // 2 + 1))
                    free(eng, sem("f0_y"), j * U0 + 1 if not isinstance(j, int) or j else 0)
                weights_hi(1 - par, r)
                if r == 1:
                    tokens_hi(j + 1, 1 - par)

            eng.wait_ge(sem("f0_dw0"), 32)
            for r in range(U0):
                weights_hi(0, r)
            tokens_hi(0, 0)
            eng.sem_inc(sem("f0_g"), 1)
            steps(eng, U0, SLT // 2, True, step)

        def ffn0_vector(eng):
            def weights_lo(par, r, count):
                a, b = ffn0_slices(r)
                eng.wait_ge(sem("f0_wh"), count)
                eng.scalar_tensor_tensor(out=wsp0[par][1][:, a:b], in0=st0[par][:, a:b], scalar=WS,
                                         in1=wsp0[par][0][:, a:b], op0=ALU.mult, op1=ALU.subtract).then_inc(sem("f0_wl"), 1)

            def tokens_lo(j, par):
                eng.wait_ge(sem("f0_xhi"), j + 1)
                eng.scalar_tensor_tensor(out=xt[:, par, 1, 0:DC * ST], in0=ps[:, 2, :], scalar=XS,
                                         in1=xt[:, par, 0, 0:DC * ST], op0=ALU.mult, op1=ALU.subtract)\
                   .then_inc(sem("f0_xlo"), 1)

            def result(i, k):
                par = (k // U0 - 1) % 2
                u, j = i * (2 * U0) + (k - 1), i * 2 + (k // U0 - 1)
                eng.wait_ge(sem("f0_y"), u + 2)
                eng.wait_ge(sem("f0_out"), (j + 1) * 16)
                eng.wait_ge(sem(f"f0_db{par}"), i * 32 + 32 * ((k // U0 - 1) // 2 + 1))
                for s in range(2):
                    ins = eng.scalar_tensor_tensor(out=y_sb[:, (par * 2 + s) * D:(par * 2 + s + 1) * D],
                                                   in0=ps[:, 4 + 2 * par + s, 0:D], scalar=1.0 / (WS * HS0),
                                                   in1=b2t[:, par, :], op0=ALU.mult, op1=ALU.add)
                ins.then_inc(sem("f0_yx"), 1)

            def step(i, k):
                par, r = half(k)
                u, j = i * (2 * U0) + k, i * 2 + k // U0
                eng.wait_ge(sem("f0_hi"), u + 1)
                eng.scalar_tensor_tensor(out=hl[:, k % 2, :], in0=hid[:, k % 2, :], scalar=HS0, in1=hh[:, k % 2, :],
                                         op0=ALU.mult, op1=ALU.subtract).then_inc(sem("f0_lo"), 1)
                if more(i, k):
                    weights_lo(1 - par, r, j * U0 + (U0 + r + 1))
                    if r == 1:
                        tokens_lo(j + 1, 1 - par)
                if k and r == 0:
                    result(i, k)

            eng.sem_inc(sem("f0_lo"), 1)
            eng.sem_inc(sem("f0_yx"), 2)
            eng.sem_inc(sem("f0_out"), 32)
            for r in range(U0):
                weights_lo(0, r, r + 1)
            tokens_lo(0, 0)
            last = steps(eng, U0, SLT // 2, True, step)
            result(last, 3 * U0)

        def ffn0_add(eng):
            for t in range(NT):
                if t % 4 == 0:
                    eng.wait_ge(sem(f"back0_{t // 4}"), 64)
                eng.tensor_tensor(xtile(t), xtile(t), xns[:, t * D:(t + 1) * D], ALU.add).then_inc(sem("add0"), 1)

        U1 = FC1
        PIECE = [(0, DC * F1), (DC * F1, DC * F1), (2 * DC * F1, FC1 * D)]
        DONE = [4, 8, 11]
        MAIN = (FC1 - 1) * D

        def ffn1_slice(f):
            if f < 8:
                w = DC * F1 // 4
                return f // 4, P, f % 4 * w, (f % 4 + 1) * w
            if f < 10:
                return 2, P, (f - 8) * MAIN // 2, (f - 7) * MAIN // 2
            return 2, FT1, MAIN, MAIN + D

        def ffn1_loads(eng):
            def piece(i, k):
                q, e = k % 3, i * 2 + k // 3
                src = (f1w0, f1w1, f1wo)[q]
                src = src[e:e + 1] if isinstance(e, int) else src[bass.ds(e, 1)]
                if k >= 2:
                    eng.wait_ge(sem("f1_wl"), i * (2 * U1) + ((k - 2) // 3 * U1 + DONE[(k - 2) % 3]))
                elif not isinstance(i, int):
                    eng.wait_ge(sem("f1_wl"), i * (2 * U1) + (DONE[k + 1] - U1))
                if q < 2:
                    eng.dma_start(stage[:, k % 2, 0:DC * F1].rearrange("p (k n) -> p k n", n=F1),
                                  src.rearrange("e (k p) n -> p (e k) n", p=P)).then_inc(sem(f"f1_st{k % 2}"), 16)
                else:
                    eng.dma_start(stage[:, k % 2, 0:MAIN].rearrange("p (k n) -> p k n", n=D),
                                  src[:, 0:F1 - FT1, :].rearrange("e (k p) n -> p (e k) n", p=P))\
                       .then_inc(sem(f"f1_st{k % 2}"), 16)
                    eng.dma_start(stage[0:FT1, k % 2, MAIN:MAIN + D], src[:, F1 - FT1:F1, :].rearrange("e p n -> p (e n)"))\
                       .then_inc(sem("f1_tail"), 16)

            for k in range(6):
                piece(0, k)
            with eng.Fori(1, E // 2) as i:
                for k in range(6):
                    piece(i, k)

        def ffn1_tensor(eng):
            def turn(e, landed):
                eng.wait_ge(sem("f1_dx"), landed)
                free(eng, sem("f1_xlo"), e)
                for c in range(DC):
                    for s in range(4):
                        mm = eng.transpose(ps[:, 6 + c, s * P:(s + 1) * P], xs4[:, s * D + c * P:s * D + (c + 1) * P], ident)
                mm.then_inc(sem("f1_tr"), 1)

            def hidden(i, k):
                par, f = k // U1 % 2, k % U1
                m = FT1 if f == FC1 - 1 else P
                u, e = i * (2 * U1) + k, i * 2 + k // U1
                free(eng, sem("f1_m"), u)
                for which in range(2):
                    if f == 0:
                        eng.wait_ge(sem("f1_wl"), e * U1 + DONE[which])
                        if which == 0:
                            eng.wait_ge(sem("f1_xlo"), e + 1)
                    w = [flat_w(par, s)[:, which * DC * F1:(which + 1) * DC * F1].rearrange("p (c n) -> p c n", c=DC)
                         for s in range(2)]
                    for c in range(DC):
                        mm = three(eng, ps[0:m, 2 * which + k % 2, :], [w[s][:, c, f * P:f * P + m] for s in range(2)],
                                   [xt[:, par, s, c * SL:(c + 1) * SL] for s in range(2)], c == 0, c == DC - 1)
                    mm.then_inc(sem("f1_b" if which else "f1_h"), 1)

            def output(i, k):
                par, f = k // U1 % 2, k % U1
                m = FT1 if f == FC1 - 1 else P
                u, e = i * (2 * U1) + k, i * 2 + k // U1
                eng.wait_ge(sem("f1_lo"), u + 2)
                if f == 0:
                    eng.wait_ge(sem("f1_wl"), e * U1 + U1)
                    eng.wait_ge(sem("f1_yx"), e + 1)
                at = 2 * DC * F1 + f * D
                for j in range(4):
                    mm = three(eng, ps[:, 4 + j // 2, j % 2 * D:(j % 2 + 1) * D],
                               [(hh, hl)[s][0:m, k % 2, j * P:(j + 1) * P] for s in range(2)],
                               [flat_w(par, s)[0:m, at:at + D] for s in range(2)],
                               f == 0 and j % 2 == 0, f == FC1 - 1, shared=True)
                mm.then_inc(sem("f1_y"), 1)

            def step(i, k):
                hidden(i, k)
                if k:
                    output(i, k - 1)
                if k % U1 == 6 and not (isinstance(i, int) and i == E // 2 - 1 and k > U1):
                    turn(i * 2 + k // U1 + 1, i * 32 + 16 * (k // U1 + 2))

            eng.sem_inc(sem("f1_y"), 1)
            turn(0, 16)
            last = steps(eng, U1, E // 2, False, step)
            output(last, 2 * U1 - 1)

        def ffn1_scalar(eng):
            def weights_hi(par, f, stbuf):
                q, rows, a, b = ffn1_slice(f)
                at = PIECE[q][0]
                eng.activation(flat_w(par, 0)[0:rows, at + a:at + b], stage[0:rows, stbuf, a:b], ACT.Copy, scale=WS)\
                   .then_inc(sem("f1_wh"), 1)

            def tokens(e):
                src = slots1[0:E * SL, :].rearrange("(e s p) n -> e p s n", e=E, p=P)
                src = src[e:e + 1] if isinstance(e, int) else src[bass.ds(e, 1)]
                eng.dma_start(xs4[:, :].rearrange("p (s n) -> p s n", s=4), src.rearrange("e p s n -> p (e s) n"))\
                   .then_inc(sem("f1_dx"), 16)

            def tokens_hi(e, par):
                eng.wait_ge(sem("f1_tr"), e + 1)
                eng.activation(xt[:, par, 0, :].rearrange("p (c n) -> p c n", c=DC), ps[:, 6:8, :], ACT.Copy)\
                   .then_inc(sem("f1_xhi"), 1)

            def result(i, k):
                e = i * 2 + (k // U1 - 1)
                eng.wait_ge(sem("f1_y"), i * (2 * U1) + (k + 1))
                eng.wait_ge(sem("f1_out"), e * 16 + 16)
                eng.activation(y_sb[:, :].rearrange("p (j n) -> p j n", j=2), ps[:, 4:6, :], ACT.Copy,
                               scale=1.0 / (WS * HS1)).then_inc(sem("f1_yx"), 1)
                eng.wait_ge(sem("f1_yx"), e + 2)
                dst = y1.rearrange("(e j p) n -> e p j n", e=E, p=P)
                dst = dst[e:e + 1] if isinstance(e, int) else dst[bass.ds(e, 1)]
                eng.dma_start(dst.rearrange("e p j n -> p (e j) n"), y_sb[:, :].rearrange("p (j n) -> p j n", n=D))\
                   .then_inc(sem("f1_out"), 16)

            def step(i, k):
                par, f = k // U1 % 2, k % U1
                m = FT1 if f == FC1 - 1 else P
                u, e = i * (2 * U1) + k, i * 2 + k // U1
                follows = not (isinstance(i, int) and i == E // 2 - 1 and k >= U1)
                eng.wait_ge(sem("f1_h"), u + 1)
                free(eng, sem("f1_m"), u)
                eng.activation(hga[0:m, k % 2, :], ps[0:m, k % 2, :], ACT.Gelu_apprx_tanh,
                               scale=1.0 / WS).then_inc(sem("f1_g"), 1)
                if follows:
                    q = ffn1_slice(f)[0]
                    piece = 3 * (k // U1 + 1) + q
                    if f in (0, 4, 8):
                        eng.wait_ge(sem(f"f1_st{piece % 2}"), i * 48 + 16 * (piece // 2 + 1))
                    if f == 10:
                        eng.wait_ge(sem("f1_tail"), i * 32 + 16 * (k // U1 + 2))
                    if f == 0:
                        free(eng, sem("f1_y"), e * U1 + 1 if not isinstance(e, int) or e else 0)
                        eng.wait_ge(sem("f1_tr"), e + 1)
                        tokens(e + 1)
                    weights_hi(1 - par, f, piece % 2)
                    if f == 7:
                        tokens_hi(e + 1, 1 - par)
                eng.wait_ge(sem("f1_m"), u + 2)
                free(eng, sem("f1_y"), u)
                eng.activation(hh[0:m, k % 2, :], hid[0:m, k % 2, :], ACT.Copy).then_inc(sem("f1_hi"), 1)
                if k and f == 0:
                    result(i, k)

            eng.sem_inc(sem("f1_yx"), 1)
            eng.sem_inc(sem("f1_out"), 16)
            for f in range(U1):
                q = ffn1_slice(f)[0]
                if f in (0, 4, 8):
                    eng.wait_ge(sem(f"f1_st{q % 2}"), 16 * (q // 2 + 1))
                if f == 10:
                    eng.wait_ge(sem("f1_tail"), 16)
                weights_hi(0, f, q % 2)
            eng.wait_ge(sem("scat1"), 32 * NT)
            tokens(0)
            tokens_hi(0, 0)
            last = steps(eng, U1, E // 2, False, step)
            result(last, 2 * U1)

        def ffn1_vector(eng):
            def weights_lo(par, f, stbuf, count):
                q, rows, a, b = ffn1_slice(f)
                at = PIECE[q][0]
                eng.wait_ge(sem("f1_wh"), count)
                eng.scalar_tensor_tensor(out=flat_w(par, 1)[0:rows, at + a:at + b], in0=stage[0:rows, stbuf, a:b],
                                         scalar=WS, in1=flat_w(par, 0)[0:rows, at + a:at + b],
                                         op0=ALU.mult, op1=ALU.subtract).then_inc(sem("f1_wl"), 1)

            def tokens_lo(e, par):
                eng.wait_ge(sem("f1_xhi"), e + 1)
                eng.tensor_tensor(xt[:, par, 1, :].rearrange("p (c n) -> p c n", c=DC), ps[:, 6:8, :],
                                  xt[:, par, 0, :].rearrange("p (c n) -> p c n", c=DC), ALU.subtract)\
                   .then_inc(sem("f1_xlo"), 1)

            def step(i, k):
                par, f = k // U1 % 2, k % U1
                m = FT1 if f == FC1 - 1 else P
                u, e = i * (2 * U1) + k, i * 2 + k // U1
                eng.wait_ge(sem("f1_b"), u + 1)
                eng.wait_ge(sem("f1_g"), u + 1)
                free(eng, sem("f1_lo"), u)
                eng.scalar_tensor_tensor(out=hid[0:m, k % 2, :], in0=ps[0:m, 2 + k % 2, :], scalar=HS1 / WS,
                                         in1=hga[0:m, k % 2, :], op0=ALU.mult, op1=ALU.mult).then_inc(sem("f1_m"), 1)
                if not (isinstance(i, int) and i == E // 2 - 1 and k >= U1):
                    piece = 3 * (k // U1 + 1) + ffn1_slice(f)[0]
                    weights_lo(1 - par, f, piece % 2, e * U1 + (U1 + f + 1))
                    if f == 7:
                        tokens_lo(e + 1, 1 - par)
                eng.wait_ge(sem("f1_hi"), u + 1)
                eng.tensor_tensor(hl[0:m, k % 2, :], hid[0:m, k % 2, :], hh[0:m, k % 2, :],
                                  ALU.subtract).then_inc(sem("f1_lo"), 1)

            eng.sem_inc(sem("f1_m"), 1)
            eng.sem_inc(sem("f1_lo"), 1)
            for f in range(U1):
                weights_lo(0, f, ffn1_slice(f)[0] % 2, f + 1)
            tokens_lo(0, 0)
            steps(eng, U1, E // 2, False, step)

        back2 = arena[:, :, :, :].rearrange("p a b c -> p (a b c)").bitcast(F32)[:, 0:NT * D]

        def ffn1_add(eng):
            for t in range(NT):
                if t % 4 == 0:
                    eng.wait_ge(sem(f"back1_{t // 4}"), 64)
                eng.scalar_tensor_tensor(out=xtile(t), in0=xns[:, t * D:(t + 1) * D], scalar=gs[:, 2, t:t + 1],
                                         in1=xtile(t), op0=ALU.mult, op1=ALU.add).then_inc(sem("add1"), 1)
                if t % 4 == 0:
                    eng.wait_ge(sem(f"back2_{t // 4}"), 64)
                eng.wait_ge(sem("add1"), t + 1)
                eng.scalar_tensor_tensor(out=xtile(t), in0=back2[:, t * D:(t + 1) * D], scalar=gs[:, 3, t:t + 1],
                                         in1=xtile(t), op0=ALU.mult, op1=ALU.add).then_inc(sem("add2"), 1)

        def x_stores(eng):
            o = out.rearrange("b (u p) n -> p (b u) n", p=P)
            for t in range(0, NT, 4):
                eng.wait_ge(sem("add2"), t + 4)
                eng.dma_start(o[:, t:t + 4, :], x_sb[:, t * D:(t + 4) * D].rearrange("p (t n) -> p t n", n=D))\
                   .then_inc(sem("xout"), 16)
            eng.wait_ge(sem("xout"), 16 * (NT // 4))

        sem("load"), sem("xload"), sem("xout")

        block = ctx.enter_context(nc.Block())

        @block.sync
        def _(sp):
            xv = x.rearrange("b (u p) n -> p (b u) n", p=P)
            sp.dma_start(cst[:, :], consts).then_inc(sem("load"), 16)
            sp.dma_start(vec[:, :], vecs).then_inc(sem("load"), 16)
            att_loads(sp, att[0])
            for t in range(0, NT, 4):
                sp.dma_start(x_sb[:, t * D:(t + 4) * D].rearrange("p (t n) -> p t n", n=D), xv[:, t:t + 4, :])\
                  .then_inc(sem("xload"), 16)
            sp.wait_ge(sem("zeros"), 1)
            for rows in (slots0, slots1[0:E * SL, :]):
                n = rows.shape[0] // P
                sp.dma_start(rows.rearrange("(k p) n -> p k n", p=P), y_sb[:, 0:D].unsqueeze(1).to_broadcast([P, n, D]))\
                  .then_inc(sem("zfill"), 16)
            sp.wait_ge(att[0].s("wl"), 5)
            att_loads(sp, att[1])
            ffn0_loads(sp)
            sp.wait_ge(att[1].s("wl"), 5)
            ffn1_loads(sp)
            x_stores(sp)
            for name, count in (("f0_out", 16 * SLT + 32), ("f1_out", 16 * E + 16), ("scat0", 16 * NT), ("scat1", 32 * NT)):
                sp.wait_ge(sem(name), count)

        @block.gpsimd
        def _(pool):
            pool.memset(y_sb[:, 0:D], 0.0).then_inc(sem("zeros"), 1)
            for n in range(2):
                a = att[n]
                if n:
                    pool.wait_ge(sem("f0_y"), SLT * U0 + 1)
                for v, one in zip(a.vs, (VS, 0.0)):
                    v = v.rearrange("p (b h n) -> p b h n", b=NB, h=a.H)
                    pool.memset(v[:, :, :, a.dh], one).then_inc(a.s("ones"), 1)
                att_prepare_pool(pool, a)
                scatter_pool(pool, n)
                if n == 0:
                    pool.wait_ge(sem("f0_out"), 16 * SLT + 32)
                    gather_pool(pool, 0, y0, gi[:, 0, :], xns)
                    ffn0_add(pool)
            pool.wait_ge(sem("f1_out"), 16 * E + 16)
            gather_pool(pool, 1, y1, gi[:, 0, :], xns)
            gather_pool(pool, 2, y1, gi[:, 1, :], back2)

        @block.scalar
        def _(act):
            act.wait_ge(sem("load"), 32)
            wr_split_scalar(act)
            att_split_scalar(act, att[0])
            act.wait_ge(sem("bias"), 2)
            att_kv_scalar(act, att[0], range(1))
            ln_stats_scalar(act, 0)
            att_kv_scalar(act, att[0], range(1, att[0].nc))
            att_scalar(act, att[0])
            ln_stats_scalar(act, 1)
            route_scalar(act, 0)
            ffn0_scalar(act)
            act.wait_ge(sem("f0_y"), SLT * U0 + 1)
            att_split_scalar(act, att[1])
            att_kv_scalar(act, att[1], range(att[1].nc))
            ln_stats_scalar(act, 2)
            att_scalar(act, att[1])
            ln_stats_scalar(act, 3)
            route_scalar(act, 1)
            gate1_scalar(act)
            ffn1_scalar(act)

        @block.vector
        def _(dve):
            dve.wait_ge(sem("load"), 32)
            wr_split_vector(dve)
            att_split_vector(dve, att[0])
            dve.wait_ge(sem("xload"), 16 * (NT // 4))
            for t in range(NT):
                dve.bn_stats(st6[:, t, :], xtile(t)).then_inc(sem("ln_st"), 1)
            for t in range(NT):
                ln_aggregate(dve, 0, t)
            ln_variance(dve, 0)
            att_kv_vector(dve, att[0], range(1))
            ln_invert(dve, 0)
            att_kv_vector(dve, att[0], range(1, att[0].nc))
            att_vector(dve, att[0])
            ln_finish_vector(dve, 1)
            route_vector(dve, 0)
            gate0_vector(dve)
            ffn0_vector(dve)
            att_split_vector(dve, att[1])
            att_kv_vector(dve, att[1], range(att[1].nc))
            for t in range(NT):
                ln_tile(dve, 2, t, sem("add0"))
            for t in range(NT):
                ln_aggregate(dve, 2, t)
            ln_finish_vector(dve, 2)
            att_vector(dve, att[1])
            ln_finish_vector(dve, 3)
            route_vector(dve, 1)
            gate1_vector(dve)
            ffn1_vector(dve)
            ffn1_add(dve)

        @block.tensor
        def _(pe):
            pe.wait_ge(sem("load"), 32)
            att_kv_tensor(pe, att[0])
            att_tensor(pe, att[0])
            route_tensor(pe, 0)
            gate0_tensor(pe)
            ffn0_tensor(pe)
            pe.wait_ge(sem("f0_yx"), SLT + 2)
            att_kv_tensor(pe, att[1])
            att_tensor(pe, att[1])
            route_tensor(pe, 1)
            gate1_tensor(pe)
            ffn1_tensor(pe)


def kernel(**inputs):
    import numpy as np
    import concourse.bacc as bacc
    from concourse.bass_utils import run_bass_kernel_spmd

    g = {k: np.ascontiguousarray(v) for k, v in inputs.items()}

    def chunks(w, rows):
        return np.ascontiguousarray(w.reshape(w.shape[0] // rows, rows, w.shape[1]).transpose(1, 0, 2))

    def cols(v):
        return v.reshape(-1, P).T

    def wide(v):
        return np.broadcast_to(v, (P, v.shape[-1]))

    p = np.arange(P)
    t, e = np.arange(NT)[:, None], np.arange(E)[None, :]
    consts = np.concatenate([
        p[:, None] == p[None, :],
        p[:, None] < p[None, :],
        np.ones((P, P)),
        wide((np.zeros((NT, 1)) + (E - e)).reshape(1, -1)),
        wide((e * SL + (t // TPB) * CAP).reshape(1, -1)),
        wide((t + 0 * e).reshape(1, -1)),
        wide((0 * e.T + ST * e).reshape(1, -1)),
        t.T * P + p[:, None],
        p[:, None] // 16 == np.arange(8)[None],
        p[:, None] // 64 == np.arange(2)[None],
    ], axis=1).astype(np.float32)
    vecs = np.ascontiguousarray(np.concatenate([
        cols(g["L0_xattn_bq"]), cols(g["L0_xattn_bk"]),
        wide(g["L0_xattn_bv"]), wide(g["L0_xattn_bo"]), wide(g["L1_xattn_bo"]), wide(g["L0_ffn_br"]),
        chunks(g["L0_ffn_wr"], P).reshape(P, -1), chunks(g["L1_ffn_router_w"], P).reshape(P, -1),
    ], axis=1))
    assert consts.shape[1] == C_END and vecs.shape[1] == V_END
    ctx_t = chunks(np.ascontiguousarray(g["ctx_768"].reshape(NB * CK, CC).T), CR)
    arrays = {
        "x": g["x"], "ctx_t": ctx_t, "consts": consts, "vecs": vecs,
        "b1c": np.ascontiguousarray(g["L0_ffn_b1"].reshape(E, FC0, P).transpose(0, 2, 1)),
        "b2w": np.ascontiguousarray(np.broadcast_to(g["L0_ffn_b2"][:, None], (E, P, D))),
        "wq0": chunks(g["L0_xattn_Wq"], P), "wk0": chunks(g["L0_xattn_Wk"], CR),
        "wv0": chunks(g["L0_xattn_Wv"], CR), "wo0": chunks(g["L0_xattn_Wo"], P),
        "wq1": chunks(g["L1_xattn_Wq"], P), "wk1": chunks(g["L1_xattn_Wk"], CR),
        "wv1": chunks(g["L1_xattn_Wv"], CR), "wo1": chunks(g["L1_xattn_Wo"], P),
        "f0w1": g["L0_ffn_w1"], "f0w2": g["L0_ffn_w2"],
        "f1w0": g["L1_ffn_w0_kernel"], "f1w1": g["L1_ffn_w1_kernel"], "f1wo": g["L1_ffn_wo_kernel"],
    }
    nc = bacc.Bacc("TRN2", target_bir_lowering=False, num_devices=1)
    args = [nc.dram_tensor(f"in_{k}", a.shape, mybir.dt.from_np(a.dtype), kind="ExternalInput").ap()
            for k, a in arrays.items()]
    out = nc.dram_tensor("out_x", (NB, TPB * P, D), F32, kind="ExternalOutput").ap()
    build(nc, *args, out)
    r = run_bass_kernel_spmd(nc, [{f"in_{k}": a for k, a in arrays.items()}], core_ids=[0])
    return r.results[0]["out_x"]
```
